# Optimizing a Trainium2 kernel written in Bass

```python
import numpy as np
import jax
import jax.numpy as jnp

def _softmax(x, axis=-1):
    return jax.nn.softmax(x, axis=axis)

def _gelu(x):
    return jax.nn.gelu(x, approximate=True)

def _silu(x):
    return jax.nn.silu(x)

def _sigmoid(x):
    return jax.nn.sigmoid(x)

def _layernorm(x, axis=-1, eps=1e-05):
    m = jnp.mean(x, axis=axis, keepdims=True)
    v = jnp.var(x, axis=axis, keepdims=True)
    return (x - m) / jnp.sqrt(v + eps)

def _scatter_add(tgt, idx, src, axis=0):
    return tgt.at[idx].add(src)

def _segment_sum(src, seg, n):
    return jax.ops.segment_sum(src, seg, n)
kernel_name = 'mk_xattn_ffn_d1_seqx_r4_7fadb3'

def setup_inputs(seed: int=0):
    np.random.seed(seed)
    _w = jnp.asarray

    def _rec_inputs():
        import jax
        import jax.numpy as jnp
        _rk = jax.random.key(seed)
        x = -0.0003929 + 0.9999 * jax.random.normal(jax.random.fold_in(_rk, 1), (4, 512, 512), jnp.float32)
        _lenS = 512 - jax.random.randint(jax.random.fold_in(_rk, 7), (4,), 0, max(1, 512 // 4) + 1, jnp.int32)
        _lenS2 = 512 - jax.random.randint(jax.random.fold_in(_rk, 8), (4,), 0, max(1, 512 // 4) + 1, jnp.int32)
        _ctx_2048P = jax.random.normal(jax.random.fold_in(_rk, 11), (4, 16, 512), jnp.float32)
        _ctx_2048c = jax.random.dirichlet(jax.random.fold_in(_rk, 511), 0.3 * jnp.ones((16,), jnp.float32), (4, 512))
        _ctx_2048t = jnp.einsum('bsk,bkd->bsd', _ctx_2048c, _ctx_2048P)
        _ctx_2048t = _ctx_2048t * jax.lax.rsqrt(jnp.mean(jnp.square(_ctx_2048t)) + 1e-12) * 0.953939
        ctx_2048 = -1.39393e-06 + 0.999914 * (_ctx_2048t + 0.3 * jax.random.normal(jax.random.fold_in(_rk, 611), (4, 512, 512), jnp.float32))
        itok_BxS_0_1023 = jax.random.randint(jax.random.fold_in(_rk, 12), (4, 512), 0, 256, jnp.int32)
        return (x, ctx_2048, itok_BxS_0_1023)
    x, ctx_2048, itok_BxS_0_1023 = _rec_inputs()

    def _L0_xattn_setup():
        import jax, jax.numpy as jnp
        import numpy as np
        B, Lq, Lk = (2, 1024, 256)
        Q_DIM, KV_DIM = (512, 512)
        H, HD = (16, 128)
        KVC, QC, R = (128, 192, 64)
        LOOKBACK = 8
        NEG = -1e+30

        def _rope(x, L):
            half = x.shape[-1] // 2
            inv_freq = 1.0 / 10000.0 ** (jnp.arange(half, dtype=jnp.float32) / half)
            ang = jnp.arange(L, dtype=jnp.float32)[:, None] * inv_freq
            cos, sin = (jnp.cos(ang), jnp.sin(ang))
            x1, x2 = (x[..., :half], x[..., half:])
            return jnp.concatenate([x1 * cos - x2 * sin, x1 * sin + x2 * cos], axis=-1)
        key = jax.random.key(seed)
        ks = jax.random.split(key, 11)

        def w(k, shape, fan_in):
            return jax.random.normal(k, shape, jnp.float32) / np.sqrt(fan_in).astype(np.float32)
        return {'q': jax.random.normal(ks[0], (B, Lq, Q_DIM), jnp.float32), 'kv': jax.random.normal(ks[1], (B, Lk, KV_DIM), jnp.float32), 'seg_id': jnp.sort(jax.random.randint(ks[2], (B, Lq), 0, Lk), axis=-1), 'W_kvc': w(ks[3], (KV_DIM, KVC), KV_DIM), 'W_dq': w(ks[4], (Q_DIM, QC), Q_DIM), 'W_uq': w(ks[5], (QC, H * HD), QC), 'W_qr': w(ks[6], (QC, H * R), QC), 'W_uk': w(ks[7], (KVC, H * HD), KVC), 'W_kr': w(ks[8], (KVC, R), KVC), 'W_uv': w(ks[9], (KVC, H * HD), KVC), 'W_o': w(ks[10], (H * HD, Q_DIM), H * HD)}
    _L0_xattn_all = _L0_xattn_setup()
    _L0_xattn_in = {k: v for k, v in _L0_xattn_all.items() if k in ('W_kvc', 'W_dq', 'W_uq', 'W_qr', 'W_uk', 'W_kr', 'W_uv', 'W_o')}
    del _L0_xattn_all

    def _L0_ffn_setup():
        import jax, jax.numpy as jnp
        import numpy as np
        D_MODEL = 512
        HIDDEN = 4 * D_MODEL
        B, S = (2, 1024)

        def bit_linear(x, w, b):
            gamma_x = jnp.clip(jnp.max(jnp.abs(x), axis=-1, keepdims=True), 1e-05, None)
            scale_x = 127.0 / gamma_x
            x_dq = jnp.clip(jnp.round(x * scale_x), -128.0, 127.0) / scale_x
            x_ste = x + jax.lax.stop_gradient(x_dq - x)
            gamma_w = jnp.clip(jnp.mean(jnp.abs(w)), 1e-05, None)
            w_dq = jnp.clip(jnp.round(w / gamma_w), -1.0, 1.0) * gamma_w
            w_ste = w + jax.lax.stop_gradient(w_dq - w)
            return jnp.einsum('bsd,hd->bsh', x_ste, w_ste) + b
        key = jax.random.key(seed)
        ks = jax.random.split(key, 7)
        std = 0.02
        return {'x': jax.random.normal(ks[0], (B, S, D_MODEL), dtype=jnp.float32), 'gate_w': jax.random.normal(ks[1], (HIDDEN, D_MODEL), dtype=jnp.float32) * std, 'gate_b': jnp.zeros((HIDDEN,), dtype=jnp.float32), 'val_w': jax.random.normal(ks[2], (HIDDEN, D_MODEL), dtype=jnp.float32) * std, 'val_b': jnp.zeros((HIDDEN,), dtype=jnp.float32), 'out_w': jax.random.normal(ks[3], (D_MODEL, HIDDEN), dtype=jnp.float32) * std, 'out_b': jnp.zeros((D_MODEL,), dtype=jnp.float32)}
    _L0_ffn_all = _L0_ffn_setup()
    _L0_ffn_in = {k: v for k, v in _L0_ffn_all.items() if k in ('gate_w', 'gate_b', 'val_w', 'val_b', 'out_w', 'out_b')}
    del _L0_ffn_all
    return {'x': x, 'ctx_2048': ctx_2048, 'itok_BxS_0_1023': itok_BxS_0_1023, 'L0_xattn_W_kvc': _L0_xattn_in['W_kvc'], 'L0_xattn_W_dq': _L0_xattn_in['W_dq'], 'L0_xattn_W_uq': _L0_xattn_in['W_uq'], 'L0_xattn_W_qr': _L0_xattn_in['W_qr'], 'L0_xattn_W_uk': _L0_xattn_in['W_uk'], 'L0_xattn_W_kr': _L0_xattn_in['W_kr'], 'L0_xattn_W_uv': _L0_xattn_in['W_uv'], 'L0_xattn_W_o': _L0_xattn_in['W_o'], 'L0_ffn_gate_w': _L0_ffn_in['gate_w'], 'L0_ffn_gate_b': _L0_ffn_in['gate_b'], 'L0_ffn_val_w': _L0_ffn_in['val_w'], 'L0_ffn_val_b': _L0_ffn_in['val_b'], 'L0_ffn_out_w': _L0_ffn_in['out_w'], 'L0_ffn_out_b': _L0_ffn_in['out_b']}

def reference(x, ctx_2048, itok_BxS_0_1023, L0_xattn_W_kvc, L0_xattn_W_dq, L0_xattn_W_uq, L0_xattn_W_qr, L0_xattn_W_uk, L0_xattn_W_kr, L0_xattn_W_uv, L0_xattn_W_o, L0_ffn_gate_w, L0_ffn_gate_b, L0_ffn_val_w, L0_ffn_val_b, L0_ffn_out_w, L0_ffn_out_b):
    import jax
    import jax.numpy as jnp

    def _L0_xattn_ref(q, kv, seg_id, W_kvc, W_dq, W_uq, W_qr, W_uk, W_kr, W_uv, W_o):
        import jax, jax.numpy as jnp
        import numpy as np
        B, Lq, Lk = (2, 1024, 256)
        Q_DIM, KV_DIM = (512, 512)
        H, HD = (16, 128)
        KVC, QC, R = (128, 192, 64)
        LOOKBACK = 8
        NEG = -1e+30

        def _rope(x, L):
            half = x.shape[-1] // 2
            inv_freq = 1.0 / 10000.0 ** (jnp.arange(half, dtype=jnp.float32) / half)
            ang = jnp.arange(L, dtype=jnp.float32)[:, None] * inv_freq
            cos, sin = (jnp.cos(ang), jnp.sin(ang))
            x1, x2 = (x[..., :half], x[..., half:])
            return jnp.concatenate([x1 * cos - x2 * sin, x1 * sin + x2 * cos], axis=-1)
        b, lq, _ = q.shape
        lk = kv.shape[1]
        kv_c = kv @ W_kvc
        q_c = q @ W_dq
        q_nope = (q_c @ W_uq).reshape(b, lq, H, HD).transpose(0, 2, 1, 3)
        q_rope = (q_c @ W_qr).reshape(b, lq, H, R).transpose(0, 2, 1, 3)
        k_nope = (kv_c @ W_uk).reshape(b, lk, H, HD)
        v = (kv_c @ W_uv).reshape(b, lk, H, HD)
        k_rope = kv_c @ W_kr
        q_rope = _rope(q_rope, lq)
        k_rope = _rope(k_rope, lk)
        scale = 1.0 / np.sqrt(HD + R).astype(np.float32)
        scores = (jnp.einsum('bhqd,bkhd->bhqk', q_nope, k_nope) + jnp.einsum('bhqr,bkr->bhqk', q_rope, k_rope)) * scale
        k_ids = jnp.arange(lk)[None, None, :]
        qs = seg_id[:, :, None]
        good = (k_ids <= qs) & (k_ids >= qs - LOOKBACK)
        scores = jnp.where(good[:, None, :, :], scores, NEG)
        attn = jax.nn.softmax(scores, axis=-1)
        out = jnp.einsum('bhqk,bkhd->bqhd', attn, v).reshape(b, lq, H * HD)
        return out @ W_o

    def _L0_ffn_ref(x, gate_w, gate_b, val_w, val_b, out_w, out_b):
        import jax, jax.numpy as jnp
        import numpy as np
        D_MODEL = 512
        HIDDEN = 4 * D_MODEL
        B, S = (2, 1024)

        def bit_linear(x, w, b):
            gamma_x = jnp.clip(jnp.max(jnp.abs(x), axis=-1, keepdims=True), 1e-05, None)
            scale_x = 127.0 / gamma_x
            x_dq = jnp.clip(jnp.round(x * scale_x), -128.0, 127.0) / scale_x
            x_ste = x + jax.lax.stop_gradient(x_dq - x)
            gamma_w = jnp.clip(jnp.mean(jnp.abs(w)), 1e-05, None)
            w_dq = jnp.clip(jnp.round(w / gamma_w), -1.0, 1.0) * gamma_w
            w_ste = w + jax.lax.stop_gradient(w_dq - w)
            return jnp.einsum('bsd,hd->bsh', x_ste, w_ste) + b
        gate = jax.nn.silu(bit_linear(x, gate_w, gate_b))
        val = bit_linear(x, val_w, val_b)
        return bit_linear(gate * val, out_w, out_b)
    x = x + _L0_xattn_ref(_layernorm(x, axis=-1), ctx_2048, itok_BxS_0_1023, L0_xattn_W_kvc, L0_xattn_W_dq, L0_xattn_W_uq, L0_xattn_W_qr, L0_xattn_W_uk, L0_xattn_W_kr, L0_xattn_W_uv, L0_xattn_W_o)
    x = x + _L0_ffn_ref(_layernorm(x, axis=-1), L0_ffn_gate_w, L0_ffn_gate_b, L0_ffn_val_w, L0_ffn_val_b, L0_ffn_out_w, L0_ffn_out_b)
    return x

_drawn_inputs = setup_inputs


def setup_inputs(seed=0):
    import zlib

    import numpy as np

    out = dict(_drawn_inputs(seed))
    spreads = {'L0_ffn_gate_b': (0.0, 0.8), 'L0_ffn_val_b': (0.0, 0.8), 'L0_ffn_out_b': (0.0, 0.1)}
    factors = {}
    for name, (base, spread) in spreads.items():
        noise = np.random.default_rng([zlib.crc32(name.encode()), seed]).standard_normal(out[name].shape)
        drawn = base * np.exp(spread * noise) if base else spread * noise
        out[name] = jnp.asarray(drawn.astype(out[name].dtype))
    for name, factor in factors.items():
        out[name] = (out[name] * factor).astype(out[name].dtype)
    return out
```

```python
from contextlib import ExitStack

import numpy as np

import concourse.bass as bass
from concourse import mybir

ALU = mybir.AluOpType
ACT = mybir.ActivationFunctionType
AX = mybir.AxisListType
F32 = mybir.dt.float32
BF16 = mybir.dt.bfloat16
I32 = mybir.dt.int32

P = 128
BATCH, LQ, LK, DM = 4, 512, 512, 512
H, HD, ROPE, KVC, QC = 16, 128, 64, 128, 192
HID = 2048
LOOKBACK = 8
NEG = -1e30
EPS = 1e-5
SCALE = float(1.0 / np.sqrt(HD + ROPE).astype(np.float32))
MAGIC = 12582912.0
TOK = BATCH * LQ
T = TOK // P
KD = DM // P
NG = 4
GH = H // NG
FC = 4
FK = HID // P
NM = 3
WCOL = DM * HID // P
WCH = 8
WC = WCOL // WCH


def wait(eng, sem, value):
    if not (isinstance(value, int) and value <= 0):
        eng.wait_ge(sem, value)


def build(nc, x, ctxT, itok, cs, cosn, sinn, wkvc, wdq, uqT, ukT, uvT, wo, qr, kr, gate, val, outw,
          gate_b, val_b, out_b, y):
    W = 4
    NU = NG * W
    HU = GH // W
    KW = W * P
    ctx = ExitStack()
    with ctx:
        def sb(name, shape, dt=F32):
            return ctx.enter_context(nc.sbuf_tensor(name, shape, dt))

        def sem(name):
            return ctx.enter_context(nc.semaphore(name))

        bank = [ctx.enter_context(nc.psum_tensor(f"bank{n}", [P, 512], F32)) for n in range(8)]
        ps_s = bank[0:2]
        ps_pt, ps_ol = bank[2:4]
        ps_qa, ps_qb = bank[4:6]
        ps_out, ps_prep = bank[6:8]
        ps_g, ps_v, ps_tr = bank[0:2], bank[2:4], bank[4:6]
        ps_o, ps_xt = bank[6:8]

        x_all = sb("x_all", [P, T, DM])
        kv_cT = sb("kv_cT", [P, TOK])
        kropeT = sb("kropeT", [P, TOK])
        identf = sb("identf", [P, P])
        identb = sb("identb", [P, P], BF16)
        ones = sb("ones", [P, P])
        iota = sb("iota", [P, KW])
        mhalf = sb("mhalf", [P, 1])
        seg_i = sb("seg_i", [P, T], I32)
        seg_hi = sb("seg_hi", [P, T])
        seg_lo = sb("seg_lo", [P, T])
        asum = sb("asum", [P, NM, WCH])
        asum1 = sb("asum1", [P, NM])
        gam = sb("gam", [P, NM])
        thr = sb("thr", [P, NM])
        nthr = sb("nthr", [P, NM])

        tern = sb("tern", [P, NM, WCOL], BF16)
        ternf = tern[:, :, :].rearrange("p m c -> p (m c)").bitcast(F32)
        wo_sb = ternf[:, 0:8192].rearrange("p (h n) -> p h n", h=H)
        ukT_sb = ternf[:, 8192:10240].rearrange("p (h n) -> p h n", h=H)
        uvT_sb = ternf[:, 10240:12288].rearrange("p (h n) -> p h n", h=H)
        tern_g = tern[:, 0, :].rearrange("p (k n) -> p k n", k=KD)
        tern_v = tern[:, 1, :].rearrange("p (k n) -> p k n", k=KD)
        tern_o = tern[:, 2, :].rearrange("p (k n) -> p k n", k=FK)

        stage = sb("stage", [P, NM, WC])
        uqT_sb = stage[:, :, :].rearrange("p m c -> p (m c)").rearrange("p (h n) -> p h n", h=H)

        vo = sb("vo", [P, H, DM])
        vof = vo[:, :, :].rearrange("p h n -> p (h n)")
        ctx_sb = vof.rearrange("p (b k n) -> p b k n", b=BATCH, k=KD)
        h_sb = vof[:, 0:2048]
        g_sb = [vof[:, 2048 + 512 * n:2560 + 512 * n] for n in range(2)]
        v_sb = [vof[:, 3072 + 512 * n:3584 + 512 * n] for n in range(2)]
        th_sb = [vof[:, 4096 + 512 * n:4608 + 512 * n] for n in range(2)]
        hq = vof[:, 5120:6144].bitcast(BF16)
        hqT = vof[:, 6144:7168].bitcast(BF16).rearrange("p (k n) -> p k n", k=FK)
        xq = vof[:, 7168:7424].bitcast(BF16)
        xqT = vof[:, 7424:7680].bitcast(BF16).rearrange("p (k n) -> p k n", k=KD)

        projw = sb("projw", [P, 6144])
        uqk1 = projw[:, 0:2048].rearrange("p (h n) -> p h n", h=H)
        uqk2 = projw[:, 2048:3072].rearrange("p (h n) -> p h n", h=H // 2)
        qrA = projw[:, 3072:4096]
        qrB = projw[:, 4096:5120]
        qr2 = projw[:, 5120:6144]
        gb_sb = projw[:, 0:2048]
        vb_sb = projw[:, 2048:4096]
        ob_sb = projw[:, 4096:4608]
        wdq_sb = sb("wdq_sb", [P, KD, 256])

        xn = sb("xn", [P, DM])
        iota_i = xn[:, 0:KW].bitcast(I32)
        xnT = sb("xnT", [P, KD, P])
        qcs = sb("qcs", [P, 5, P])
        cs_sb = sb("cs_sb", [P, 2 * P])
        kwin = sb("kwin", [P, KW])
        krz = sb("krz", [P, 2, KW])
        kvwin = sb("kvwin", [P, W, KVC])
        mask = sb("mask", [P, KW], BF16)
        st6 = sb("st6", [P, 6])
        mv = sb("mv", [P, 2])
        carry = sb("carry", [P, 1])
        ve = sb("ve", [P, 1])
        rstd = sb("rstd", [P, 1])
        ql = [sb(f"ql{n}", [P, GH, P]) for n in range(2)]
        wkvc_sb = ql[0]
        kr_sb = ql[1]
        qrt = [sb(f"qrt{n}", [P, GH // 2, P]) for n in range(2)]
        tA = sb("tA", [P, GH // 2, P])
        tB = sb("tB", [P, GH // 2, P])
        pr_all = sb("pr_all", [P, 2, 512])
        pr = [pr_all[:, n, :] for n in range(2)]
        cosn_sb, sinn_sb = pr
        mx = [sb(f"mx{n}", [P, HU]) for n in range(2)]
        sm = [sb(f"sm{n}", [P, HU]) for n in range(2)]
        rc = [sb(f"rc{n}", [P, HU]) for n in range(2)]
        pt_sb = sb("pt_sb", [P, 512])
        ol = [sb(f"ol{n}", [P, HU, P]) for n in range(2)]
        tmpb = sb("tmpb", [P, WC], BF16)
        maskt = tmpb[:, 0:KW]
        gx = sb("gx", [P, 1])
        gxc = sb("gxc", [P, 1])
        rx = sb("rx", [P, 1])
        sx = sb("sx", [P, 1])
        dx = sb("dx", [P, 1])
        sgv = sb("sgv", [P, 2])
        mh4 = sb("mh4", [P, FC])
        mh = sb("mh", [P, 1])
        gh = sb("gh", [P, 1])
        rh = sb("rh", [P, 1])
        sh = sb("sh", [P, 1])
        so = sb("so", [P, 1])

        names = """const_ld ctx_ld0 ctx_ld1 ctx_ld2 ctx_ld3 kvw_ld uw_ld vow_ld x_ld qw_ld cs_ld st_ld bias_ld stored
            pool_const dve_const zeros kv_ps kv_ev kr_ps kr_mul kr_ready uqk_ps uqk_ev vo_ps vo_ev
            sc_done pt_done pv_done ql_done qr_done op_done xt_done qc_done kt_done
            max_done sub_done sum_done rec_done ol_ready rope_ab out_added win_copied mask_parts
            win_ready bn_done aggr_done veps_done xn_ready exp_done pt_ready ql_ready kv_ready
            xnT_ready qc_ready p_ready qr_ready rstd_ready sums_done tern_lt tern_done
            asum_red gam_ps gam_ready gam_a gam_b
            bn2 aggr2 veps2 rstd2 xn2 gx2 gxc2 rx2 sx2 xr2 xq_ready dx2 sgv_ready xt2 xqT_ready gate_ps val_ps
            g_ready v_ready th_ready t_ready h_ready mh_part mh_done gh_done rh_done sh_done hr_done
            hq_ready tr_done hqT_ready o_done so_ready xb_ready y_ready""".split()
        S = {n: sem(n) for n in names}

        block = ctx.enter_context(nc.Block())

        @block.sync
        def _(sp):
            sp.dma_start(seg_i[:, :], itok).then_inc(S["const_ld"], 16)
            sp.dma_start(pr_all[:, 0, :], cosn).then_inc(S["const_ld"], 16)
            sp.dma_start(pr_all[:, 1, :], sinn).then_inc(S["const_ld"], 16)
            sp.dma_start(wkvc_sb[:, :, :], wkvc.rearrange("(k p) n -> p k n", p=P)).then_inc(S["kvw_ld"], 16)
            sp.dma_start(kr_sb[:, 0:2, :], kr).then_inc(S["kvw_ld"], 16)
            for b in range(BATCH):
                sp.dma_start(ctx_sb[:, b, :, :], ctxT[b].rearrange("(k p) n -> p k n", p=P)).then_inc(S[f"ctx_ld{b}"], 16)
            sp.dma_start(uqT_sb, uqT.rearrange("(h p) n -> p h n", p=P)).then_inc(S["uw_ld"], 16)
            sp.dma_start(ukT_sb, ukT.rearrange("(h p) n -> p h n", p=P)).then_inc(S["uw_ld"], 16)
            sp.dma_start(wdq_sb[:, :, :], wdq.rearrange("(k p) n -> p k n", p=P)).then_inc(S["qw_ld"], 16)
            sp.dma_start(projw[:, 3072:6144], qr).then_inc(S["qw_ld"], 16)
            sp.dma_start(x_all[:, 0:4, :], x[0:512].rearrange("(t p) n -> p t n", p=P)).then_inc(S["x_ld"], 16)
            sp.dma_start(cs_sb[:, :], cs[0:P, :]).then_inc(S["cs_ld"], 16)
            sp.dma_start(uvT_sb, uvT.rearrange("(h p) n -> p h n", p=P)).then_inc(S["vow_ld"], 16)
            sp.dma_start(wo_sb, wo.rearrange("(h p) n -> p h n", p=P)).then_inc(S["vow_ld"], 16)
            sp.dma_start(x_all[:, 4:T, :], x[512:TOK].rearrange("(t p) n -> p t n", p=P)).then_inc(S["x_ld"], 16)

            def pieces(c):
                for m, w in enumerate((gate, val, outw)):
                    sp.dma_start(stage[:, m, :], w[bass.ds(c, 1)].rearrange("o p n -> (o p) n")).then_inc(S["st_ld"], 16)

            def next_cs(i):
                sp.wait_ge(S["qc_done"], i + 1)
                sp.dma_start(cs_sb[:, :], cs[bass.ds(((i + 1) % 4) * P, P), :]).then_inc(S["cs_ld"], 16)

            sp.wait_ge(S["uqk_ps"], NG)
            pieces(0)
            next_cs(0)
            with sp.Fori(1, WCH) as i:
                sp.wait_ge(S["sums_done"], NM * i)
                pieces(i)
                next_cs(i)
            sp.wait_ge(S["sums_done"], NM * WCH)
            pieces(0)
            next_cs(WCH)
            with sp.Fori(WCH + 1, T - 1) as i:
                sp.wait_ge(S["tern_done"], NM * (i - WCH))
                pieces(i - WCH)
                next_cs(i)
            sp.wait_ge(S["tern_done"], NM * (T - 1 - WCH))
            pieces(WCH - 1)
            sp.wait_ge(S["ql_done"], T * NG)
            sp.wait_ge(S["qr_done"], T * NG)
            sp.dma_start(gb_sb, gate_b.partition_broadcast(P)).then_inc(S["bias_ld"], 16)
            sp.dma_start(vb_sb, val_b.partition_broadcast(P)).then_inc(S["bias_ld"], 16)
            sp.dma_start(ob_sb, out_b.partition_broadcast(P)).then_inc(S["bias_ld"], 16)
            with sp.Fori(0, T) as t:
                sp.wait_ge(S["y_ready"], t + 1)
                sp.dma_start(y[bass.ds(t * P, P), :], x_all[:, bass.ds(t, 1), :].rearrange("p o n -> p (o n)")).then_inc(S["stored"], 16)
            sp.wait_ge(S["stored"], 16 * T)

        @block.tensor
        def _(pe):
            pe.wait_ge(S["kvw_ld"], 32)
            for b in range(BATCH):
                pe.wait_ge(S[f"ctx_ld{b}"], 16)
                wait(pe, S["kv_ev"], b)
                for k in range(KD):
                    mm = nc.tensor.matmul(ps_s[0][:, :], wkvc_sb[:, k, :], ctx_sb[:, b, k, :],
                                          start=(k == 0), stop=(k == KD - 1))
                mm.then_inc(S["kv_ps"], 1)
                pe.wait_ge(S["kv_ev"], b + 1)
                wait(pe, S["kr_mul"], 2 * b)
                nc.tensor.matmul(ps_s[1][:, :], kr_sb[:, 0, :], kv_cT[:, b * LK:(b + 1) * LK], start=True, stop=True)
                nc.tensor.matmul(ps_pt[:, :], kr_sb[:, 1, :], kv_cT[:, b * LK:(b + 1) * LK],
                                 start=True, stop=True).then_inc(S["kr_ps"], 1)
            pe.wait_ge(S["uw_ld"], 32)
            for g in range(NG):
                wait(pe, S["uqk_ev"], 2 * g)
                half = 64 * (g // 2)
                for j in range(GH):
                    h = g * GH + j
                    nc.tensor.matmul(ps_qa[:, j * P:(j + 1) * P], uqT_sb[:, h, 0:P], ukT_sb[:, h, :],
                                     start=True, stop=True)
                    mm = nc.tensor.matmul(ps_qb[half:half + 64, j * P:(j + 1) * P], uqT_sb[:, h, P:QC], ukT_sb[:, h, :],
                                          start=True, stop=True)
                mm.then_inc(S["uqk_ps"], 1)
            pe.wait_ge(S["vow_ld"], 32)
            for h in range(H):
                wait(pe, S["uqk_ev"], 2 * NG) if h == 0 else None
                wait(pe, S["vo_ev"], h - 1)
                nc.tensor.matmul((ps_qa if h % 2 == 0 else ps_qb)[:, :], uvT_sb[:, h, :], wo_sb[:, h, :],
                                 start=True, stop=True).then_inc(S["vo_ps"], 1)

            def turn_x(i):
                wait(pe, S["kv_ready"], i)
                pe.wait_ge(S["xn_ready"], i + 1)
                for k in range(KD):
                    mm = nc.tensor.transpose(ps_prep[:, k * P:(k + 1) * P], xn[:, k * P:(k + 1) * P], identf[:, :])
                mm.then_inc(S["xt_done"], 1)

            def latent_q(i):
                pe.wait_ge(S["xnT_ready"], i + 1)
                pe.wait_ge(S["cs_ld"], (i + 1) * 16)
                for j in range(2):
                    for k in range(KD):
                        nc.tensor.matmul(ps_prep[:, j * P:(j + 1) * P], wdq_sb[:, k, j * P:(j + 1) * P], xnT[:, k, :],
                                         start=(k == 0), stop=(k == KD - 1))
                nc.tensor.transpose(ps_prep[:, 2 * P:3 * P], cs_sb[:, 0:P], identf[:, :])
                nc.tensor.transpose(ps_prep[:, 3 * P:4 * P], cs_sb[:, P:2 * P], identf[:, :]).then_inc(S["qc_done"], 1)

            def turn_keys(i):
                pe.wait_ge(S["qc_ready"], i + 1)
                for w in range(W):
                    mm = nc.tensor.transpose(ps_prep[:, w * P:(w + 1) * P], kwin[:, w * P:(w + 1) * P], identf[:, :])
                mm.then_inc(S["kt_done"], 1)

            def project(i, g):
                G = i * NG + g
                pe.wait_ge(S["qc_ready"], i + 1)
                wait(pe, S["ql_ready"], G)
                for j in range(GH):
                    h = g * GH + j
                    o = ps_qa[:, j * P:(j + 1) * P]
                    nc.tensor.matmul(o, uqk1[:, h, :], qcs[:, 0, :], start=True, stop=False)
                    mm = nc.tensor.matmul(o, uqk2[:, h % 8, :], qcs[:, 1 + h // 8, :], start=False, stop=True)
                mm.then_inc(S["ql_done"], 1)
                wait(pe, S["rope_ab"], G)
                for j in range(GH // 2):
                    c = (g * GH // 2 + j) * P
                    for n, w1 in enumerate((qrA, qrB)):
                        o = ps_qb[:, (2 * n + j) * P:(2 * n + j + 1) * P]
                        nc.tensor.matmul(o, w1[:, c:c + P], qcs[:, 0, :], start=True, stop=False)
                        mm = nc.tensor.matmul(o, qr2[:, c:c + P], qcs[:, 1 + n, :], start=False, stop=True)
                mm.then_inc(S["qr_done"], 1)

            def scores(i, u):
                U, g, s = i * NU + u, u // W, u % W
                G = i * NG + g
                wait(pe, S["sub_done"], U - 1)
                if s == 0:
                    pe.wait_ge(S["ql_ready"], G + 1)
                    pe.wait_ge(S["qr_ready"], G + 1)
                if u == 0:
                    pe.wait_ge(S["win_ready"], i + 1)
                bk = ps_s[u % 2]
                nc.tensor.matmul(bk[:, :], identb[:, :], mask[:, :].unsqueeze(1).to_broadcast([P, HU, KW]),
                                 start=True, stop=False)
                for j in range(HU):
                    hh = s * HU + j
                    o = bk[:, j * KW:(j + 1) * KW]
                    nc.tensor.matmul(o, ql[g % 2][:, hh, :], kwin[:, :], start=False, stop=False)
                    mm = nc.tensor.matmul(o, qrt[g % 2][:, hh // 2, :], krz[:, hh % 2, :], start=False, stop=(j == HU - 1))
                mm.then_inc(S["sc_done"], 1)

            def turn_probs(U, r):
                pe.wait_ge(S["p_ready"], U + 1)
                wait(pe, S["pt_ready"], U)
                for k in range(4):
                    mm = nc.tensor.transpose(ps_pt[:, k * P:(k + 1) * P], pr[r][:, k * P:(k + 1) * P], identf[:, :])
                mm.then_inc(S["pt_done"], 1)

            def mix(U, i):
                pe.wait_ge(S["pt_ready"], U + 1)
                pe.wait_ge(S["kv_ready"], i + 1)
                wait(pe, S["ol_ready"], U)
                for w in range(W):
                    mm = nc.tensor.matmul(ps_ol[:, 0:HU * P], kvwin[:, w, :],
                                          pt_sb[:, :].rearrange("p (j w n) -> p j w n", j=HU, w=W)[:, :, w, :],
                                          start=(w == 0), stop=(w == W - 1))
                mm.then_inc(S["pv_done"], 1)

            def out_proj(U, i, u):
                pe.wait_ge(S["ol_ready"], U + 1)
                if u == 0:
                    wait(pe, S["out_added"], i)
                for j in range(HU):
                    h = u * HU + j
                    mm = nc.tensor.matmul(ps_out[:, :], ol[u % 2][:, j, :], vo[:, h, :],
                                          start=(h == 0), stop=(h == H - 1))
                mm.then_inc(S["op_done"], 1)

            def tile(i, first=False, last=False):
                for u in range(NU):
                    U, g = i * NU + u, u // W
                    scores(i, u)
                    if not (first and u == 0):
                        turn_probs(U - 1, (u - 1) % 2)
                    if u == 0:
                        turn_keys(i)
                    if u % W == 0:
                        if g < NG - 1:
                            project(i, g + 1)
                        elif not last:
                            project(i + 1, 0)
                        if g == 1 and not last:
                            turn_x(i + 1)
                        if g == 2 and not last:
                            latent_q(i + 1)
                    if not (first and u == 0):
                        mix(U - 1, i if u else i - 1)
                    if not (first and u <= 1):
                        out_proj(U - 2, i if u > 1 else i - 1, (u - 2) % NU)

            pe.wait_ge(S["pool_const"], 4)
            pe.wait_ge(S["qw_ld"], 32)
            pe.wait_ge(S["uqk_ev"], 2 * NG)
            turn_x(0)
            latent_q(0)
            pe.wait_ge(S["vo_ev"], H)
            project(0, 0)
            tile(0, first=True)
            with pe.Fori(1, WCH) as i:
                tile(i)
            pe.wait_ge(S["asum_red"], 1)
            pe.wait_ge(S["qc_ready"], WCH + 1)
            nc.tensor.matmul(ps_prep[:, 0:NM], ones[:, :], asum1[:, :], start=True, stop=True).then_inc(S["gam_ps"], 1)
            pe.wait_ge(S["gam_a"], 1)
            with pe.Fori(WCH, T - 1) as i:
                tile(i)
            tile(T - 1, last=True)
            U = T * NU
            turn_probs(U - 1, (NU - 1) % 2)
            mix(U - 1, T - 1)
            out_proj(U - 2, T - 1, NU - 2)
            out_proj(U - 1, T - 1, NU - 1)

            def turn_xq(t):
                pe.wait_ge(S["xq_ready"], t + 1)
                wait(pe, S["xqT_ready"], t)
                for k in range(KD):
                    mm = nc.tensor.transpose(ps_xt[:, 0:256].bitcast(BF16)[:, k * P:(k + 1) * P], xq[:, k * P:(k + 1) * P], identb[:, :])
                mm.then_inc(S["xt2"], 1)

            def gate_val(t, c):
                C = t * FC + c
                if c == 0:
                    pe.wait_ge(S["xqT_ready"], t + 1)
                wait(pe, S["g_ready"], C - 1)
                for k in range(KD):
                    mm = nc.tensor.matmul(ps_g[c % 2][:, :], xqT[:, k, :], tern_g[:, k, c * 512:(c + 1) * 512],
                                          start=(k == 0), stop=(k == KD - 1))
                mm.then_inc(S["gate_ps"], 1)
                wait(pe, S["v_ready"], C - 1)
                for k in range(KD):
                    mm = nc.tensor.matmul(ps_v[c % 2][:, :], xqT[:, k, :], tern_v[:, k, c * 512:(c + 1) * 512],
                                          start=(k == 0), stop=(k == KD - 1))
                mm.then_inc(S["val_ps"], 1)

            def turn_h(t):
                pe.wait_ge(S["hq_ready"], t + 1)
                for j in range(4):
                    wait(pe, S["hqT_ready"], 4 * t + max(j - 1, 0))
                    for k in range(4):
                        mm = nc.tensor.transpose(ps_tr[j % 2][:, 0:256].bitcast(BF16)[:, k * P:(k + 1) * P],
                                                 hq[:, (4 * j + k) * P:(4 * j + k + 1) * P], identb[:, :])
                    mm.then_inc(S["tr_done"], 1)

            def down(t):
                wait(pe, S["y_ready"], t)
                for k in range(FK):
                    if k % 4 == 0:
                        pe.wait_ge(S["hqT_ready"], 4 * t + k // 4 + 1)
                    mm = nc.tensor.matmul(ps_o[:, :], hqT[:, k, :], tern_o[:, k, :], start=(k == 0), stop=(k == FK - 1))
                mm.then_inc(S["o_done"], 1)

            def ffn(t, first=False, last=False):
                gate_val(t, 0)
                gate_val(t, 1)
                if not first:
                    turn_h(t - 1)
                gate_val(t, 2)
                if not first:
                    down(t - 1)
                gate_val(t, 3)
                if not last:
                    turn_xq(t + 1)

            pe.wait_ge(S["sub_done"], T * NU)
            pe.wait_ge(S["ol_ready"], T * NU)
            pe.wait_ge(S["out_added"], T)
            pe.wait_ge(S["tern_done"], NM * WCH)
            turn_xq(0)
            ffn(0, first=True)
            with pe.Fori(1, T - 1) as t:
                ffn(t)
            ffn(T - 1, last=True)
            turn_h(T - 1)
            down(T - 1)

        @block.scalar
        def _(act):
            for g in range(NG):
                act.wait_ge(S["uqk_ps"], g + 1)
                half = 64 * (g // 2)
                nc.scalar.copy(uqk1[:, g * GH:(g + 1) * GH, :], ps_qa[:, :].rearrange("p (h n) -> p h n", h=GH)).then_inc(S["uqk_ev"], 1)
                nc.scalar.copy(uqk2[half:half + 64, (g % 2) * GH:(g % 2 + 1) * GH, :],
                               ps_qb[half:half + 64, :].rearrange("p (h n) -> p h n", h=GH)).then_inc(S["uqk_ev"], 1)
            act.wait_ge(S["kv_ps"], BATCH)
            for h in range(H):
                act.wait_ge(S["vo_ps"], h + 1)
                nc.scalar.copy(vo[:, h, :], (ps_qa if h % 2 == 0 else ps_qb)[:, :]).then_inc(S["vo_ev"], 1)

            def xT_out(i):
                act.wait_ge(S["xt_done"], i + 1)
                wait(act, S["qc_done"], i)
                nc.scalar.copy(xnT[:, :, :], ps_prep[:, :].rearrange("p (k n) -> p k n", k=KD)).then_inc(S["xnT_ready"], 1)

            def q_out(i):
                act.wait_ge(S["qc_done"], i + 1)
                wait(act, S["ql_done"], i * NG)
                wait(act, S["qr_done"], i * NG)
                wait(act, S["rope_ab"], i * NG)
                nc.scalar.copy(qcs[:, 0, :], ps_prep[:, 0:P])
                nc.scalar.copy(qcs[0:64, 1, :], ps_prep[0:64, P:2 * P])
                nc.scalar.copy(qcs[64:P, 2, :], ps_prep[64:P, P:2 * P])
                nc.scalar.copy(qcs[:, 3:5, :], ps_prep[:, 2 * P:4 * P].rearrange("p (k n) -> p k n", k=2)).then_inc(S["qc_ready"], 1)

            def keys_out(i):
                act.wait_ge(S["kt_done"], i + 1)
                wait(act, S["pv_done"], i * NU)
                nc.scalar.copy(kvwin[:, :, :], ps_prep[:, 0:KW].rearrange("p (w n) -> p w n", w=W)).then_inc(S["kv_ready"], 1)

            def ql_out(i, g):
                G = i * NG + g
                act.wait_ge(S["ql_done"], G + 1)
                wait(act, S["sc_done"], (G - 1) * W)
                nc.scalar.copy(ql[g % 2][:, :, :], ps_qa[:, :].rearrange("p (h n) -> p h n", h=GH)).then_inc(S["ql_ready"], 1)

            def probsT_out(U):
                act.wait_ge(S["pt_done"], U + 1)
                wait(act, S["pv_done"], U)
                nc.scalar.copy(pt_sb[:, :], ps_pt[:, :]).then_inc(S["pt_ready"], 1)

            def tile(i, first=False, last=False, sums=False):
                for u in range(NU):
                    U, g = i * NU + u, u // W
                    if not (first and u == 0):
                        probsT_out(U - 1)
                    act.wait_ge(S["sub_done"], U + 1)
                    nc.scalar.activation(pr[u % 2], pr[u % 2], ACT.Exp, scale=SCALE).then_inc(S["exp_done"], 1)
                    if u % W == 0:
                        if g < NG - 1:
                            ql_out(i, g + 1)
                        elif not last:
                            ql_out(i + 1, 0)
                        if g == 1 and not last:
                            xT_out(i + 1)
                        if g == 2 and not last:
                            q_out(i + 1)
                        if g == 3 and sums:
                            act.wait_ge(S["st_ld"], (i + 1) * 16 * NM)
                            for m in range(NM):
                                nc.scalar.activation(stage[:, m, :], stage[:, m, :], ACT.Abs,
                                                     accum_out=asum[:, m, bass.ds(i, 1)]).then_inc(S["sums_done"], 1)
                    if u == 0:
                        keys_out(i)

            act.wait_ge(S["zeros"], 1)
            xT_out(0)
            q_out(0)
            ql_out(0, 0)
            tile(0, first=True, sums=True)
            with act.Fori(1, WCH) as i:
                tile(i, sums=True)
            with act.Fori(WCH, T - 1) as i:
                tile(i)
            tile(T - 1, last=True)
            probsT_out(T * NU - 1)

            def xqT_out(t):
                act.wait_ge(S["xt2"], t + 1)
                wait(act, S["val_ps"], t * FC)
                nc.scalar.copy(xqT, ps_xt[:, 0:256].bitcast(BF16).rearrange("p (k n) -> p k n", k=KD)).then_inc(S["xqT_ready"], 1)

            def tanh(t, c):
                C = t * FC + c
                act.wait_ge(S["g_ready"], C + 1)
                wait(act, S["h_ready"], C - 1)
                nc.scalar.activation(th_sb[c % 2], g_sb[c % 2], ACT.Tanh, scale=0.5).then_inc(S["th_ready"], 1)

            def hT_out(t):
                for j in range(4):
                    act.wait_ge(S["tr_done"], 4 * t + j + 1)
                    wait(act, S["o_done"], t)
                    nc.scalar.copy(hqT[:, 4 * j:4 * j + 4, :],
                                   ps_tr[j % 2][:, 0:256].bitcast(BF16).rearrange("p (k n) -> p k n", k=4)).then_inc(S["hqT_ready"], 1)

            def hq_out(t):
                act.wait_ge(S["hr_done"], t + 1)
                wait(act, S["tr_done"], 4 * t)
                nc.scalar.activation(hq, h_sb, ACT.Copy, bias=-MAGIC).then_inc(S["hq_ready"], 1)

            def ffn(t, first=False, last=False):
                tanh(t, 0)
                tanh(t, 1)
                if not first:
                    hT_out(t - 1)
                tanh(t, 2)
                tanh(t, 3)
                if not last:
                    xqT_out(t + 1)
                hq_out(t)

            xqT_out(0)
            ffn(0, first=True)
            with act.Fori(1, T - 1) as t:
                ffn(t)
            ffn(T - 1, last=True)
            hT_out(T - 1)

        @block.gpsimd
        def _(pool):
            nc.gpsimd.memset(identf[:, :], 0.0).then_inc(S["pool_const"], 1)
            nc.gpsimd.memset(ones[:, :], 1.0).then_inc(S["pool_const"], 1)
            nc.gpsimd.memset(mhalf[:, :], -0.5)
            nc.gpsimd.iota(iota_i, pattern=[[1, KW]], base=0, channel_multiplier=0).then_inc(S["pool_const"], 1)
            nc.gpsimd.memset(krz[:, :, :], 0.0)
            nc.gpsimd.memset(qcs[:, :, :], 0.0).then_inc(S["zeros"], 1)
            pool.wait_ge(S["pool_const"], 3)
            nc.gpsimd.affine_select(out=identf[:, :], in_=identf[:, :], compare_op=ALU.not_equal, fill=1.0, base=0,
                                    pattern=[[-1, P]], channel_multiplier=1).then_inc(S["pool_const"], 1)

            def inv_std(i, veps, done):
                pool.wait_ge(veps, i + 1)
                nc.gpsimd.tensor_tensor(rstd[:, :], ve[:, :], mhalf[:, :], ALU.pow).then_inc(done, 1)

            def rope_add(i, g):
                G = i * NG + g
                pool.wait_ge(S["rope_ab"], G + 1)
                wait(pool, S["sc_done"], (G - 1) * W)
                nc.gpsimd.tensor_tensor(qrt[g % 2][:, :, :], tA[:, :, :], tB[:, :, :], ALU.add).then_inc(S["qr_ready"], 1)

            def tile(i, last=False):
                for u in range(NU):
                    U, g = i * NU + u, u // W
                    pool.wait_ge(S["rec_done"], U + 1)
                    p3 = pr[u % 2].rearrange("p (j n) -> p j n", j=HU)
                    nc.gpsimd.tensor_tensor(p3, p3, rc[u % 2][:, :].unsqueeze(2).to_broadcast([P, HU, KW]),
                                            ALU.mult).then_inc(S["p_ready"], 1)
                    if u % W == 0:
                        if g < NG - 1:
                            rope_add(i, g + 1)
                        elif not last:
                            rope_add(i + 1, 0)
                    if u == 0 and not last:
                        inv_std(i + 1, S["veps_done"], S["rstd_ready"])

            inv_std(0, S["veps_done"], S["rstd_ready"])
            rope_add(0, 0)
            with pool.Fori(0, T - 1) as i:
                tile(i)
            tile(T - 1, last=True)

            def hidden(t, c):
                C = t * FC + c
                pool.wait_ge(S["t_ready"], C + 1)
                pool.wait_ge(S["v_ready"], C + 1)
                wait(pool, S["hq_ready"], t)
                nc.gpsimd.tensor_tensor(h_sb[:, c * 512:(c + 1) * 512], th_sb[c % 2], v_sb[c % 2], ALU.mult).then_inc(S["h_ready"], 1)

            def x_bias(t):
                xt = x_all[:, bass.ds(t, 1), :].rearrange("p o n -> p (o n)")
                nc.gpsimd.tensor_tensor(xt, xt, ob_sb, ALU.add).then_inc(S["xb_ready"], 1)

            def ffn(t, last=False):
                for c in range(FC):
                    if c == 2:
                        if not last:
                            inv_std(t + 1, S["veps2"], S["rstd2"])
                        pool.wait_ge(S["xn2"], t + 1)
                        x_bias(t)
                    hidden(t, c)

            inv_std(0, S["veps2"], S["rstd2"])
            pool.wait_ge(S["bias_ld"], 48)
            with pool.Fori(0, T - 1) as t:
                ffn(t)
            ffn(T - 1, last=True)

        @block.vector
        def _(dve):
            dve.wait_ge(S["pool_const"], 4)
            nc.vector.tensor_copy(iota[:, :], iota_i)
            nc.vector.tensor_copy(identb[:, :], identf[:, :])
            dve.wait_ge(S["const_ld"], 48)
            nc.vector.tensor_copy(seg_hi[:, :], seg_i[:, :]).then_inc(S["dve_const"], 1)
            dve.wait_ge(S["dve_const"], 1)
            nc.vector.tensor_scalar(seg_lo[:, :], seg_hi[:, :], -float(LOOKBACK), None, ALU.add).then_inc(S["dve_const"], 1)
            for b in range(BATCH):
                kb = slice(b * LK, (b + 1) * LK)
                dve.wait_ge(S["kv_ps"], b + 1)
                nc.vector.tensor_copy(kv_cT[:, kb], ps_s[0][:, :]).then_inc(S["kv_ev"], 1)
                dve.wait_ge(S["kr_ps"], b + 1)
                nc.vector.tensor_tensor(kropeT[:, kb], ps_s[1][:, :], cosn_sb, ALU.mult).then_inc(S["kr_mul"], 1)
                wait(dve, S["kr_ready"], b)
                nc.vector.tensor_tensor(pt_sb[:, :], ps_pt[:, :], sinn_sb, ALU.mult).then_inc(S["kr_mul"], 1)
                dve.wait_ge(S["kr_mul"], 2 * b + 2)
                nc.vector.tensor_tensor(kropeT[:, kb], kropeT[:, kb], pt_sb[:, :], ALU.add).then_inc(S["kr_ready"], 1)
            dve.wait_ge(S["kr_ready"], BATCH)

            def stats(i, bn, aggr, veps):
                nc.vector.bn_stats(st6[:, :], x_all[:, bass.ds(i, 1), :].rearrange("p o n -> p (o n)")).then_inc(bn, 1)
                dve.wait_ge(bn, i + 1)
                nc.vector.memset(carry[:, :], 0.0)
                nc.vector.bn_aggr(mv[:, :], st6[:, :]).then_inc(aggr, 1)
                dve.wait_ge(aggr, i + 1)
                nc.vector.tensor_scalar(ve[:, :], mv[:, 1:2], EPS, None, ALU.add).then_inc(veps, 1)

            def norm(i, rs, done):
                dve.wait_ge(rs, i + 1)
                nc.vector.tensor_scalar(xn[:, :], x_all[:, bass.ds(i, 1), :].rearrange("p o n -> p (o n)"),
                                        mv[:, 0:1], rstd[:, :], ALU.subtract, ALU.mult).then_inc(done, 1)

            def windows(i):
                wait(dve, S["sc_done"], i * NU)
                wait(dve, S["kt_done"], i)
                off = (i // 4) * LK
                nc.vector.tensor_copy(kwin[:, :], kv_cT[:, bass.ds(off, KW)]).then_inc(S["win_copied"], 1)
                nc.vector.tensor_copy(krz[0:64, 0, :], kropeT[0:64, bass.ds(off, KW)]).then_inc(S["win_copied"], 1)
                nc.vector.tensor_copy(krz[64:P, 1, :], kropeT[64:P, bass.ds(off, KW)]).then_inc(S["win_copied"], 1)
                nc.vector.tensor_scalar(mask[:, :], iota[:, :], seg_hi[:, bass.ds(i, 1)], NEG, ALU.is_gt, ALU.mult).then_inc(S["mask_parts"], 1)
                nc.vector.tensor_scalar(maskt[:, :], iota[:, :], seg_lo[:, bass.ds(i, 1)], NEG, ALU.is_lt, ALU.mult).then_inc(S["mask_parts"], 1)
                dve.wait_ge(S["mask_parts"], 2 * i + 2)
                dve.wait_ge(S["win_copied"], 3 * i + 3)
                nc.vector.tensor_tensor(mask[:, :], mask[:, :], maskt[:, :], ALU.add).then_inc(S["win_ready"], 1)

            def rope_mul(i, g):
                G = i * NG + g
                n = GH // 2
                dve.wait_ge(S["qr_done"], G + 1)
                dve.wait_ge(S["qc_ready"], i + 1)
                wait(dve, S["qr_ready"], G)
                nc.vector.tensor_tensor(tA[:, :, :], ps_qb[:, 0:n * P].rearrange("p (j n) -> p j n", j=n),
                                        qcs[:, 3, :].unsqueeze(1).to_broadcast([P, n, P]), ALU.mult)
                nc.vector.tensor_tensor(tB[:, :, :], ps_qb[:, n * P:2 * n * P].rearrange("p (j n) -> p j n", j=n),
                                        qcs[:, 4, :].unsqueeze(1).to_broadcast([P, n, P]), ALU.mult).then_inc(S["rope_ab"], 1)

            def latent_out(U, r):
                dve.wait_ge(S["pv_done"], U + 1)
                wait(dve, S["op_done"], U - 1)
                nc.vector.tensor_copy(ol[r][:, :, :], ps_ol[:, 0:HU * P].rearrange("p (j n) -> p j n", j=HU)).then_inc(S["ol_ready"], 1)

            def add_out(i):
                dve.wait_ge(S["op_done"], (i + 1) * NU)
                xt = x_all[:, bass.ds(i, 1), :].rearrange("p o n -> p (o n)")
                nc.vector.tensor_tensor(xt, ps_out[:, :], xt, ALU.add).then_inc(S["out_added"], 1)

            def ternary(i):
                c = i - WCH
                dve.wait_ge(S["st_ld"], (i + 1) * 16 * NM)
                for m in range(NM):
                    if m:
                        dve.wait_ge(S["tern_done"], c * NM + m)
                    nc.vector.tensor_scalar(tmpb[:, :], stage[:, m, :], nthr[:, m:m + 1], None, ALU.is_lt).then_inc(S["tern_lt"], 1)
                    dve.wait_ge(S["tern_lt"], c * NM + m + 1)
                    nc.vector.scalar_tensor_tensor(out=tern[:, m, bass.ds(c * WC, WC)], in0=stage[:, m, :], scalar=thr[:, m:m + 1],
                                                   in1=tmpb[:, :], op0=ALU.is_gt, op1=ALU.subtract).then_inc(S["tern_done"], 1)

            def tile(i, first=False, last=False, terns=False):
                for u in range(NU):
                    U, g = i * NU + u, u // W
                    if u == 0:
                        windows(i)
                    sc3 = ps_s[u % 2][:, :].rearrange("p (j n) -> p j n", j=HU)
                    p3 = pr[u % 2].rearrange("p (j n) -> p j n", j=HU)
                    dve.wait_ge(S["sc_done"], U + 1)
                    nc.vector.tensor_reduce(mx[u % 2][:, :], sc3, AX.X, ALU.max).then_inc(S["max_done"], 1)
                    dve.wait_ge(S["max_done"], U + 1)
                    wait(dve, S["pt_done"], U - 1)
                    nc.vector.tensor_tensor(p3, sc3, mx[u % 2][:, :].unsqueeze(2).to_broadcast([P, HU, KW]),
                                            ALU.subtract).then_inc(S["sub_done"], 1)
                    dve.wait_ge(S["exp_done"], U + 1)
                    nc.vector.tensor_reduce(sm[u % 2][:, :], p3, AX.X, ALU.add).then_inc(S["sum_done"], 1)
                    dve.wait_ge(S["sum_done"], U + 1)
                    nc.vector.reciprocal(rc[u % 2][:, :], sm[u % 2][:, :]).then_inc(S["rec_done"], 1)
                    if u % W == 0:
                        if g < NG - 1:
                            rope_mul(i, g + 1)
                        elif not last:
                            rope_mul(i + 1, 0)
                    if not (first and u == 0):
                        latent_out(U - 1, (u - 1) % 2)
                    if u == 1 and not first:
                        add_out(i - 1)
                    if u == 0 and not last:
                        wait(dve, S["xt_done"], i + 1)
                        stats(i + 1, S["bn_done"], S["aggr_done"], S["veps_done"])
                        norm(i + 1, S["rstd_ready"], S["xn_ready"])
                    if u == 3 * W and terns:
                        ternary(i)

            dve.wait_ge(S["x_ld"], 32)
            stats(0, S["bn_done"], S["aggr_done"], S["veps_done"])
            norm(0, S["rstd_ready"], S["xn_ready"])
            rope_mul(0, 0)
            dve.wait_ge(S["zeros"], 1)
            tile(0, first=True)
            with dve.Fori(1, WCH) as i:
                tile(i)
            dve.wait_ge(S["sums_done"], NM * WCH)
            nc.vector.tensor_reduce(asum1[:, :], asum[:, :, :], AX.X, ALU.add).then_inc(S["asum_red"], 1)
            dve.wait_ge(S["gam_ps"], 1)
            nc.vector.tensor_scalar(gam[:, :], ps_prep[:, 0:NM], 1.0 / (DM * HID), 1e-5, ALU.mult, ALU.max).then_inc(S["gam_a"], 1)
            dve.wait_ge(S["gam_a"], 1)
            nc.vector.tensor_scalar(thr[:, :], gam[:, :], 0.5, None, ALU.mult).then_inc(S["gam_b"], 1)
            nc.vector.tensor_scalar(nthr[:, :], gam[:, :], -0.5, None, ALU.mult).then_inc(S["gam_b"], 1)
            dve.wait_ge(S["gam_b"], 2)
            dve.wait_ge(S["vo_ps"], H)
            with dve.Fori(WCH, T - 1) as i:
                tile(i, terns=True)
            tile(T - 1, last=True, terns=True)
            latent_out(T * NU - 1, (NU - 1) % 2)
            add_out(T - 1)

            def quant_x(t):
                dve.wait_ge(S["out_added"], T) if isinstance(t, int) and t == 0 else None
                stats(t, S["bn2"], S["aggr2"], S["veps2"])
                norm(t, S["rstd2"], S["xn2"])
                dve.wait_ge(S["xn2"], t + 1)
                nc.vector.tensor_reduce(gx[:, :], xn[:, :], AX.X, ALU.max, apply_absolute_value=True).then_inc(S["gx2"], 1)
                dve.wait_ge(S["gx2"], t + 1)
                nc.vector.tensor_scalar(gxc[:, :], gx[:, :], 1e-5, None, ALU.max).then_inc(S["gxc2"], 1)
                dve.wait_ge(S["gxc2"], t + 1)
                nc.vector.reciprocal(rx[:, :], gxc[:, :]).then_inc(S["rx2"], 1)
                nc.vector.tensor_scalar(dx[:, :], gxc[:, :], 1.0 / 127.0, None, ALU.mult).then_inc(S["dx2"], 1)
                dve.wait_ge(S["rx2"], t + 1)
                nc.vector.tensor_scalar(sx[:, :], rx[:, :], 127.0, None, ALU.mult).then_inc(S["sx2"], 1)
                dve.wait_ge(S["sx2"], t + 1)
                nc.vector.tensor_scalar(xn[:, :], xn[:, :], sx[:, :], MAGIC, ALU.mult, ALU.add).then_inc(S["xr2"], 1)
                dve.wait_ge(S["xr2"], t + 1)
                wait(dve, S["xt2"], t)
                nc.vector.tensor_scalar(xq, xn[:, :], -MAGIC, None, ALU.add).then_inc(S["xq_ready"], 1)

            def scale_x(t):
                dve.wait_ge(S["dx2"], t + 1)
                nc.vector.tensor_scalar(sgv[:, :], gam[:, 0:2], dx[:, :], None, ALU.mult).then_inc(S["sgv_ready"], 1)
                dve.wait_ge(S["sgv_ready"], t + 1)

            def max_h(t, c):
                dve.wait_ge(S["h_ready"], t * FC + c + 1)
                nc.vector.tensor_reduce(mh4[:, c:c + 1], h_sb[:, c * 512:(c + 1) * 512], AX.X, ALU.max,
                                        apply_absolute_value=True).then_inc(S["mh_part"], 1)

            def chunk(t, c):
                C = t * FC + c
                dve.wait_ge(S["gate_ps"], C + 1)
                wait(dve, S["t_ready"], C - 1)
                nc.vector.scalar_tensor_tensor(out=g_sb[c % 2], in0=ps_g[c % 2][:, :], scalar=sgv[:, 0:1],
                                               in1=gb_sb[:, c * 512:(c + 1) * 512], op0=ALU.mult, op1=ALU.add).then_inc(S["g_ready"], 1)
                dve.wait_ge(S["val_ps"], C + 1)
                wait(dve, S["h_ready"], C - 1)
                nc.vector.scalar_tensor_tensor(out=v_sb[c % 2], in0=ps_v[c % 2][:, :], scalar=sgv[:, 1:2],
                                               in1=vb_sb[:, c * 512:(c + 1) * 512], op0=ALU.mult, op1=ALU.add).then_inc(S["v_ready"], 1)
                if c:
                    max_h(t, c - 1)
                dve.wait_ge(S["th_ready"], C + 1)
                nc.vector.scalar_tensor_tensor(out=th_sb[c % 2], in0=th_sb[c % 2], scalar=1.0, in1=g_sb[c % 2],
                                               op0=ALU.add, op1=ALU.mult).then_inc(S["t_ready"], 1)

            def quant_h(t):
                dve.wait_ge(S["mh_part"], (t + 1) * FC)
                nc.vector.tensor_reduce(mh[:, :], mh4[:, :], AX.X, ALU.max).then_inc(S["mh_done"], 1)
                dve.wait_ge(S["mh_done"], t + 1)
                nc.vector.tensor_scalar(gh[:, :], mh[:, :], 0.5, 1e-5, ALU.mult, ALU.max).then_inc(S["gh_done"], 1)
                dve.wait_ge(S["gh_done"], t + 1)
                nc.vector.reciprocal(rh[:, :], gh[:, :]).then_inc(S["rh_done"], 1)
                dve.wait_ge(S["rh_done"], t + 1)
                nc.vector.tensor_scalar(sh[:, :], rh[:, :], 63.5, None, ALU.mult).then_inc(S["sh_done"], 1)
                dve.wait_ge(S["sh_done"], t + 1)
                nc.vector.tensor_scalar(h_sb, h_sb, sh[:, :], MAGIC, ALU.mult, ALU.add).then_inc(S["hr_done"], 1)

            def finish(t):
                dve.wait_ge(S["o_done"], t + 1)
                dve.wait_ge(S["xb_ready"], t + 1)
                dve.wait_ge(S["so_ready"], t + 1)
                xt = x_all[:, bass.ds(t, 1), :].rearrange("p o n -> p (o n)")
                nc.vector.scalar_tensor_tensor(out=xt, in0=ps_o[:, :], scalar=so[:, :], in1=xt,
                                               op0=ALU.mult, op1=ALU.add).then_inc(S["y_ready"], 1)

            def scale_o(t):
                nc.vector.tensor_scalar(so[:, :], gh[:, :], 1.0 / 127.0, gam[:, 2:3], ALU.mult, ALU.mult).then_inc(S["so_ready"], 1)

            def ffn(t, first=False, last=False):
                scale_x(t)
                chunk(t, 0)
                chunk(t, 1)
                chunk(t, 2)
                if not last:
                    quant_x(t + 1)
                chunk(t, 3)
                if not first:
                    finish(t - 1)
                max_h(t, 3)
                quant_h(t)
                scale_o(t)

            quant_x(0)
            dve.wait_ge(S["op_done"], T * NU)
            dve.wait_ge(S["bias_ld"], 48)
            ffn(0, first=True)
            with dve.Fori(1, T - 1) as t:
                ffn(t)
            ffn(T - 1, last=True)
            finish(T - 1)


def kernel(x, ctx_2048, itok_BxS_0_1023, L0_xattn_W_kvc, L0_xattn_W_dq, L0_xattn_W_uq, L0_xattn_W_qr,
           L0_xattn_W_uk, L0_xattn_W_kr, L0_xattn_W_uv, L0_xattn_W_o, L0_ffn_gate_w, L0_ffn_gate_b,
           L0_ffn_val_w, L0_ffn_val_b, L0_ffn_out_w, L0_ffn_out_b):
    import concourse.bacc as bacc
    from concourse.bass_utils import run_bass_kernel_spmd

    a = np.asarray
    half = ROPE // 2
    inv = (np.float32(1.0) / np.float32(10000.0) ** (np.arange(half, dtype=np.float32) / np.float32(half))).astype(np.float32)
    ang = np.arange(LQ, dtype=np.float32)[:, None] * inv
    cos, sin = np.cos(ang).astype(np.float32), np.sin(ang).astype(np.float32)
    cs = np.concatenate([cos] * 4 + [-sin, sin] * 2, axis=1)
    cosn = np.concatenate([cos.T] * 4, axis=0)
    sinn = np.concatenate([-sin.T, sin.T] * 2, axis=0)

    def swap(w):
        return np.concatenate([w.reshape(w.shape[0], -1, 2, half)[:, :, 1:2], w.reshape(w.shape[0], -1, 2, half)[:, :, 0:1]],
                              axis=2).reshape(w.shape)

    dq, wqr, wkr = a(L0_xattn_W_dq), a(L0_xattn_W_qr), a(L0_xattn_W_kr)
    arrays = {
        "x": a(x).reshape(TOK, DM),
        "ctxT": a(ctx_2048).transpose(0, 2, 1),
        "itok": a(itok_BxS_0_1023).reshape(T, P).T,
        "cs": cs, "cosn": cosn, "sinn": sinn,
        "wkvc": a(L0_xattn_W_kvc),
        "wdq": np.concatenate([dq, dq[:, P:QC]], axis=1),
        "uqT": a(L0_xattn_W_uq).T,
        "ukT": a(L0_xattn_W_uk).T,
        "uvT": a(L0_xattn_W_uv).T,
        "wo": a(L0_xattn_W_o),
        "qr": np.concatenate([wqr[0:P], swap(wqr)[0:P], np.concatenate([wqr[P:QC], swap(wqr)[P:QC]], axis=0)], axis=1),
        "kr": np.stack([np.concatenate([wkr, wkr], axis=1), np.concatenate([swap(wkr), swap(wkr)], axis=1)], axis=1),
        "gate": a(L0_ffn_gate_w).T.reshape(KD, P, 2, HID // 2).transpose(0, 2, 1, 3).reshape(WCH, P, WC),
        "val": a(L0_ffn_val_w).T.reshape(KD, P, 2, HID // 2).transpose(0, 2, 1, 3).reshape(WCH, P, WC),
        "outw": a(L0_ffn_out_w).T.reshape(WCH, 2, P, DM).transpose(0, 2, 1, 3).reshape(WCH, P, WC),
        "gate_b": a(L0_ffn_gate_b), "val_b": a(L0_ffn_val_b), "out_b": a(L0_ffn_out_b),
    }
    arrays = {n: np.ascontiguousarray(v) for n, v in arrays.items()}
    nc = bacc.Bacc("TRN2", target_bir_lowering=False, num_devices=1)
    args = [nc.dram_tensor(f"in_{n}", v.shape, mybir.dt.from_np(v.dtype), kind="ExternalInput").ap() for n, v in arrays.items()]
    args.append(nc.dram_tensor("y", (TOK, DM), F32, kind="ExternalOutput").ap())
    build(nc, *args)
    r = run_bass_kernel_spmd(nc, [{f"in_{n}": v for n, v in arrays.items()}], core_ids=[0])
    return r.results[0]["y"].reshape(BATCH, LQ, DM)
```

```python
from contextlib import ExitStack

import numpy as np

import concourse.bass as bass
from concourse import mybir

ALU = mybir.AluOpType
ACT = mybir.ActivationFunctionType
AX = mybir.AxisListType
F32 = mybir.dt.float32
BF16 = mybir.dt.bfloat16
I32 = mybir.dt.int32
U32 = mybir.dt.uint32

P = 128
BATCH, LQ, LK, DM = 4, 512, 512, 512
H, HD, ROPE, KVC, QC = 16, 128, 64, 128, 192
HID = 2048
LOOKBACK = 8
NEG = -1e30
EPS = 1e-5
SCALE = float(1.0 / np.sqrt(HD + ROPE).astype(np.float32))
MAGIC = 12582912.0
TOK = BATCH * LQ
T = TOK // P
KD = DM // P
NG = 4
GH = H // NG
FC = 4
FK = HID // P
NM = 3
WCOL = DM * HID // P
WCH = 8
WC = WCOL // WCH


def wait(eng, sem, value):
    if not (isinstance(value, int) and value <= 0):
        eng.wait_ge(sem, value)


def build(nc, x, ctxT, itok, itokT, cs, cosn, sinn, wkvc, wdq, uqT, ukT, uvT, wo, qr, kr, gate, val, outw,
          gate_b, val_b, out_b, y):
    WMAX = LK // P
    ctx = ExitStack()
    with ctx:
        def sb(name, shape, dt=F32):
            return ctx.enter_context(nc.sbuf_tensor(name, shape, dt))

        def sem(name):
            return ctx.enter_context(nc.semaphore(name))

        bank = [ctx.enter_context(nc.psum_tensor(f"bank{n}", [P, 512], F32)) for n in range(8)]
        ps_s = bank[0:2]
        ps_pt, ps_ol = bank[2:4]
        ps_qa, ps_qb = bank[4:6]
        ps_out, ps_prep = bank[6:8]
        ps_g, ps_v, ps_tr = bank[0:2], bank[2:4], bank[4:6]
        ps_o, ps_xt = bank[6:8]

        x_all = sb("x_all", [P, T, DM])
        kv_cT = sb("kv_cT", [P, TOK])
        kropeT = sb("kropeT", [P, TOK])
        identf = sb("identf", [P, P])
        identb = sb("identb", [P, P], BF16)
        ones = sb("ones", [P, P])
        iota = sb("iota", [P, LK])
        mhalf = sb("mhalf", [P, 1])
        sel = sb("sel", [P, 2, P])
        seg_i = sb("seg_i", [P, T], I32)
        xnT = sb("xnT", [P, KD, P])
        early = xnT[:, :, :].rearrange("p k n -> p (k n)")
        gpos_i = early[:, 0:16].bitcast(I32)
        lpos_i = early[:, 16:32].bitcast(I32)
        bpos_i = early[:, 32:48].bitcast(I32)
        bpos = early[:, 48:64]
        key_c = early[:, 64:80]
        rank = early[:, 80:96]
        val_c = early[:, 96:128].rearrange("p (t n) -> p t n", n=2)
        bad = early[:, 128:192].rearrange("p (n t) -> p n t", n=4)
        seg_s = sb("seg_s", [P, T])
        idx = sb("idx", [P, T], I32)
        idx_b = sb("idx_b", [P, T], I32)
        idx_cs = sb("idx_cs", [P, 1], I32)
        idx_y = sb("idx_y", [P, 1], I32)
        base = sb("base", [P, T])
        off_i = sb("off_i", [P, T], I32)
        flag = sb("flag", [P, 1])
        flag_i = sb("flag_i", [P, 1], I32)
        seg_hi = {1: sb("seg_hi1", [P, T]), WMAX: seg_s}
        seg_lo = {1: sb("seg_lo1", [P, T]), WMAX: sb("seg_lo4", [P, T])}
        asum = sb("asum", [P, NM, WCH])
        asum1 = sb("asum1", [P, NM])
        gam = sb("gam", [P, NM])
        thr = sb("thr", [P, NM])
        nthr = sb("nthr", [P, NM])

        xf = x_all[:, :, :].rearrange("p t n -> p (t n)")
        seg_r = xf[:, 0:2048].bitcast(I32)
        key_r = xf[:, 2048:4096]
        onehot = xf[:, 4096:6144].rearrange("p (t n) -> p t n", t=4)
        sort_junk = xf[:, 6144:6656]
        lrow_i = xf[:, 6656:7168].bitcast(I32)

        tern = sb("tern", [P, NM, WCOL], BF16)
        ternf = tern[:, :, :].rearrange("p m c -> p (m c)").bitcast(F32)
        wo_sb = ternf[:, 0:8192].rearrange("p (h n) -> p h n", h=H)
        ukT_sb = ternf[:, 8192:10240].rearrange("p (h n) -> p h n", h=H)
        uvT_sb = ternf[:, 10240:12288].rearrange("p (h n) -> p h n", h=H)
        tern_g = tern[:, 0, :].rearrange("p (k n) -> p k n", k=KD)
        tern_v = tern[:, 1, :].rearrange("p (k n) -> p k n", k=KD)
        tern_o = tern[:, 2, :].rearrange("p (k n) -> p k n", k=FK)

        stage = sb("stage", [P, NM, WC])
        uqT_sb = stage[:, :, :].rearrange("p m c -> p (m c)").rearrange("p (h n) -> p h n", h=H)

        vo = sb("vo", [P, H, DM])
        vof = vo[:, :, :].rearrange("p h n -> p (h n)")
        ctx_sb = vof.rearrange("p (b k n) -> p b k n", b=BATCH, k=KD)
        h_sb = vof[:, 0:2048]
        s_sb = [vof[:, 2048 + 512 * n:2560 + 512 * n] for n in range(2)]
        hq = vof[:, 3072:4096].bitcast(BF16)
        hqT = vof[:, 4096:5120].bitcast(BF16).rearrange("p (k n) -> p k n", k=FK)
        stf = stage[:, :, :].rearrange("p m c -> p (m c)")
        xq = stf[:, 0:256].bitcast(BF16)
        xqT = stf[:, 256:512].bitcast(BF16).rearrange("p (k n) -> p k n", k=KD)
        sxs = stf[:, 512:516].bitcast(BF16)
        sxT = stf[:, 576:640].bitcast(BF16)

        projw = sb("projw", [P, 6144])
        uqk1 = projw[:, 0:2048].rearrange("p (h n) -> p h n", h=H)
        uqk2 = projw[:, 2048:3072].rearrange("p (h n) -> p h n", h=H // 2)
        qrA = projw[:, 3072:4096]
        qrB = projw[:, 4096:5120]
        qr2 = projw[:, 5120:6144]
        brow = projw[:, 0:2048].bitcast(BF16).rearrange("p (m n) -> p m n", m=2)
        ob_sb = projw[:, 4096:4608]
        b_sb = sb("b_sb", [P, 2, HID // P])
        brest = sb("brest", [P, 2, HID // P])
        bsplit = sb("bsplit", [P, 3, 2, HID // P], BF16)
        rgam = sb("rgam", [P, 2])
        wdq_sb = sb("wdq_sb", [P, KD, 256])

        xn = sb("xn", [P, DM])
        iota_i = xn[:, :].bitcast(I32)
        qcs = sb("qcs", [P, 5, P])
        cs_sb = sb("cs_sb", [P, 2 * P])
        win = sb("win", [P, 4 * LK])
        ol_few = sb("ol_few", [P, 2, P])

        def key_windows(W):
            KW, HU = W * P, GH // W
            kwin = win[:, 0:KW]
            krz = win[:, KW:3 * KW].rearrange("p (n k) -> p n k", n=2)
            kvwin = win[:, 3 * KW:4 * KW].rearrange("p (w n) -> p w n", w=W)
            wide = win[:, 2 * LK:4 * LK].rearrange("p (r j n) -> p r j n", r=2, j=GH)
            ol = [wide[:, n, :, :] if W == 1 else ol_few[:, n:n + 1, :] for n in range(2)]
            return kwin, krz, kvwin, ol

        mask4 = sb("mask", [P, LK], BF16)
        st6 = sb("st6", [P, 6])
        mv = sb("mv", [P, 2])
        carry = sb("carry", [P, 1])
        carry_p = sb("carry_p", [P, 1])
        ve = sb("ve", [P, 1])
        rstd = sb("rstd", [P, 1])
        ql = [sb(f"ql{n}", [P, GH, P]) for n in range(2)]
        wkvc_sb = ql[0]
        kr_sb = ql[1]
        qrt = [sb(f"qrt{n}", [P, GH // 2, P]) for n in range(2)]
        tA = sb("tA", [P, GH // 2, P])
        tB = sb("tB", [P, GH // 2, P])
        pr_all = sb("pr_all", [P, 2, 512])
        pr = [pr_all[:, n, :] for n in range(2)]
        cosn_sb, sinn_sb = pr
        mx4 = [sb(f"mx{n}", [P, GH]) for n in range(2)]
        sm4 = [sb(f"sm{n}", [P, GH]) for n in range(2)]
        rc4 = [sb(f"rc{n}", [P, GH]) for n in range(2)]
        pt_sb = sb("pt_sb", [P, 512])
        tmpb = sb("tmpb", [P, WC], BF16)
        maskt4 = tmpb[:, 0:LK]
        y_sb = pt_sb[:, :]
        tAf = tA[:, :, :].rearrange("p j n -> p (j n)")
        gx, gxc, rx, sx, dx, mh, gh, rh, sh, so, sxr = (tAf[:, n:n + 1] for n in range(11))
        sgv, mh4 = tAf[:, 16:18], tAf[:, 20:20 + FC]

        names = """const_ld seg_ld ctx_ld0 ctx_ld1 ctx_ld2 ctx_ld3 kvw_ld uw_ld vow_ld x0_ld x_ld qw_ld cs_ld st_ld bias_ld stored
            pool_const dve_const zeros sort_step onehot_ready perm_ps idx_ready seg_ready edge_ps
            flag_ready cs_idx y_idx kv_ps kv_ev kr_ps kr_mul kr_ready uqk_ps uqk_ev vo_ps vo_ev
            sc_done pt_done pv_done ql_done qr_done op_done xt_done qc_done kt_done
            max_done sub_done sum_done rec_done ol_ready rope_ab out_added win_copied mask_parts
            win_ready bn_done aggr_done veps_done xn_ready exp_done pt_ready ql_ready kv_ready
            xnT_ready qc_ready p_ready qr_ready rstd_ready sums_done tern_lt tern_done
            asum_red gam_ps gam_ready gam_a gam_b
            bn2 aggr2 veps2 rstd2 xn2 gx2 gxc2 rx2 sx2 xr2 xq_ready dx2 sgv_ready xt2 xqT_ready gate_ps val_ps
            b_ld brow_zero brow_ld bias_step c0 c1 c2
            s_ready h_ready mh_part mh_done gh_done rh_done sh_done hr_done
            hq_ready tr_done hqT_ready o_done so_ready xb_ready y_ready""".split()
        S = {n: sem(n) for n in names}

        block = ctx.enter_context(nc.Block())

        @block.sync
        def _(sp):
            sp.dma_start(b_sb[:, 0, :], gate_b.rearrange("(p n) -> p n", p=P)).then_inc(S["b_ld"], 16)
            sp.dma_start(b_sb[:, 1, :], val_b.rearrange("(p n) -> p n", p=P)).then_inc(S["b_ld"], 16)
            sp.dma_start(seg_i[:, :], itokT).then_inc(S["seg_ld"], 16)
            sp.dma_start(seg_r, itok.partition_broadcast(P)).then_inc(S["seg_ld"], 16)
            sp.dma_start(pr_all[:, 0, :], cosn).then_inc(S["const_ld"], 16)
            sp.dma_start(pr_all[:, 1, :], sinn).then_inc(S["const_ld"], 16)
            sp.dma_start(wkvc_sb[:, :, :], wkvc.rearrange("(k p) n -> p k n", p=P)).then_inc(S["kvw_ld"], 16)
            sp.dma_start(kr_sb[:, 0:2, :], kr).then_inc(S["kvw_ld"], 16)
            for b in range(BATCH):
                sp.dma_start(ctx_sb[:, b, :, :], ctxT[b].rearrange("(k p) n -> p k n", p=P)).then_inc(S[f"ctx_ld{b}"], 16)
            sp.dma_start(uqT_sb, uqT.rearrange("(h p) n -> p h n", p=P)).then_inc(S["uw_ld"], 16)
            sp.dma_start(ukT_sb, ukT.rearrange("(h p) n -> p h n", p=P)).then_inc(S["uw_ld"], 16)
            sp.dma_start(wdq_sb[:, :, :], wdq.rearrange("(k p) n -> p k n", p=P)).then_inc(S["qw_ld"], 16)
            sp.dma_start(projw[:, 3072:6144], qr).then_inc(S["qw_ld"], 16)
            sp.dma_start(uvT_sb, uvT.rearrange("(h p) n -> p h n", p=P)).then_inc(S["vow_ld"], 16)
            sp.dma_start(wo_sb, wo.rearrange("(h p) n -> p h n", p=P)).then_inc(S["vow_ld"], 16)

            def pieces(c):
                for m, w in enumerate((gate, val, outw)):
                    sp.dma_start(stage[:, m, :], w[bass.ds(c, 1)].rearrange("o p n -> (o p) n")).then_inc(S["st_ld"], 16)

            sp.wait_ge(S["uqk_ps"], NG)
            pieces(0)
            with sp.Fori(1, WCH) as i:
                sp.wait_ge(S["sums_done"], NM * i)
                pieces(i)
            sp.wait_ge(S["sums_done"], NM * WCH)
            pieces(0)
            with sp.Fori(WCH + 1, T - 1) as i:
                sp.wait_ge(S["tern_done"], NM * (i - WCH))
                pieces(i - WCH)
            sp.wait_ge(S["tern_done"], NM * (T - 1 - WCH))
            pieces(WCH - 1)
            sp.wait_ge(S["ql_done"], T * NG)
            sp.wait_ge(S["qr_done"], T * NG)
            sp.dma_start(ob_sb, out_b.partition_broadcast(P)).then_inc(S["bias_ld"], 16)
            sp.wait_ge(S["brow_zero"], 1)
            sp.wait_ge(S["bias_step"], 8)
            for r, part in enumerate((0, 1, 2, 0, 1, 0)):
                for m in range(2):
                    sp.dma_start(brow[r:r + 1, m, :], bsplit[:, part, m, :]).then_inc(S["brow_ld"], 16)

        @block.tensor
        def _(pe):
            pe.wait_ge(S["kvw_ld"], 32)
            for b in range(BATCH):
                pe.wait_ge(S[f"ctx_ld{b}"], 16)
                wait(pe, S["kv_ev"], b)
                for k in range(KD):
                    mm = nc.tensor.matmul(ps_s[0][:, :], wkvc_sb[:, k, :], ctx_sb[:, b, k, :],
                                          start=(k == 0), stop=(k == KD - 1))
                mm.then_inc(S["kv_ps"], 1)
                pe.wait_ge(S["onehot_ready"], 4 * (b + 1))
                for r in range(4):
                    for q in range(4):
                        mm = nc.tensor.matmul(ps_ol[:, 2 * (4 * b + r):2 * (4 * b + r) + 2], onehot[:, q, r * P:(r + 1) * P],
                                              val_c[:, 4 * b + q, :], start=(q == 0), stop=(q == 3))
                mm.then_inc(S["perm_ps"], 1)
                pe.wait_ge(S["kv_ev"], b + 1)
                wait(pe, S["kr_mul"], 2 * b)
                nc.tensor.matmul(ps_s[1][:, :], kr_sb[:, 0, :], kv_cT[:, b * LK:(b + 1) * LK], start=True, stop=True)
                nc.tensor.matmul(ps_pt[:, :], kr_sb[:, 1, :], kv_cT[:, b * LK:(b + 1) * LK],
                                 start=True, stop=True).then_inc(S["kr_ps"], 1)
            pe.wait_ge(S["pool_const"], 6)
            pe.wait_ge(S["seg_ready"], 1)
            pe.wait_ge(S["idx_ready"], 1)
            for n in range(2):
                mm = nc.tensor.matmul(ps_ol[:, 32 + n * T:32 + (n + 1) * T], sel[:, n, :], seg_s[:, :], start=True, stop=True)
            mm.then_inc(S["edge_ps"], 1)
            pe.wait_ge(S["uw_ld"], 32)
            for g in range(NG):
                wait(pe, S["uqk_ev"], 2 * g)
                half = 64 * (g // 2)
                for j in range(GH):
                    h = g * GH + j
                    nc.tensor.matmul(ps_qa[:, j * P:(j + 1) * P], uqT_sb[:, h, 0:P], ukT_sb[:, h, :],
                                     start=True, stop=True)
                    mm = nc.tensor.matmul(ps_qb[half:half + 64, j * P:(j + 1) * P], uqT_sb[:, h, P:QC], ukT_sb[:, h, :],
                                          start=True, stop=True)
                mm.then_inc(S["uqk_ps"], 1)
            pe.wait_ge(S["vow_ld"], 32)
            pe.wait_ge(S["uqk_ev"], 2 * NG)
            for h in range(H):
                wait(pe, S["vo_ev"], h - 1)
                nc.tensor.matmul((ps_qa if h % 2 == 0 else ps_qb)[:, :], uvT_sb[:, h, :], wo_sb[:, h, :],
                                 start=True, stop=True).then_inc(S["vo_ps"], 1)

            def phase1(W):
                NU, HU, KW = NG * W, GH // W, W * P
                kwin, krz, kvwin, ol = key_windows(W)
                mask = mask4[:, 0:KW]

                def turn_x(i):
                    wait(pe, S["kv_ready"], i)
                    pe.wait_ge(S["xn_ready"], i + 1)
                    for k in range(KD):
                        mm = nc.tensor.transpose(ps_prep[:, k * P:(k + 1) * P], xn[:, k * P:(k + 1) * P], identf[:, :])
                    mm.then_inc(S["xt_done"], 1)

                def latent_q(i):
                    pe.wait_ge(S["xnT_ready"], i + 1)
                    pe.wait_ge(S["cs_ld"], (i + 1) * 16)
                    for j in range(2):
                        for k in range(KD):
                            nc.tensor.matmul(ps_prep[:, j * P:(j + 1) * P], wdq_sb[:, k, j * P:(j + 1) * P], xnT[:, k, :],
                                             start=(k == 0), stop=(k == KD - 1))
                    nc.tensor.transpose(ps_prep[:, 2 * P:3 * P], cs_sb[:, 0:P], identf[:, :])
                    nc.tensor.transpose(ps_prep[:, 3 * P:4 * P], cs_sb[:, P:2 * P], identf[:, :]).then_inc(S["qc_done"], 1)

                def turn_keys(i):
                    pe.wait_ge(S["qc_ready"], i + 1)
                    for w in range(W):
                        mm = nc.tensor.transpose(ps_prep[:, w * P:(w + 1) * P], kwin[:, w * P:(w + 1) * P], identf[:, :])
                    mm.then_inc(S["kt_done"], 1)

                def project(i, g):
                    G = i * NG + g
                    pe.wait_ge(S["qc_ready"], i + 1)
                    wait(pe, S["ql_ready"], G)
                    for j in range(GH):
                        h = g * GH + j
                        o = ps_qa[:, j * P:(j + 1) * P]
                        nc.tensor.matmul(o, uqk1[:, h, :], qcs[:, 0, :], start=True, stop=False)
                        mm = nc.tensor.matmul(o, uqk2[:, h % 8, :], qcs[:, 1 + h // 8, :], start=False, stop=True)
                    mm.then_inc(S["ql_done"], 1)
                    wait(pe, S["rope_ab"], G)
                    for j in range(GH // 2):
                        c = (g * GH // 2 + j) * P
                        for n, w1 in enumerate((qrA, qrB)):
                            o = ps_qb[:, (2 * n + j) * P:(2 * n + j + 1) * P]
                            nc.tensor.matmul(o, w1[:, c:c + P], qcs[:, 0, :], start=True, stop=False)
                            mm = nc.tensor.matmul(o, qr2[:, c:c + P], qcs[:, 1 + n, :], start=False, stop=True)
                    mm.then_inc(S["qr_done"], 1)

                def scores(i, u):
                    U, g, s = i * NU + u, u // W, u % W
                    G = i * NG + g
                    wait(pe, S["sub_done"], U - 1)
                    if s == 0:
                        pe.wait_ge(S["ql_ready"], G + 1)
                        pe.wait_ge(S["qr_ready"], G + 1)
                    if u == 0:
                        pe.wait_ge(S["win_ready"], i + 1)
                    bk = ps_s[u % 2]
                    nc.tensor.matmul(bk[:, :], identb[:, :], mask[:, :].unsqueeze(1).to_broadcast([P, HU, KW]),
                                     start=True, stop=False)
                    for j in range(HU):
                        hh = s * HU + j
                        o = bk[:, j * KW:(j + 1) * KW]
                        nc.tensor.matmul(o, ql[g % 2][:, hh, :], kwin[:, :], start=False, stop=False)
                        mm = nc.tensor.matmul(o, qrt[g % 2][:, hh // 2, :], krz[:, hh % 2, :], start=False, stop=(j == HU - 1))
                    mm.then_inc(S["sc_done"], 1)

                def turn_probs(U, r):
                    pe.wait_ge(S["p_ready"], U + 1)
                    wait(pe, S["pt_ready"], U)
                    for k in range(4):
                        mm = nc.tensor.transpose(ps_pt[:, k * P:(k + 1) * P], pr[r][:, k * P:(k + 1) * P], identf[:, :])
                    mm.then_inc(S["pt_done"], 1)

                def mix(U, i):
                    pe.wait_ge(S["pt_ready"], U + 1)
                    pe.wait_ge(S["kv_ready"], i + 1)
                    wait(pe, S["ol_ready"], U)
                    for w in range(W):
                        mm = nc.tensor.matmul(ps_ol[:, 0:HU * P], kvwin[:, w, :],
                                              pt_sb[:, :].rearrange("p (j w n) -> p j w n", j=HU, w=W)[:, :, w, :],
                                              start=(w == 0), stop=(w == W - 1))
                    mm.then_inc(S["pv_done"], 1)

                def out_proj(U, i, u):
                    pe.wait_ge(S["ol_ready"], U + 1)
                    if u == 0:
                        wait(pe, S["out_added"], i)
                    for j in range(HU):
                        h = u * HU + j
                        mm = nc.tensor.matmul(ps_out[:, :], ol[u % 2][:, j, :], vo[:, h, :],
                                              start=(h == 0), stop=(h == H - 1))
                    mm.then_inc(S["op_done"], 1)

                def tile(i, first=False, last=False):
                    for u in range(NU):
                        U, g = i * NU + u, u // W
                        scores(i, u)
                        if not (first and u == 0):
                            turn_probs(U - 1, (u - 1) % 2)
                        if u == 0:
                            turn_keys(i)
                        if u % W == 0:
                            if g < NG - 1:
                                project(i, g + 1)
                            elif not last:
                                project(i + 1, 0)
                            if g == 1 and not last:
                                turn_x(i + 1)
                            if g == 2 and not last:
                                latent_q(i + 1)
                        if not (first and u == 0):
                            mix(U - 1, i if u else i - 1)
                        if not (first and u <= 1):
                            out_proj(U - 2, i if u > 1 else i - 1, (u - 2) % NU)

                pe.wait_ge(S["qw_ld"], 32)
                pe.wait_ge(S["uqk_ev"], 2 * NG)
                turn_x(0)
                latent_q(0)
                pe.wait_ge(S["vo_ev"], H)
                project(0, 0)
                tile(0, first=True)
                with pe.Fori(1, WCH) as i:
                    tile(i)
                pe.wait_ge(S["asum_red"], 1)
                pe.wait_ge(S["qc_ready"], WCH + 1)
                nc.tensor.matmul(ps_prep[:, 0:NM], ones[:, :], asum1[:, :], start=True, stop=True).then_inc(S["gam_ps"], 1)
                pe.wait_ge(S["gam_a"], 1)
                with pe.Fori(WCH, T - 1) as i:
                    tile(i)
                tile(T - 1, last=True)
                U = T * NU
                turn_probs(U - 1, (NU - 1) % 2)
                pe.wait_ge(S["kv_ready"], T)
                turn_xq(0)
                mix(U - 1, T - 1)
                out_proj(U - 2, T - 1, NU - 2)
                out_proj(U - 1, T - 1, NU - 1)
                pe.wait_ge(S["sub_done"], T * NU)
                pe.wait_ge(S["ol_ready"], T * NU)
                pe.wait_ge(S["out_added"], T)

            def turn_xq(t):
                pe.wait_ge(S["xq_ready"], t + 1)
                pe.wait_ge(S["c2"], t + 1)
                wait(pe, S["xqT_ready"], t)
                for k in range(KD):
                    nc.tensor.transpose(ps_xt[:, 0:256].bitcast(BF16)[:, k * P:(k + 1) * P], xq[:, k * P:(k + 1) * P], identb[:, :])
                nc.tensor.transpose(ps_xt[0:6, 256:320].bitcast(BF16), sxs[:, 0:6], identb[:, :]).then_inc(S["xt2"], 1)

            def gate_val(t, c):
                C = t * FC + c
                if c == 0:
                    pe.wait_ge(S["xqT_ready"], t + 1)
                for n, (ps, w, done) in enumerate(((ps_g, tern_g, "gate_ps"), (ps_v, tern_v, "val_ps"))):
                    wait(pe, S[("s_ready", "h_ready")[n]], C - 1)
                    for k in range(KD):
                        nc.tensor.matmul(ps[c % 2][:, :], xqT[:, k, :], w[:, k, c * 512:(c + 1) * 512],
                                         start=(k == 0), stop=False)
                    nc.tensor.matmul(ps[c % 2][:, :], sxT, brow[:, n, c * 512:(c + 1) * 512],
                                     start=False, stop=True).then_inc(S[done], 1)

            def turn_h(t):
                pe.wait_ge(S["hq_ready"], t + 1)
                for j in range(4):
                    wait(pe, S["hqT_ready"], 4 * t + max(j - 1, 0))
                    for k in range(4):
                        mm = nc.tensor.transpose(ps_tr[j % 2][:, 0:256].bitcast(BF16)[:, k * P:(k + 1) * P],
                                                 hq[:, (4 * j + k) * P:(4 * j + k + 1) * P], identb[:, :])
                    mm.then_inc(S["tr_done"], 1)

            def down(t):
                wait(pe, S["y_ready"], t)
                for k in range(FK):
                    if k % 4 == 0:
                        pe.wait_ge(S["hqT_ready"], 4 * t + k // 4 + 1)
                    mm = nc.tensor.matmul(ps_o[:, :], hqT[:, k, :], tern_o[:, k, :], start=(k == 0), stop=(k == FK - 1))
                mm.then_inc(S["o_done"], 1)

            def ffn(t, first=False, last=False):
                gate_val(t, 0)
                gate_val(t, 1)
                if not first:
                    turn_h(t - 1)
                gate_val(t, 2)
                gate_val(t, 3)
                if not last:
                    turn_xq(t + 1)
                if not first:
                    down(t - 1)

            pe.wait_ge(S["flag_ready"], 1)
            spread = pe.value_load(flag_i[0:1, 0:1], min_val=0, max_val=4 * T)
            with pe.If(spread < 1):
                phase1(1)
            with pe.Else():
                phase1(WMAX)

            pe.wait_ge(S["tern_done"], NM * WCH)
            pe.wait_ge(S["brow_ld"], 16 * 12)
            ffn(0, first=True)
            with pe.Fori(1, T - 1) as t:
                ffn(t)
            ffn(T - 1, last=True)
            turn_h(T - 1)
            down(T - 1)

        @block.scalar
        def _(act):
            for g in range(NG):
                act.wait_ge(S["uqk_ps"], g + 1)
                half = 64 * (g // 2)
                nc.scalar.copy(uqk1[:, g * GH:(g + 1) * GH, :], ps_qa[:, :].rearrange("p (h n) -> p h n", h=GH)).then_inc(S["uqk_ev"], 1)
                nc.scalar.copy(uqk2[half:half + 64, (g % 2) * GH:(g % 2 + 1) * GH, :],
                               ps_qb[half:half + 64, :].rearrange("p (h n) -> p h n", h=GH)).then_inc(S["uqk_ev"], 1)
            act.wait_ge(S["kv_ps"], BATCH)
            for h in range(H):
                act.wait_ge(S["vo_ps"], h + 1)
                nc.scalar.copy(vo[:, h, :], (ps_qa if h % 2 == 0 else ps_qb)[:, :]).then_inc(S["vo_ev"], 1)

            def phase1(W):
                NU, HU, KW = NG * W, GH // W, W * P
                kvwin = key_windows(W)[2]

                def xT_out(i):
                    act.wait_ge(S["xt_done"], i + 1)
                    wait(act, S["qc_done"], i)
                    nc.scalar.copy(xnT[:, :, :], ps_prep[:, :].rearrange("p (k n) -> p k n", k=KD)).then_inc(S["xnT_ready"], 1)

                def q_out(i):
                    act.wait_ge(S["qc_done"], i + 1)
                    wait(act, S["ql_done"], i * NG)
                    wait(act, S["qr_done"], i * NG)
                    wait(act, S["rope_ab"], i * NG)
                    nc.scalar.copy(qcs[:, 0, :], ps_prep[:, 0:P])
                    nc.scalar.copy(qcs[0:64, 1, :], ps_prep[0:64, P:2 * P])
                    nc.scalar.copy(qcs[64:P, 2, :], ps_prep[64:P, P:2 * P])
                    nc.scalar.copy(qcs[:, 3:5, :], ps_prep[:, 2 * P:4 * P].rearrange("p (k n) -> p k n", k=2)).then_inc(S["qc_ready"], 1)

                def keys_out(i):
                    act.wait_ge(S["kt_done"], i + 1)
                    wait(act, S["pv_done"], i * NU)
                    nc.scalar.copy(kvwin[:, :, :], ps_prep[:, 0:KW].rearrange("p (w n) -> p w n", w=W)).then_inc(S["kv_ready"], 1)

                def ql_out(i, g):
                    G = i * NG + g
                    act.wait_ge(S["ql_done"], G + 1)
                    wait(act, S["sc_done"], (G - 1) * W)
                    nc.scalar.copy(ql[g % 2][:, :, :], ps_qa[:, :].rearrange("p (h n) -> p h n", h=GH)).then_inc(S["ql_ready"], 1)

                def probsT_out(U):
                    act.wait_ge(S["pt_done"], U + 1)
                    wait(act, S["pv_done"], U)
                    nc.scalar.copy(pt_sb[:, :], ps_pt[:, :]).then_inc(S["pt_ready"], 1)

                def tile(i, first=False, last=False, sums=False):
                    for u in range(NU):
                        U, g = i * NU + u, u // W
                        if not (first and u == 0):
                            probsT_out(U - 1)
                        act.wait_ge(S["sub_done"], U + 1)
                        nc.scalar.activation(pr[u % 2], pr[u % 2], ACT.Exp, scale=SCALE).then_inc(S["exp_done"], 1)
                        if u % W == 0:
                            if g < NG - 1:
                                ql_out(i, g + 1)
                            elif not last:
                                ql_out(i + 1, 0)
                            if g == 1 and not last:
                                xT_out(i + 1)
                            if g == 2 and not last:
                                q_out(i + 1)
                            if g == 3 and sums:
                                act.wait_ge(S["st_ld"], (i + 1) * 16 * NM)
                                for m in range(NM):
                                    nc.scalar.activation(stage[:, m, :], stage[:, m, :], ACT.Abs,
                                                         accum_out=asum[:, m, bass.ds(i, 1)]).then_inc(S["sums_done"], 1)
                        if u == 0:
                            keys_out(i)

                act.wait_ge(S["zeros"], 1)
                xT_out(0)
                q_out(0)
                ql_out(0, 0)
                tile(0, first=True, sums=True)
                with act.Fori(1, WCH) as i:
                    tile(i, sums=True)
                with act.Fori(WCH, T - 1) as i:
                    tile(i)
                tile(T - 1, last=True)
                probsT_out(T * NU - 1)
                act.wait_ge(S["brow_zero"], 1)

            def xqT_out(t):
                act.wait_ge(S["xt2"], t + 1)
                wait(act, S["val_ps"], t * FC)
                nc.scalar.copy(xqT, ps_xt[:, 0:256].bitcast(BF16).rearrange("p (k n) -> p k n", k=KD))
                nc.scalar.copy(sxT[0:6, :], ps_xt[0:6, 256:320].bitcast(BF16)).then_inc(S["xqT_ready"], 1)

            def silu(t, c):
                C = t * FC + c
                act.wait_ge(S["gate_ps"], C + 1)
                if c == 0:
                    act.wait_ge(S["sgv_ready"], t + 1)
                wait(act, S["h_ready"], C - 1)
                nc.scalar.activation(s_sb[c % 2], ps_g[c % 2][:, :], ACT.Silu, scale=sgv[:, 0:1]).then_inc(S["s_ready"], 1)

            def hT_out(t):
                for j in range(4):
                    act.wait_ge(S["tr_done"], 4 * t + j + 1)
                    wait(act, S["o_done"], t)
                    nc.scalar.copy(hqT[:, 4 * j:4 * j + 4, :],
                                   ps_tr[j % 2][:, 0:256].bitcast(BF16).rearrange("p (k n) -> p k n", k=4)).then_inc(S["hqT_ready"], 1)

            def hq_out(t):
                act.wait_ge(S["hr_done"], t + 1)
                wait(act, S["tr_done"], 4 * t)
                nc.scalar.activation(hq, h_sb, ACT.Copy, bias=-MAGIC).then_inc(S["hq_ready"], 1)

            def ffn(t, first=False, last=False):
                silu(t, 0)
                silu(t, 1)
                if not first:
                    hT_out(t - 1)
                silu(t, 2)
                silu(t, 3)
                if not last:
                    xqT_out(t + 1)
                hq_out(t)

            act.wait_ge(S["flag_ready"], 1)
            spread = act.value_load(flag_i[0:1, 0:1], min_val=0, max_val=4 * T)
            with act.If(spread < 1):
                phase1(1)
            with act.Else():
                phase1(WMAX)

            xqT_out(0)
            ffn(0, first=True)
            with act.Fori(1, T - 1) as t:
                ffn(t)
            ffn(T - 1, last=True)
            hT_out(T - 1)

        @block.gpsimd
        def _(pool):
            nc.gpsimd.memset(identf[:, :], 0.0).then_inc(S["pool_const"], 1)
            nc.gpsimd.memset(sel[:, :, :], 0.0).then_inc(S["pool_const"], 1)
            nc.gpsimd.iota(gpos_i, pattern=[[P, T]], base=0, channel_multiplier=1)
            nc.gpsimd.iota(lpos_i, pattern=[[0, BATCH], [P, 4]], base=0, channel_multiplier=1)
            nc.gpsimd.iota(bpos_i, pattern=[[LQ, BATCH], [0, 4]], base=0, channel_multiplier=0)
            nc.gpsimd.iota(lrow_i, pattern=[[1, LQ]], base=0, channel_multiplier=0)
            nc.gpsimd.iota(iota_i, pattern=[[1, LK]], base=0, channel_multiplier=0).then_inc(S["pool_const"], 1)
            pool.wait_ge(S["pool_const"], 3)
            nc.gpsimd.affine_select(out=identf[:, :], in_=identf[:, :], compare_op=ALU.not_equal, fill=1.0, base=0,
                                    pattern=[[-1, P]], channel_multiplier=1).then_inc(S["pool_const"], 1)
            for n in range(2):
                nc.gpsimd.affine_select(out=sel[:, n, :], in_=sel[:, n, :], compare_op=ALU.not_equal, fill=1.0,
                                        base=-n * (P - 1), pattern=[[0, P]], channel_multiplier=1).then_inc(S["pool_const"], 1)
            nc.gpsimd.memset(ones[:, :], 1.0)
            nc.gpsimd.memset(mhalf[:, :], -0.5)
            nc.gpsimd.memset(win[:, :], 0.0)
            nc.gpsimd.memset(qcs[:, :, :], 0.0).then_inc(S["zeros"], 1)

            def gather_x(t):
                nc.gpsimd.indirect_dma_start(x_all[:, t, :], None, x, bass.IndirectOffsetOnAxis(ap=idx[:, t:t + 1].bitcast(U32), axis=0)) \
                    .then_inc(S["x_ld" if t else "x0_ld"], 16)

            def gather_cs(i):
                wait(pool, S["qc_done"], i)
                nc.gpsimd.tensor_copy(idx_cs[:, :], idx_b[:, bass.ds(i, 1)]).then_inc(S["cs_idx"], 1)
                pool.wait_ge(S["cs_idx"], i + 1)
                nc.gpsimd.tensor_tensor(carry_p[:, :], mhalf[:, :], mhalf[:, :], ALU.add)
                nc.gpsimd.indirect_dma_start(cs_sb[:, :], None, cs, bass.IndirectOffsetOnAxis(ap=idx_cs[:, :].bitcast(U32), axis=0)) \
                    .then_inc(S["cs_ld"], 16)

            pool.wait_ge(S["idx_ready"], 1)
            gather_x(0)
            gather_cs(0)
            for t in range(1, T):
                gather_x(t)

            def inv_std(i, veps, done):
                pool.wait_ge(veps, i + 1)
                nc.gpsimd.tensor_tensor(rstd[:, :], ve[:, :], mhalf[:, :], ALU.pow).then_inc(done, 1)

            def phase1(W):
                NU, HU, KW = NG * W, GH // W, W * P
                rc = [r[:, 0:HU] for r in rc4]

                def rope_add(i, g):
                    G = i * NG + g
                    pool.wait_ge(S["rope_ab"], G + 1)
                    wait(pool, S["sc_done"], (G - 1) * W)
                    nc.gpsimd.tensor_tensor(qrt[g % 2][:, :, :], tA[:, :, :], tB[:, :, :], ALU.add).then_inc(S["qr_ready"], 1)

                def tile(i, last=False):
                    for u in range(NU):
                        U, g = i * NU + u, u // W
                        if last and u == NU - 1:
                            inv_std(0, S["veps2"], S["rstd2"])
                            pool.wait_ge(S["ql_done"], T * NG)
                            pool.wait_ge(S["qr_done"], T * NG)
                            pool.wait_ge(S["tern_done"], NM * WCH)
                            nc.gpsimd.memset(projw[:, 0:2048], 0.0)
                            nc.gpsimd.memset(stf[:, 576:640], 0.0).then_inc(S["brow_zero"], 1)
                        pool.wait_ge(S["rec_done"], U + 1)
                        p3 = pr[u % 2].rearrange("p (j n) -> p j n", j=HU)
                        nc.gpsimd.tensor_tensor(p3, p3, rc[u % 2][:, :].unsqueeze(2).to_broadcast([P, HU, KW]),
                                                ALU.mult).then_inc(S["p_ready"], 1)
                        if u % W == 0:
                            if g < NG - 1:
                                rope_add(i, g + 1)
                            elif not last:
                                rope_add(i + 1, 0)
                        if u == 0 and not last:
                            inv_std(i + 1, S["veps_done"], S["rstd_ready"])
                            gather_cs(i + 1)

                inv_std(0, S["veps_done"], S["rstd_ready"])
                rope_add(0, 0)
                tile(0)
                with pool.Fori(1, T - 1) as i:
                    tile(i)
                tile(T - 1, last=True)

            def x_bias(t):
                xt = x_all[:, bass.ds(t, 1), :].rearrange("p o n -> p (o n)")
                nc.gpsimd.tensor_tensor(xt, xt, ob_sb, ALU.add).then_inc(S["xb_ready"], 1)

            def scatter_y(t):
                pool.wait_ge(S["y_ready"], t + 1)
                wait(pool, S["stored"], t * 16)
                nc.gpsimd.tensor_copy(idx_y[:, :], idx[:, bass.ds(t, 1)]).then_inc(S["y_idx"], 1)
                pool.wait_ge(S["y_idx"], t + 1)
                nc.gpsimd.tensor_tensor(carry_p[:, :], mhalf[:, :], mhalf[:, :], ALU.add)
                nc.gpsimd.indirect_dma_start(y, bass.IndirectOffsetOnAxis(ap=idx_y[:, :].bitcast(U32), axis=0),
                                             y_sb, None).then_inc(S["stored"], 16)

            def ffn(t, first=False, last=False):
                if not last:
                    inv_std(t + 1, S["veps2"], S["rstd2"])
                pool.wait_ge(S["xn2"], t + 1)
                x_bias(t)
                if not first:
                    scatter_y(t - 1)

            pool.wait_ge(S["flag_ready"], 1)
            spread = pool.value_load(flag_i[0:1, 0:1], min_val=0, max_val=4 * T)
            with pool.If(spread < 1):
                phase1(1)
            with pool.Else():
                phase1(WMAX)

            pool.wait_ge(S["bias_ld"], 16)
            ffn(0, first=True)
            with pool.Fori(1, T - 1) as t:
                ffn(t)
            ffn(T - 1, last=True)
            scatter_y(T - 1)
            pool.wait_ge(S["stored"], 16 * T)

        @block.vector
        def _(dve):
            dve.wait_ge(S["pool_const"], 4)
            nc.vector.tensor_copy(iota[:, :], iota_i)
            nc.vector.tensor_copy(identb[:, :], identf[:, :])
            nc.vector.tensor_copy(bpos[:, :], bpos_i[:, :])
            nc.vector.tensor_copy(val_c[:, :, 0], gpos_i[:, :])
            dve.wait_ge(S["seg_ld"], 32)
            step = [0]

            def stepped(ins):
                ins.then_inc(S["sort_step"], 1)
                step[0] += 1
                dve.wait_ge(S["sort_step"], step[0])

            stepped(nc.vector.tensor_scalar(val_c[:, :, 1], seg_i[:, :], -1.0, float(LK + LOOKBACK), ALU.max, ALU.min))
            stepped(nc.vector.scalar_tensor_tensor(out=key_c[:, :], in0=val_c[:, :, 1], scalar=float(LQ), in1=lpos_i[:, :],
                                                   op0=ALU.mult, op1=ALU.add))
            stepped(nc.vector.tensor_scalar(key_r, seg_r, -1.0, float(LK + LOOKBACK), ALU.max, ALU.min))
            stepped(nc.vector.scalar_tensor_tensor(out=key_r.rearrange("p (b n) -> p b n", b=BATCH),
                                                   in0=key_r.rearrange("p (b n) -> p b n", b=BATCH), scalar=float(LQ),
                                                   in1=lrow_i.unsqueeze(1).to_broadcast([P, BATCH, LQ]),
                                                   op0=ALU.mult, op1=ALU.add))
            dve.wait_ge(S["const_ld"], 32)
            for b in range(BATCH):
                kb = slice(b * LK, (b + 1) * LK)
                for q in range(4):
                    t = 4 * b + q
                    stepped(nc.vector.tensor_scalar(sort_junk, key_r[:, b * LQ:(b + 1) * LQ], key_c[:, t:t + 1], None,
                                                    ALU.is_lt, ALU.add, accum_out=rank[:, t:t + 1]))
                wait(dve, S["perm_ps"], b)
                for q in range(4):
                    nc.vector.tensor_scalar(onehot[:, q, :], iota[:, :], rank[:, 4 * b + q:4 * b + q + 1], None,
                                            ALU.is_equal).then_inc(S["onehot_ready"], 1)
                dve.wait_ge(S["kv_ps"], b + 1)
                nc.vector.tensor_copy(kv_cT[:, kb], ps_s[0][:, :]).then_inc(S["kv_ev"], 1)
                dve.wait_ge(S["kr_ps"], b + 1)
                nc.vector.tensor_tensor(kropeT[:, kb], ps_s[1][:, :], cosn_sb, ALU.mult).then_inc(S["kr_mul"], 1)
                wait(dve, S["kr_ready"], b)
                nc.vector.tensor_tensor(pt_sb[:, :], ps_pt[:, :], sinn_sb, ALU.mult).then_inc(S["kr_mul"], 1)
                dve.wait_ge(S["kr_mul"], 2 * b + 2)
                nc.vector.tensor_tensor(kropeT[:, kb], kropeT[:, kb], pt_sb[:, :], ALU.add).then_inc(S["kr_ready"], 1)
            dve.wait_ge(S["kr_ready"], BATCH)
            dve.wait_ge(S["perm_ps"], BATCH)
            perm = ps_ol[:, 0:2 * T].rearrange("p (t n) -> p t n", n=2)
            nc.vector.tensor_copy(seg_s[:, :], perm[:, :, 1]).then_inc(S["seg_ready"], 1)
            nc.vector.tensor_copy(idx[:, :], perm[:, :, 0])
            nc.vector.tensor_tensor(idx_b[:, :], perm[:, :, 0], bpos[:, :], ALU.subtract).then_inc(S["idx_ready"], 1)
            dve.wait_ge(S["edge_ps"], 1)
            least, most = ps_ol[:, 2 * T:3 * T], ps_ol[:, 3 * T:4 * T]
            stepped(nc.vector.tensor_scalar(base[:, :], least, -float(LOOKBACK), 0.0, ALU.add, ALU.max))
            stepped(nc.vector.tensor_scalar(base[:, :], base[:, :], float(LK - P), None, ALU.min))
            nc.vector.tensor_scalar(bad[:, 0, :], least, 0.0, None, ALU.is_lt)
            nc.vector.tensor_scalar(bad[:, 1, :], most, float(LK + LOOKBACK - 1), None, ALU.is_gt)
            stepped(nc.vector.tensor_scalar(bad[:, 3, :], most, float(LK - 1), None, ALU.min))
            stepped(nc.vector.tensor_tensor(bad[:, 3, :], bad[:, 3, :], base[:, :], ALU.subtract))
            stepped(nc.vector.tensor_scalar(bad[:, 2, :], bad[:, 3, :], float(P - 1), None, ALU.is_gt))
            stepped(nc.vector.tensor_reduce(flag[:, :], bad[:, 0:3, :], AX.XY, ALU.add))
            nc.vector.tensor_tensor(off_i[:, :], base[:, :], bpos[:, :], ALU.add)
            stepped(nc.vector.tensor_tensor(seg_hi[1][:, :], seg_s[:, :], base[:, :], ALU.subtract))
            nc.vector.tensor_scalar(seg_lo[1][:, :], seg_hi[1][:, :], -float(LOOKBACK), None, ALU.add)
            nc.vector.tensor_scalar(seg_lo[WMAX][:, :], seg_s[:, :], -float(LOOKBACK), None, ALU.add)
            stepped(nc.vector.tensor_copy(flag_i[:, :], flag[:, :]))
            nc.vector.memset(carry[:, :], 0.0).then_inc(S["flag_ready"], 1)

            def stats(i, bn, aggr, veps):
                nc.vector.bn_stats(st6[:, :], x_all[:, bass.ds(i, 1), :].rearrange("p o n -> p (o n)")).then_inc(bn, 1)
                dve.wait_ge(bn, i + 1)
                nc.vector.memset(carry[:, :], 0.0)
                nc.vector.bn_aggr(mv[:, :], st6[:, :]).then_inc(aggr, 1)
                dve.wait_ge(aggr, i + 1)
                nc.vector.tensor_scalar(ve[:, :], mv[:, 1:2], EPS, None, ALU.add).then_inc(veps, 1)

            def norm(i, rs, done):
                dve.wait_ge(rs, i + 1)
                nc.vector.tensor_scalar(xn[:, :], x_all[:, bass.ds(i, 1), :].rearrange("p o n -> p (o n)"),
                                        mv[:, 0:1], rstd[:, :], ALU.subtract, ALU.mult).then_inc(done, 1)

            def phase1(W):
                NU, HU, KW = NG * W, GH // W, W * P
                kwin, krz, _, ol = key_windows(W)
                mask, maskt = mask4[:, 0:KW], maskt4[:, 0:KW]
                mx, sm, rc = ([r[:, 0:HU] for r in rs] for rs in (mx4, sm4, rc4))

                def windows(i):
                    wait(dve, S["sc_done"], i * NU)
                    wait(dve, S["kt_done"], i)
                    if W == 1:
                        off = dve.value_load(off_i[0:1, bass.ds(i, 1)], min_val=0, max_val=TOK - P)
                    else:
                        off = (i // 4) * LK
                    nc.vector.tensor_copy(kwin[:, :], kv_cT[:, bass.ds(off, KW)]).then_inc(S["win_copied"], 1)
                    nc.vector.tensor_copy(krz[0:64, 0, :], kropeT[0:64, bass.ds(off, KW)]).then_inc(S["win_copied"], 1)
                    nc.vector.tensor_copy(krz[64:P, 1, :], kropeT[64:P, bass.ds(off, KW)]).then_inc(S["win_copied"], 1)
                    nc.vector.tensor_scalar(mask[:, :], iota[:, 0:KW], seg_hi[W][:, bass.ds(i, 1)], NEG, ALU.is_gt, ALU.mult).then_inc(S["mask_parts"], 1)
                    nc.vector.tensor_scalar(maskt[:, :], iota[:, 0:KW], seg_lo[W][:, bass.ds(i, 1)], NEG, ALU.is_lt, ALU.mult).then_inc(S["mask_parts"], 1)
                    dve.wait_ge(S["mask_parts"], 2 * i + 2)
                    dve.wait_ge(S["win_copied"], 3 * i + 3)
                    nc.vector.tensor_tensor(mask[:, :], mask[:, :], maskt[:, :], ALU.add).then_inc(S["win_ready"], 1)

                def rope_mul(i, g):
                    G = i * NG + g
                    n = GH // 2
                    dve.wait_ge(S["qr_done"], G + 1)
                    dve.wait_ge(S["qc_ready"], i + 1)
                    wait(dve, S["qr_ready"], G)
                    nc.vector.tensor_tensor(tA[:, :, :], ps_qb[:, 0:n * P].rearrange("p (j n) -> p j n", j=n),
                                            qcs[:, 3, :].unsqueeze(1).to_broadcast([P, n, P]), ALU.mult)
                    nc.vector.tensor_tensor(tB[:, :, :], ps_qb[:, n * P:2 * n * P].rearrange("p (j n) -> p j n", j=n),
                                            qcs[:, 4, :].unsqueeze(1).to_broadcast([P, n, P]), ALU.mult).then_inc(S["rope_ab"], 1)

                def latent_out(U, r):
                    dve.wait_ge(S["pv_done"], U + 1)
                    wait(dve, S["op_done"], U - 1)
                    nc.vector.tensor_copy(ol[r][:, :, :], ps_ol[:, 0:HU * P].rearrange("p (j n) -> p j n", j=HU)).then_inc(S["ol_ready"], 1)

                def add_out(i):
                    dve.wait_ge(S["op_done"], (i + 1) * NU)
                    xt = x_all[:, bass.ds(i, 1), :].rearrange("p o n -> p (o n)")
                    nc.vector.tensor_tensor(xt, ps_out[:, :], xt, ALU.add).then_inc(S["out_added"], 1)

                def ternary(i, m):
                    c = i - WCH
                    if m == 0:
                        dve.wait_ge(S["st_ld"], (i + 1) * 16 * NM)
                    nc.vector.tensor_scalar(tmpb[:, :], stage[:, m, :], nthr[:, m:m + 1], None, ALU.is_lt).then_inc(S["tern_lt"], 1)
                    dve.wait_ge(S["tern_lt"], c * NM + m + 1)
                    nc.vector.scalar_tensor_tensor(out=tern[:, m, bass.ds(c * WC, WC)], in0=stage[:, m, :], scalar=thr[:, m:m + 1],
                                                   in1=tmpb[:, :], op0=ALU.is_gt, op1=ALU.subtract).then_inc(S["tern_done"], 1)
                    dve.wait_ge(S["tern_done"], c * NM + m + 1)

                def tile(i, first=False, last=False, terns=False):
                    for u in range(NU):
                        U, g = i * NU + u, u // W
                        sc3 = ps_s[u % 2][:, :].rearrange("p (j n) -> p j n", j=HU)
                        p3 = pr[u % 2].rearrange("p (j n) -> p j n", j=HU)
                        dve.wait_ge(S["sc_done"], U + 1)
                        nc.vector.tensor_reduce(mx[u % 2][:, :], sc3, AX.X, ALU.max).then_inc(S["max_done"], 1)
                        dve.wait_ge(S["max_done"], U + 1)
                        wait(dve, S["pt_done"], U - 1)
                        nc.vector.tensor_tensor(p3, sc3, mx[u % 2][:, :].unsqueeze(2).to_broadcast([P, HU, KW]),
                                                ALU.subtract).then_inc(S["sub_done"], 1)
                        dve.wait_ge(S["exp_done"], U + 1)
                        nc.vector.tensor_reduce(sm[u % 2][:, :], p3, AX.X, ALU.add).then_inc(S["sum_done"], 1)
                        dve.wait_ge(S["sum_done"], U + 1)
                        nc.vector.reciprocal(rc[u % 2][:, :], sm[u % 2][:, :]).then_inc(S["rec_done"], 1)
                        if u == NU - 1 and not last:
                            windows(i + 1)
                        if u % W == 0:
                            if g < NG - 1:
                                rope_mul(i, g + 1)
                            elif not last:
                                rope_mul(i + 1, 0)
                        if not (first and u == 0):
                            latent_out(U - 1, (u - 1) % 2)
                        if u == 1 and not first:
                            add_out(i - 1)
                        if u == 0 and first:
                            dve.wait_ge(S["x_ld"], 16 * (T - 1))
                        if u == 0 and not last:
                            wait(dve, S["xt_done"], i + 1)
                            stats(i + 1, S["bn_done"], S["aggr_done"], S["veps_done"])
                            norm(i + 1, S["rstd_ready"], S["xn_ready"])
                        if u % W == 0 and g < NM and terns:
                            ternary(i, g)
                        if last and u == NU - 2:
                            dve.wait_ge(S["qr_ready"], T * NG)
                            quant_x(0)

                dve.wait_ge(S["x0_ld"], 16)
                stats(0, S["bn_done"], S["aggr_done"], S["veps_done"])
                norm(0, S["rstd_ready"], S["xn_ready"])
                rope_mul(0, 0)
                dve.wait_ge(S["zeros"], 1)
                windows(0)
                tile(0, first=True)
                with dve.Fori(1, WCH) as i:
                    tile(i)
                dve.wait_ge(S["sums_done"], NM * WCH)
                nc.vector.tensor_reduce(asum1[:, :], asum[:, :, :], AX.X, ALU.add).then_inc(S["asum_red"], 1)
                dve.wait_ge(S["gam_ps"], 1)
                nc.vector.tensor_scalar(gam[:, :], ps_prep[:, 0:NM], 1.0 / (DM * HID), 1e-5, ALU.mult, ALU.max).then_inc(S["gam_a"], 1)
                dve.wait_ge(S["gam_a"], 1)
                nc.vector.tensor_scalar(thr[:, :], gam[:, :], 0.5, None, ALU.mult).then_inc(S["gam_b"], 1)
                nc.vector.tensor_scalar(nthr[:, :], gam[:, :], -0.5, None, ALU.mult).then_inc(S["gam_b"], 1)
                dve.wait_ge(S["gam_b"], 2)
                stepb = [0]

                def stepped_b(ins):
                    ins.then_inc(S["bias_step"], 1)
                    stepb[0] += 1
                    dve.wait_ge(S["bias_step"], stepb[0])

                dve.wait_ge(S["b_ld"], 32)
                stepped_b(nc.vector.reciprocal(rgam[:, :], gam[:, 0:2]))
                for m in range(2):
                    stepped_b(nc.vector.tensor_scalar(b_sb[:, m, :], b_sb[:, m, :], rgam[:, m:m + 1], None, ALU.mult))
                stepped_b(nc.vector.tensor_copy(bsplit[:, 0, :, :], b_sb[:, :, :]))
                stepped_b(nc.vector.tensor_tensor(brest[:, :, :], b_sb[:, :, :], bsplit[:, 0, :, :], ALU.subtract))
                stepped_b(nc.vector.tensor_copy(bsplit[:, 1, :, :], brest[:, :, :]))
                stepped_b(nc.vector.tensor_tensor(b_sb[:, :, :], brest[:, :, :], bsplit[:, 1, :, :], ALU.subtract))
                stepped_b(nc.vector.tensor_copy(bsplit[:, 2, :, :], b_sb[:, :, :]))
                dve.wait_ge(S["vo_ps"], H)
                with dve.Fori(WCH, T - 1) as i:
                    tile(i, terns=True)
                tile(T - 1, last=True, terns=True)
                latent_out(T * NU - 1, (NU - 1) % 2)
                add_out(T - 1)

            def quant_x(t):
                stats(t, S["bn2"], S["aggr2"], S["veps2"])
                norm(t, S["rstd2"], S["xn2"])
                dve.wait_ge(S["xn2"], t + 1)
                nc.vector.tensor_reduce(gx[:, :], xn[:, :], AX.X, ALU.max, apply_absolute_value=True).then_inc(S["gx2"], 1)
                dve.wait_ge(S["gx2"], t + 1)
                nc.vector.tensor_scalar(gxc[:, :], gx[:, :], 1e-5, None, ALU.max).then_inc(S["gxc2"], 1)
                dve.wait_ge(S["gxc2"], t + 1)
                nc.vector.reciprocal(rx[:, :], gxc[:, :]).then_inc(S["rx2"], 1)
                nc.vector.tensor_scalar(dx[:, :], gxc[:, :], 1.0 / 127.0, None, ALU.mult).then_inc(S["dx2"], 1)
                dve.wait_ge(S["rx2"], t + 1)
                nc.vector.tensor_scalar(sx[:, :], rx[:, :], 127.0, None, ALU.mult).then_inc(S["sx2"], 1)
                dve.wait_ge(S["sx2"], t + 1)
                nc.vector.tensor_scalar(xn[:, :], xn[:, :], sx[:, :], MAGIC, ALU.mult, ALU.add).then_inc(S["xr2"], 1)
                dve.wait_ge(S["xr2"], t + 1)
                wait(dve, S["xt2"], t)
                nc.vector.tensor_scalar(xq, xn[:, :], -MAGIC, None, ALU.add).then_inc(S["xq_ready"], 1)
                nc.vector.tensor_copy(sxs[:, 0:3], sx.to_broadcast([P, 3])).then_inc(S["c0"], 1)
                dve.wait_ge(S["c0"], t + 1)
                nc.vector.tensor_tensor(sxr, sx, sxs[:, 0:1], ALU.subtract).then_inc(S["c1"], 1)
                dve.wait_ge(S["c1"], 2 * t + 1)
                nc.vector.tensor_copy(sxs[:, 3:5], sxr.to_broadcast([P, 2])).then_inc(S["c1"], 1)
                dve.wait_ge(S["c1"], 2 * t + 2)
                nc.vector.tensor_tensor(sxs[:, 5:6], sxr, sxs[:, 3:4], ALU.subtract).then_inc(S["c2"], 1)

            def scale_x(t):
                dve.wait_ge(S["dx2"], t + 1)
                nc.vector.tensor_scalar(sgv[:, :], gam[:, 0:2], dx[:, :], None, ALU.mult).then_inc(S["sgv_ready"], 1)
                dve.wait_ge(S["sgv_ready"], t + 1)

            def max_h(t, c):
                dve.wait_ge(S["h_ready"], t * FC + c + 1)
                nc.vector.tensor_reduce(mh4[:, c:c + 1], h_sb[:, c * 512:(c + 1) * 512], AX.X, ALU.max,
                                        apply_absolute_value=True).then_inc(S["mh_part"], 1)

            def chunk(t, c):
                C = t * FC + c
                dve.wait_ge(S["s_ready"], C + 1)
                dve.wait_ge(S["val_ps"], C + 1)
                wait(dve, S["hq_ready"], t)
                nc.vector.scalar_tensor_tensor(out=h_sb[:, c * 512:(c + 1) * 512], in0=ps_v[c % 2][:, :], scalar=sgv[:, 1:2],
                                               in1=s_sb[c % 2], op0=ALU.mult, op1=ALU.mult).then_inc(S["h_ready"], 1)
                if c:
                    max_h(t, c - 1)

            def quant_h(t):
                dve.wait_ge(S["mh_part"], (t + 1) * FC)
                nc.vector.tensor_reduce(mh[:, :], mh4[:, :], AX.X, ALU.max).then_inc(S["mh_done"], 1)
                dve.wait_ge(S["mh_done"], t + 1)
                nc.vector.tensor_scalar(gh[:, :], mh[:, :], 1e-5, None, ALU.max).then_inc(S["gh_done"], 1)
                dve.wait_ge(S["gh_done"], t + 1)
                nc.vector.reciprocal(rh[:, :], gh[:, :]).then_inc(S["rh_done"], 1)
                dve.wait_ge(S["rh_done"], t + 1)
                nc.vector.tensor_scalar(sh[:, :], rh[:, :], 127.0, None, ALU.mult).then_inc(S["sh_done"], 1)
                dve.wait_ge(S["sh_done"], t + 1)
                nc.vector.tensor_scalar(h_sb, h_sb, sh[:, :], MAGIC, ALU.mult, ALU.add).then_inc(S["hr_done"], 1)

            def finish(t):
                dve.wait_ge(S["o_done"], t + 1)
                dve.wait_ge(S["xb_ready"], t + 1)
                dve.wait_ge(S["so_ready"], t + 1)
                xt = x_all[:, bass.ds(t, 1), :].rearrange("p o n -> p (o n)")
                wait(dve, S["stored"], t * 16)
                nc.vector.scalar_tensor_tensor(out=y_sb, in0=ps_o[:, :], scalar=so[:, :], in1=xt,
                                               op0=ALU.mult, op1=ALU.add).then_inc(S["y_ready"], 1)

            def scale_o(t):
                wait(dve, S["y_ready"], t)
                nc.vector.tensor_scalar(so[:, :], gh[:, :], 1.0 / 127.0, gam[:, 2:3], ALU.mult, ALU.mult).then_inc(S["so_ready"], 1)

            def ffn(t, first=False, last=False):
                chunk(t, 0)
                chunk(t, 1)
                if not last:
                    quant_x(t + 1)
                chunk(t, 2)
                chunk(t, 3)
                max_h(t, 3)
                quant_h(t)
                if not last:
                    scale_x(t + 1)
                if not first:
                    finish(t - 1)
                scale_o(t)

            dve.wait_ge(S["flag_ready"], 1)
            spread = dve.value_load(flag_i[0:1, 0:1], min_val=0, max_val=4 * T)
            with dve.If(spread < 1):
                phase1(1)
            with dve.Else():
                phase1(WMAX)

            scale_x(0)
            ffn(0, first=True)
            with dve.Fori(1, T - 1) as t:
                ffn(t)
            ffn(T - 1, last=True)
            finish(T - 1)


def kernel(x, ctx_2048, itok_BxS_0_1023, L0_xattn_W_kvc, L0_xattn_W_dq, L0_xattn_W_uq, L0_xattn_W_qr,
           L0_xattn_W_uk, L0_xattn_W_kr, L0_xattn_W_uv, L0_xattn_W_o, L0_ffn_gate_w, L0_ffn_gate_b,
           L0_ffn_val_w, L0_ffn_val_b, L0_ffn_out_w, L0_ffn_out_b):
    import concourse.bacc as bacc
    from concourse.bass_utils import run_bass_kernel_spmd

    a = np.asarray
    half = ROPE // 2
    inv = (np.float32(1.0) / np.float32(10000.0) ** (np.arange(half, dtype=np.float32) / np.float32(half))).astype(np.float32)
    ang = np.arange(LQ, dtype=np.float32)[:, None] * inv
    cos, sin = np.cos(ang).astype(np.float32), np.sin(ang).astype(np.float32)
    cs = np.concatenate([cos] * 4 + [-sin, sin] * 2, axis=1)
    cosn = np.concatenate([cos.T] * 4, axis=0)
    sinn = np.concatenate([-sin.T, sin.T] * 2, axis=0)

    def swap(w):
        return np.concatenate([w.reshape(w.shape[0], -1, 2, half)[:, :, 1:2], w.reshape(w.shape[0], -1, 2, half)[:, :, 0:1]],
                              axis=2).reshape(w.shape)

    dq, wqr, wkr = a(L0_xattn_W_dq), a(L0_xattn_W_qr), a(L0_xattn_W_kr)
    arrays = {
        "x": a(x).reshape(TOK, DM),
        "ctxT": a(ctx_2048).transpose(0, 2, 1),
        "itok": a(itok_BxS_0_1023).reshape(TOK),
        "itokT": a(itok_BxS_0_1023).reshape(T, P).T,
        "cs": cs, "cosn": cosn, "sinn": sinn,
        "wkvc": a(L0_xattn_W_kvc),
        "wdq": np.concatenate([dq, dq[:, P:QC]], axis=1),
        "uqT": a(L0_xattn_W_uq).T,
        "ukT": a(L0_xattn_W_uk).T,
        "uvT": a(L0_xattn_W_uv).T,
        "wo": a(L0_xattn_W_o),
        "qr": np.concatenate([wqr[0:P], swap(wqr)[0:P], np.concatenate([wqr[P:QC], swap(wqr)[P:QC]], axis=0)], axis=1),
        "kr": np.stack([np.concatenate([wkr, wkr], axis=1), np.concatenate([swap(wkr), swap(wkr)], axis=1)], axis=1),
        "gate": a(L0_ffn_gate_w).T.reshape(KD, P, 2, HID // 2).transpose(0, 2, 1, 3).reshape(WCH, P, WC),
        "val": a(L0_ffn_val_w).T.reshape(KD, P, 2, HID // 2).transpose(0, 2, 1, 3).reshape(WCH, P, WC),
        "outw": a(L0_ffn_out_w).T.reshape(WCH, 2, P, DM).transpose(0, 2, 1, 3).reshape(WCH, P, WC),
        "gate_b": a(L0_ffn_gate_b), "val_b": a(L0_ffn_val_b), "out_b": a(L0_ffn_out_b),
    }
    arrays = {n: np.ascontiguousarray(v) for n, v in arrays.items()}
    nc = bacc.Bacc("TRN2", target_bir_lowering=False, num_devices=1)
    args = [nc.dram_tensor(f"in_{n}", v.shape, mybir.dt.from_np(v.dtype), kind="ExternalInput").ap() for n, v in arrays.items()]
    args.append(nc.dram_tensor("y", (TOK, DM), F32, kind="ExternalOutput").ap())
    build(nc, *args)
    r = run_bass_kernel_spmd(nc, [{f"in_{n}": v for n, v in arrays.items()}], core_ids=[0])
    return r.results[0]["y"].reshape(BATCH, LQ, DM)
```

```python
from contextlib import ExitStack

import numpy as np

import concourse.bass as bass
from concourse import mybir

ALU = mybir.AluOpType
ACT = mybir.ActivationFunctionType
AX = mybir.AxisListType
F32 = mybir.dt.float32
BF16 = mybir.dt.bfloat16
F16 = mybir.dt.float16
I32 = mybir.dt.int32
U32 = mybir.dt.uint32

P = 128
BATCH, LQ, LK, DM = 4, 512, 512, 512
H, HD, ROPE, KVC, QC = 16, 128, 64, 128, 192
HID = 2048
LOOKBACK = 8
NEG = -1e30
EPS = 1e-5
SCALE = float(1.0 / np.sqrt(HD + ROPE).astype(np.float32))
MAGIC = 12582912.0
TOK = BATCH * LQ
T = TOK // P
KD = DM // P
NG = 4
GH = H // NG
FC = 4
FK = HID // P
SCALE_STEPS = 7
NM = 3
WCOL = DM * HID // P
WCH = 8
WC = WCOL // WCH


def wait(eng, sem, value):
    if not (isinstance(value, int) and value <= 0):
        eng.wait_ge(sem, value)


def build(nc, x, ctxT, itok, itokT, cs, cosn, sinn, wkvc, wdq, uqT, ukT, uvT, wo, qr, kr, gate, val, outw,
          gate_b, val_b, out_b, y):
    WMAX = LK // P
    ctx = ExitStack()
    with ctx:
        def sb(name, shape, dt=F32):
            return ctx.enter_context(nc.sbuf_tensor(name, shape, dt))

        def sem(name):
            return ctx.enter_context(nc.semaphore(name))

        bank = [ctx.enter_context(nc.psum_tensor(f"bank{n}", [P, 512], F32)) for n in range(8)]
        ps_s = bank[0:2]
        ps_pt, ps_ol = bank[2:4]
        ps_qa, ps_qb = bank[4:6]
        ps_out, ps_prep = bank[6:8]
        kv_bank = (ps_s[0], ps_qa)
        uqk_banks = ((ps_qa, ps_qb), (ps_s[0], ps_s[1]))
        vo_banks = (ps_s[0], ps_s[1], ps_pt, ps_out)
        ps_g, ps_v, ps_tr = bank[0:2], bank[2:4], bank[4:6]
        ps_o, ps_xt = bank[6:8]

        x_all = sb("x_all", [P, T, DM])
        kv_cT = sb("kv_cT", [P, TOK])
        kropeT = sb("kropeT", [P, TOK])
        identf = sb("identf", [P, P])
        identb = sb("identb", [P, P], BF16)
        identh = sb("identh", [P, P], F16)
        ones = sb("ones", [P, P])
        iota = sb("iota", [P, LK], F16)
        mhalf = sb("mhalf", [P, 1])
        seg_i = sb("seg_i", [P, T], I32)
        xnT = sb("xnT", [P, KD, P])
        early = xnT[:, :, :].rearrange("p k n -> p (k n)")
        gpos_i = early[:, 0:16].bitcast(I32)
        lpos_i = early[:, 16:32].bitcast(I32)
        bpos_i = early[:, 32:48].bitcast(I32)
        bpos = early[:, 48:64]
        key_c = early[:, 64:80]
        rank = early[:, 80:96]
        val_c = early[:, 96:112].bitcast(F16).rearrange("p (t n) -> p t n", n=2)
        bad = early[:, 128:192].rearrange("p (n t) -> p n t", n=4)
        seg_s = sb("seg_s", [P, T])
        idx = sb("idx", [P, T], I32)
        idx_b = sb("idx_b", [P, T], I32)
        idx_cs = sb("idx_cs", [P, 1], I32)
        idx_y = sb("idx_y", [P, 1], I32)
        base = sb("base", [P, T])
        off_i = sb("off_i", [P, T], I32)
        flag = sb("flag", [P, 1])
        flag_i = sb("flag_i", [P, 1], I32)
        seg_hi = {1: sb("seg_hi1", [P, T]), WMAX: seg_s}
        seg_lo = {1: sb("seg_lo1", [P, T]), WMAX: sb("seg_lo4", [P, T])}
        asum = sb("asum", [P, NM, WCH])
        asum1 = sb("asum1", [P, NM])
        gam = sb("gam", [P, NM])

        xf = x_all[:, :, :].rearrange("p t n -> p (t n)")
        seg_r = xf[:, 0:2048].bitcast(I32)
        key_r = xf[:, 2048:4096]
        onehot = xf[:, 4096:6144].bitcast(F16).rearrange("p (b t n) -> p b t n", b=2, t=4)
        sort_junk = xf[:, 6144:6656]
        lrow_i = xf[:, 6656:7168].bitcast(I32)

        tern = sb("tern", [P, NM, WCOL], BF16)
        ternf = tern[:, :, :].rearrange("p m c -> p (m c)").bitcast(F32)
        wo_sb = ternf[:, 0:8192].rearrange("p (h n) -> p h n", h=H)
        ukT_sb = ternf[:, 8192:10240].rearrange("p (h n) -> p h n", h=H)
        uvT_sb = ternf[:, 10240:12288].rearrange("p (h n) -> p h n", h=H)
        tern_g = tern[:, 0, :].rearrange("p (k n) -> p k n", k=KD)
        tern_v = tern[:, 1, :].rearrange("p (k n) -> p k n", k=KD)
        tern_o = tern[:, 2, :].rearrange("p (k n) -> p k n", k=FK)

        stage = sb("stage", [P, NM, WC])
        uqT_sb = stage[:, :, :].rearrange("p m c -> p (m c)").rearrange("p (h n) -> p h n", h=H)

        vof = sb("vo", [P, H * DM])[:, :]
        vo = vof.bitcast(F16).rearrange("p (h s n) -> p h s n", h=H, s=2)
        ctx_sb = vof.rearrange("p (b k n) -> p b k n", b=BATCH, k=KD)
        h_sb = vof[:, 0:2048]
        s_sb = [vof[:, 2048 + 512 * n:2560 + 512 * n] for n in range(2)]
        hq = vof[:, 3072:4096].bitcast(BF16)
        hqT = vof[:, 4096:5120].bitcast(BF16).rearrange("p (k n) -> p k n", k=FK)
        stf = stage[:, :, :].rearrange("p m c -> p (m c)")
        xq = stf[:, 0:256].bitcast(BF16)
        xqT = stf[:, 256:512].bitcast(BF16).rearrange("p (k n) -> p k n", k=KD)
        sxs = stf[:, 512:516].bitcast(BF16)
        sxT = stf[:, 576:640].bitcast(BF16)

        projw = sb("projw", [P, 4608])
        uqk1 = projw[:, 0:2048].bitcast(F16).rearrange("p (s h n) -> p s h n", s=2, h=H)
        uqk2 = projw[:, 2048:3072].bitcast(F16).rearrange("p (s h n) -> p s h n", s=2, h=H // 2)
        qrs = projw[:, 3072:4608].bitcast(F16).rearrange("p (s n) -> p s n", s=2)
        qr_in = sb("qr_in", [P, 1536])
        brow = projw[:, 0:2048].bitcast(BF16).rearrange("p (m n) -> p m n", m=2)
        ob_sb = projw[:, 4096:4608]
        b_sb = sb("b_sb", [P, 2, HID // P])
        brest = sb("brest", [P, 2, HID // P])
        bsplit = sb("bsplit", [P, 3, 2, HID // P], BF16)
        rgam = sb("rgam", [P, NM])
        wdq_sb = sb("wdq_sb", [P, KD, 256])

        xn = sb("xn", [P, DM])
        iota_i = xn[:, :].bitcast(I32)
        qcs = sb("qcs", [P, 3, 2, P], F16)
        csT = sb("csT", [P, 2, P])
        cs_sb = sb("cs_sb", [P, 2 * P])
        win = sb("win", [P, 4 * LK])
        ol_few = sb("ol_few", [P, 2, P])
        sums = sb("sums", [P, 110])
        ssq = sums[:, 0:80].rearrange("p (s n c) -> p s n c", s=2, n=5)
        ssum = sums[:, 80:90].rearrange("p (s n) -> p s n", s=2)
        bound = sums[:, 90:100].rearrange("p (s n) -> p s n", s=2)
        bexp = sums[:, 100:105].bitcast(I32)
        up = sb("up", [P, 5])
        inv = sums[:, 105:110]
        undo = sb("undo", [P, 3])

        def key_windows(W):
            KW, HU = W * P, GH // W
            kwin = win[:, 0:KW]
            krz = win[:, KW:3 * KW].rearrange("p (n k) -> p n k", n=2)
            kvwin = win[:, 3 * KW:4 * KW].bitcast(F16).rearrange("p (s w n) -> p s w n", s=2, w=W)
            wide = win[:, 2 * LK:4 * LK].rearrange("p (r j n) -> p r j n", r=2, j=GH)
            ol = [(wide[:, n, :, :].rearrange("p j n -> p (j n)") if W == 1 else ol_few[:, n, :])
                  .bitcast(F16).rearrange("p (s j n) -> p s j n", s=2, j=GH // W) for n in range(2)]
            return kwin, krz, kvwin, ol

        mask4 = sb("mask", [P, LK], BF16)
        st6 = sb("st6", [P, 6])
        mv = sb("mv", [P, 2])
        carry = sb("carry", [P, 1])
        carry_p = sb("carry_p", [P, 1])
        magic = sb("magic", [P, 2])
        ve = sb("ve", [P, 1])
        rstd = sb("rstd", [P, 1])
        ql = [sb(f"ql{n}", [P, GH, P]) for n in range(2)]
        wkvc_sb = ql[0]
        kr_sb = ql[1]
        qrt = [sb(f"qrt{n}", [P, GH // 2, P]) for n in range(2)]
        tA = sb("tA", [P, GH // 2, P])
        sel = tA
        tB = sb("tB", [P, GH // 2, P])
        pr_all = sb("pr_all", [P, 2, 512])
        pr = [pr_all[:, n, :] for n in range(2)]
        cosn_sb, sinn_sb = pr
        mx4 = [sb(f"mx{n}", [P, GH]) for n in range(2)]
        sm4 = [sb(f"sm{n}", [P, GH]) for n in range(2)]
        rc4 = [sb(f"rc{n}", [P, GH]) for n in range(2)]
        nm4 = [sb(f"nm{n}", [P, GH]) for n in range(2)]
        psplit = sb("psplit", [P, 2, 512], F16)
        pt_sb = sb("pt_sb", [P, 512])
        ptT = pt_sb[:, :].bitcast(F16)
        maskt4 = sb("maskt", [P, LK], BF16)
        y_sb = pt_sb[:, :]
        tAf = tA[:, :, :].rearrange("p j n -> p (j n)")
        gx, gxc, rx, sx, dx, mh, gh, rh, sh, so, sxr = (tAf[:, n:n + 1] for n in range(11))
        sgv, mh4 = tAf[:, 16:18], tAf[:, 20:20 + FC]

        names = """const_ld seg_ld ctx_ld0 ctx_ld1 ctx_ld2 ctx_ld3 kvw_ld uw_ld vow_ld x0_ld x_ld qw_ld cs_ld st_ld bias_ld stored
            pool_const dve_const zeros sort_step onehot_ready perm_ps idx_ready seg_ready edge_ps
            flag_ready cs_idx y_idx kv_ps kv_ev kr_ps kr_mul kr_ready uqk_ps uqk_ev vo_ps vo_ev
            sc_done pt_done pv_done ql_done qr_done op_done xt_done qc_done kt_done
            max_done sub_done sum_done rec_done ol_ready rope_ab out_added win_copied mask_parts
            win_ready bn_done aggr_done veps_done xn_ready exp_done pt_ready ql_ready kv_ready
            xnT_ready qc_ready p_ready qr_ready rstd_ready sums_done w_round tern_done
            asum_red gam_ps gam_ready gam_a
            bn2 aggr2 veps2 rstd2 xn2 gx2 gxc2 rx2 sx2 xr2 xq_ready dx2 sgv_ready xt2 xqT_ready gate_ps val_ps
            b_ld brow_zero brow_ld bias_step c0 c1 c2
            nm_done p_hi p_split kv_hi
            squared squared_too sum_step tot_ps scale_step qr_hi qr_parts uqk_hi vo_hi qc_hi ol_hi
            s_ready h_ready mh_part mh_done gh_done rh_done sh_done hr_done
            hq_ready tr_done hqT_ready o_done so_ready xb_ready y_ready""".split()
        S = {n: sem(n) for n in names}

        block = ctx.enter_context(nc.Block())

        @block.sync
        def _(sp):
            sp.dma_start(seg_i[:, :], itokT).then_inc(S["seg_ld"], 16)
            sp.dma_start(seg_r, itok.partition_broadcast(P)).then_inc(S["seg_ld"], 16)
            sp.dma_start(pr_all[:, 0, :], cosn).then_inc(S["const_ld"], 16)
            sp.dma_start(pr_all[:, 1, :], sinn).then_inc(S["const_ld"], 16)
            sp.dma_start(wkvc_sb[:, :, :], wkvc.rearrange("(k p) n -> p k n", p=P)).then_inc(S["kvw_ld"], 16)
            sp.dma_start(kr_sb[:, 0:2, :], kr).then_inc(S["kvw_ld"], 16)

            def context(b):
                sp.dma_start(ctx_sb[:, b, :, :], ctxT[b].rearrange("(k p) n -> p k n", p=P)).then_inc(S[f"ctx_ld{b}"], 16)

            context(0)
            context(1)
            sp.dma_start(uqT_sb, uqT.rearrange("(h p) n -> p h n", p=P)).then_inc(S["uw_ld"], 16)
            sp.dma_start(ukT_sb, ukT.rearrange("(h p) n -> p h n", p=P)).then_inc(S["uw_ld"], 16)
            context(2)
            sp.dma_start(wdq_sb[:, :, :], wdq.rearrange("(k p) n -> p k n", p=P)).then_inc(S["qw_ld"], 16)
            sp.dma_start(qr_in[:, :], qr).then_inc(S["qw_ld"], 16)
            context(3)
            sp.dma_start(uvT_sb, uvT.rearrange("(h p) n -> p h n", p=P)).then_inc(S["vow_ld"], 16)
            sp.dma_start(wo_sb, wo.rearrange("(h p) n -> p h n", p=P)).then_inc(S["vow_ld"], 16)

            sp.dma_start(b_sb[:, 0, :], gate_b.rearrange("(p n) -> p n", p=P)).then_inc(S["b_ld"], 16)
            sp.dma_start(b_sb[:, 1, :], val_b.rearrange("(p n) -> p n", p=P)).then_inc(S["b_ld"], 16)

            def pieces(c):
                for m, w in enumerate((gate, val, outw)):
                    sp.dma_start(stage[:, m, :], w[bass.ds(c, 1)].rearrange("o p n -> (o p) n")).then_inc(S["st_ld"], 16)

            sp.wait_ge(S["uqk_ps"], NG)
            pieces(0)
            with sp.Fori(1, WCH) as i:
                sp.wait_ge(S["sums_done"], NM * i)
                pieces(i)
            sp.wait_ge(S["sums_done"], NM * WCH)
            pieces(0)
            with sp.Fori(WCH + 1, T - 1) as i:
                sp.wait_ge(S["tern_done"], NM * (i - WCH))
                pieces(i - WCH)
            sp.wait_ge(S["tern_done"], NM * (T - 1 - WCH))
            pieces(WCH - 1)
            sp.wait_ge(S["ql_done"], T * NG)
            sp.wait_ge(S["qr_done"], T * NG)
            sp.dma_start(ob_sb, out_b.partition_broadcast(P)).then_inc(S["bias_ld"], 16)
            sp.wait_ge(S["brow_zero"], 1)
            sp.wait_ge(S["bias_step"], 8)
            for r, part in enumerate((0, 1, 2, 0, 1, 0)):
                for m in range(2):
                    sp.dma_start(brow[r:r + 1, m, :], bsplit[:, part, m, :]).then_inc(S["brow_ld"], 16)

        @block.tensor
        def _(pe):
            def latent_keys(b):
                pe.wait_ge(S[f"ctx_ld{b}"], 16)
                wait(pe, S["kv_ev"], b - 1)
                for k in range(KD):
                    mm = nc.tensor.matmul(kv_bank[b % 2][:, :], wkvc_sb[:, k, :], ctx_sb[:, b, k, :],
                                          start=(k == 0), stop=(k == KD - 1))
                mm.then_inc(S["kv_ps"], 1)

            pe.wait_ge(S["kvw_ld"], 32)
            latent_keys(0)
            for b in range(BATCH):
                if b < BATCH - 1:
                    latent_keys(b + 1)
                pe.wait_ge(S["onehot_ready"], 4 * (b + 1))
                for r in range(4):
                    for q in range(4):
                        mm = nc.tensor.matmul(ps_ol[:, 2 * (4 * b + r):2 * (4 * b + r) + 2], onehot[:, b % 2, q, r * P:(r + 1) * P],
                                              val_c[:, 4 * b + q, :], start=(q == 0), stop=(q == 3))
                mm.then_inc(S["perm_ps"], 1)
                pe.wait_ge(S["kv_ev"], b + 1)
                wait(pe, S["kr_mul"], 2 * b)
                nc.tensor.matmul(ps_s[1][:, :], kr_sb[:, 0, :], kv_cT[:, b * LK:(b + 1) * LK], start=True, stop=True)
                nc.tensor.matmul(ps_pt[:, :], kr_sb[:, 1, :], kv_cT[:, b * LK:(b + 1) * LK],
                                 start=True, stop=True).then_inc(S["kr_ps"], 1)

            def query_product(g):
                wait(pe, S["uqk_ev"], 2 * (g - 1))
                a, b = uqk_banks[g % 2]
                half = 64 * (g // 2)
                for j in range(GH):
                    h = g * GH + j
                    nc.tensor.matmul(a[:, j * P:(j + 1) * P], uqT_sb[:, h, 0:P], ukT_sb[:, h, :],
                                     start=True, stop=True)
                    mm = nc.tensor.matmul(b[half:half + 64, j * P:(j + 1) * P], uqT_sb[:, h, P:QC], ukT_sb[:, h, :],
                                          start=True, stop=True)
                mm.then_inc(S["uqk_ps"], 1)

            def turn_x(i):
                wait(pe, S["kv_ready"], i)
                pe.wait_ge(S["xn_ready"], i + 1)
                for k in range(KD):
                    mm = nc.tensor.transpose(ps_prep[:, k * P:(k + 1) * P], xn[:, k * P:(k + 1) * P], identf[:, :])
                mm.then_inc(S["xt_done"], 1)

            def latent_q(i):
                pe.wait_ge(S["xnT_ready"], i + 1)
                pe.wait_ge(S["cs_ld"], (i + 1) * 16)
                for j in range(2):
                    for k in range(KD):
                        nc.tensor.matmul(ps_prep[:, j * P:(j + 1) * P], wdq_sb[:, k, j * P:(j + 1) * P], xnT[:, k, :],
                                         start=(k == 0), stop=(k == KD - 1))
                nc.tensor.transpose(ps_prep[:, 2 * P:3 * P], cs_sb[:, 0:P], identf[:, :])
                nc.tensor.transpose(ps_prep[:, 3 * P:4 * P], cs_sb[:, P:2 * P], identf[:, :]).then_inc(S["qc_done"], 1)

            def totals(n, columns):
                wait(pe, S["scale_step"], n)
                pe.wait_ge(S["sum_step"], n + 1)
                nc.tensor.matmul(ps_out[:, 0:2 * (columns.stop - columns.start)], ones[:, :], ssum[:, :, columns],
                                 start=True, stop=True).then_inc(S["tot_ps"], 1)

            pe.wait_ge(S["zeros"], 1)
            pe.wait_ge(S["uw_ld"], 32)
            query_product(0)
            totals(0, slice(1, 5))
            pe.wait_ge(S["pool_const"], 6)
            pe.wait_ge(S["seg_ready"], 1)
            pe.wait_ge(S["idx_ready"], 1)
            for n in range(2):
                mm = nc.tensor.matmul(ps_ol[:, 32 + n * T:32 + (n + 1) * T], sel[:, n, :], seg_s[:, :], start=True, stop=True)
            mm.then_inc(S["edge_ps"], 1)
            pe.wait_ge(S["kr_mul"], 2 * BATCH)
            query_product(1)
            query_product(2)
            turn_x(0)
            query_product(3)
            pe.wait_ge(S["qw_ld"], 32)
            latent_q(0)
            totals(1, slice(0, 1))

            def output_products():
                pe.wait_ge(S["vow_ld"], 32)
                pe.wait_ge(S["uqk_ev"], 2 * NG)
                pe.wait_ge(S["scale_step"], SCALE_STEPS + 1)
                for h in range(H):
                    wait(pe, S["vo_ev"], h - 3)
                    nc.tensor.matmul(vo_banks[h % 4][:, :], uvT_sb[:, h, :], wo_sb[:, h, :],
                                     start=True, stop=True).then_inc(S["vo_ps"], 1)

            def phase1(W):
                NU, HU, KW = NG * W, GH // W, W * P
                kwin, krz, kvwin, ol = key_windows(W)
                mask = mask4[:, 0:KW]
                scores_read = S["exp_done" if W == 1 else "sub_done"]

                def turn_keys(i):
                    pe.wait_ge(S["qc_ready"], i + 1)
                    for w in range(W):
                        mm = nc.tensor.transpose(ps_prep[:, w * P:(w + 1) * P], kwin[:, w * P:(w + 1) * P], identf[:, :])
                    mm.then_inc(S["kt_done"], 1)

                def project(i, g):
                    G = i * NG + g
                    pe.wait_ge(S["qc_ready"], i + 1)
                    wait(pe, S["ql_ready"], G)
                    for j in range(GH):
                        h = g * GH + j
                        o = ps_qa[:, j * P:(j + 1) * P]
                        for w, q in ((0, 0), (0, 1), (1, 0)):
                            nc.tensor.matmul(o, uqk1[:, w, h, :], qcs[:, 0, q, :], start=(w + q == 0), stop=False)
                            mm = nc.tensor.matmul(o, uqk2[:, w, h % 8, :], qcs[:, 1 + h // 8, q, :], start=False, stop=(w == 1))
                    mm.then_inc(S["ql_done"], 1)
                    wait(pe, S["rope_ab"], G)
                    for j in range(GH // 2):
                        c = g * GH // 2 + j
                        o = ps_qb[:, j * P:(j + 1) * P]
                        for w, q in ((0, 0), (0, 1), (1, 0)):
                            nc.tensor.matmul(o, qrs[:, w, c * P:(c + 1) * P], qcs[:, 0, q, :], start=(w + q == 0), stop=False)
                            mm = nc.tensor.matmul(o, qrs[:, w, (8 + c % 4) * P:(9 + c % 4) * P], qcs[:, 1 + c // 4, q, :],
                                                  start=False, stop=(w == 1))
                    mm.then_inc(S["qr_done"], 1)

                def scores(i, u):
                    U, g, s = i * NU + u, u // W, u % W
                    G = i * NG + g
                    wait(pe, scores_read, U - 1)
                    if s == 0:
                        pe.wait_ge(S["ql_ready"], G + 1)
                        pe.wait_ge(S["qr_ready"], G + 1)
                    if u == 0:
                        pe.wait_ge(S["win_ready"], i + 1)
                    bk = ps_s[u % 2]
                    nc.tensor.matmul(bk[:, :], identb[:, :], mask[:, :].unsqueeze(1).to_broadcast([P, HU, KW]),
                                     start=True, stop=False)
                    for j in range(HU):
                        hh = s * HU + j
                        o = bk[:, j * KW:(j + 1) * KW]
                        nc.tensor.matmul(o, ql[g % 2][:, hh, :], kwin[:, :], start=False, stop=False)
                        mm = nc.tensor.matmul(o, qrt[g % 2][:, hh // 2, :], krz[:, hh % 2, :], start=False, stop=(j == HU - 1))
                    mm.then_inc(S["sc_done"], 1)

                def turn_probs(U):
                    pe.wait_ge(S["p_split"], U + 1)
                    wait(pe, S["pt_ready"], U)
                    flat = psplit[:, :, :].rearrange("p s n -> p (s n)")
                    for k in range(8):
                        mm = nc.tensor.transpose(ps_pt[:, :].bitcast(F16)[:, k * P:(k + 1) * P], flat[:, k * P:(k + 1) * P], identh[:, :])
                    mm.then_inc(S["pt_done"], 1)

                def mix(U, i):
                    pe.wait_ge(S["pt_ready"], U + 1)
                    pe.wait_ge(S["kv_ready"], i + 1)
                    wait(pe, S["ol_ready"], U)
                    probs = ptT.rearrange("p (s j w n) -> p s j w n", s=2, j=HU, w=W)
                    for w in range(W):
                        for k, q in ((0, 0), (0, 1), (1, 0)):
                            mm = nc.tensor.matmul(ps_ol[:, 0:HU * P], kvwin[:, k, w, :], probs[:, q, :, w, :],
                                                  start=(w + k + q == 0), stop=(w == W - 1 and k == 1))
                    mm.then_inc(S["pv_done"], 1)

                def out_proj(U, i, u):
                    pe.wait_ge(S["ol_ready"], U + 1)
                    if u == 0:
                        wait(pe, S["out_added"], i)
                    for j in range(HU):
                        h = u * HU + j
                        for w, q in ((0, 0), (0, 1), (1, 0)):
                            mm = nc.tensor.matmul(ps_out[:, :], ol[u % 2][:, q, j, :], vo[:, h, w, :],
                                                  start=(h + w + q == 0), stop=(h == H - 1 and w == 1))
                    mm.then_inc(S["op_done"], 1)

                def tile(i, first=False, last=False):
                    for u in range(NU):
                        U, g = i * NU + u, u // W
                        scores(i, u)
                        if not (first and u == 0):
                            turn_probs(U - 1)
                        if u == 0:
                            turn_keys(i)
                        if u % W == 0:
                            if g < NG - 1:
                                project(i, g + 1)
                            elif not last:
                                project(i + 1, 0)
                            if g == 1 and not last:
                                turn_x(i + 1)
                            if g == 2 and not last:
                                latent_q(i + 1)
                        if not (first and u == 0):
                            mix(U - 1, i if u else i - 1)
                        if not (first and u <= 1):
                            out_proj(U - 2, i if u > 1 else i - 1, (u - 2) % NU)

                pe.wait_ge(S["qr_parts"], 1)
                project(0, 0)
                output_products()
                pe.wait_ge(S["vo_ev"], H)
                tile(0, first=True)
                with pe.Fori(1, WCH) as i:
                    tile(i)
                pe.wait_ge(S["asum_red"], 1)
                pe.wait_ge(S["qc_ready"], WCH + 1)
                nc.tensor.matmul(ps_prep[:, 0:NM], ones[:, :], asum1[:, :], start=True, stop=True).then_inc(S["gam_ps"], 1)
                pe.wait_ge(S["gam_a"], 1)
                with pe.Fori(WCH, T - 1) as i:
                    tile(i)
                tile(T - 1, last=True)
                U = T * NU
                turn_probs(U - 1)
                pe.wait_ge(S["kv_ready"], T)
                mix(U - 1, T - 1)
                out_proj(U - 2, T - 1, NU - 2)
                turn_xq(0)
                out_proj(U - 1, T - 1, NU - 1)
                pe.wait_ge(scores_read, T * NU)
                pe.wait_ge(S["ol_ready"], T * NU)
                pe.wait_ge(S["out_added"], T)

            def turn_xq(t):
                pe.wait_ge(S["xq_ready"], t + 1)
                pe.wait_ge(S["c2"], t + 1)
                wait(pe, S["xqT_ready"], t)
                for k in range(KD):
                    nc.tensor.transpose(ps_xt[:, 0:256].bitcast(BF16)[:, k * P:(k + 1) * P], xq[:, k * P:(k + 1) * P], identb[:, :])
                nc.tensor.transpose(ps_xt[0:6, 256:320].bitcast(BF16), sxs[:, 0:6], identb[:, :]).then_inc(S["xt2"], 1)

            def gate_val(t, c):
                C = t * FC + c
                if c == 0:
                    pe.wait_ge(S["xqT_ready"], t + 1)
                for n, (ps, w, done) in enumerate(((ps_g, tern_g, "gate_ps"), (ps_v, tern_v, "val_ps"))):
                    wait(pe, S[("s_ready", "h_ready")[n]], C - 1)
                    for k in range(KD):
                        nc.tensor.matmul(ps[c % 2][:, :], xqT[:, k, :], w[:, k, c * 512:(c + 1) * 512],
                                         start=(k == 0), stop=False)
                    nc.tensor.matmul(ps[c % 2][:, :], sxT, brow[:, n, c * 512:(c + 1) * 512],
                                     start=False, stop=True).then_inc(S[done], 1)

            def turn_h(t, pieces):
                for j in pieces:
                    pe.wait_ge(S["hq_ready"], 2 * t + 1 + j // 2)
                    wait(pe, S["hqT_ready"], 4 * t + max(j - 1, 0))
                    for k in range(4):
                        mm = nc.tensor.transpose(ps_tr[j % 2][:, 0:256].bitcast(BF16)[:, k * P:(k + 1) * P],
                                                 hq[:, (4 * j + k) * P:(4 * j + k + 1) * P], identb[:, :])
                    mm.then_inc(S["tr_done"], 1)

            def down(t, pieces):
                wait(pe, S["y_ready"], t)
                for k in pieces:
                    if k % 4 == 0:
                        pe.wait_ge(S["hqT_ready"], 4 * t + k // 4 + 1)
                    mm = nc.tensor.matmul(ps_o[:, :], hqT[:, k, :], tern_o[:, k, :], start=(k == 0), stop=(k == FK - 1))
                if k == FK - 1:
                    mm.then_inc(S["o_done"], 1)

            def ffn(t, first=False, last=False):
                gate_val(t, 0)
                gate_val(t, 1)
                if not first:
                    turn_h(t - 1, (0, 1))
                gate_val(t, 2)
                if not first:
                    turn_h(t - 1, (2, 3))
                gate_val(t, 3)
                if not first:
                    down(t - 1, range(0, FK // 2))
                if not last:
                    turn_xq(t + 1)
                if not first:
                    down(t - 1, range(FK // 2, FK))

            pe.wait_ge(S["flag_ready"], 1)
            spread = pe.value_load(flag_i[0:1, 0:1], min_val=0, max_val=4 * T)
            with pe.If(spread < 1):
                phase1(1)
            with pe.Else():
                phase1(WMAX)

            pe.wait_ge(S["tern_done"], NM * WCH)
            pe.wait_ge(S["brow_ld"], 16 * 12)
            ffn(0, first=True)
            with pe.Fori(1, T - 1) as t:
                ffn(t)
            ffn(T - 1, last=True)
            turn_h(T - 1, range(4))
            down(T - 1, range(FK))

        @block.scalar
        def _(act):
            def xT_out(i):
                act.wait_ge(S["xt_done"], i + 1)
                wait(act, S["qc_done"], i)
                nc.scalar.copy(xnT[:, :, :], ps_prep[:, :].rearrange("p (k n) -> p k n", k=KD)).then_inc(S["xnT_ready"], 1)

            def q_out(i):
                act.wait_ge(S["qc_done"], i + 1)
                wait(act, S["ql_done"], i * NG)
                wait(act, S["qr_done"], i * NG)
                wait(act, S["rope_ab"], i * NG)
                for rows, n in ((slice(0, P), 0), (slice(0, 64), 1), (slice(64, P), 2)):
                    nc.scalar.activation(qcs[rows, n, 0, :], ps_prep[rows, (n > 0) * P:((n > 0) + 1) * P],
                                         ACT.Identity, scale=up[rows, 3:4])
                nc.scalar.activation(csT[:, :, :], ps_prep[:, 2 * P:4 * P].rearrange("p (k n) -> p k n", k=2),
                                     ACT.Identity, scale=undo[:, 2:3]).then_inc(S["qc_hi"], 1)

            count = [0]

            def square(src, side, n, columns=None):
                for c in columns or range(0, src.shape[1], 1024):
                    w = min(1024, src.shape[1] - c)
                    nc.scalar.activation(psplit[:, :, :].rearrange("p s n -> p (s n)")[:, 0:w], src[:, c:c + w], ACT.Square,
                                         accum_out=ssq[:, side, n, c // 1024:c // 1024 + 1]).then_inc(S["squared"], 1)
                    count[0] += 1
                    act.wait_ge(S["squared"], count[0])

            def keys_copy(b):
                act.wait_ge(S["kv_ps"], b + 1)
                nc.scalar.copy(kv_cT[:, b * LK:(b + 1) * LK], kv_bank[b % 2][:, :]).then_inc(S["kv_ev"], 1)

            keys_copy(0)
            keys_copy(1)
            act.wait_ge(S["zeros"], 1)
            act.wait_ge(S["uw_ld"], 32)
            square(stf, 0, 1)
            square(ternf[:, 8192:10240], 1, 1)
            keys_copy(2)
            act.wait_ge(S["qw_ld"], 32)
            square(qr_in[:, :], 0, 2)
            square(wdq_sb[:, :, :].rearrange("p k n -> p (k n)"), 0, 3)
            keys_copy(3)
            act.wait_ge(S["kv_ev"], BATCH)
            square(kv_cT[:, :], 0, 4)
            act.wait_ge(S["scale_step"], SCALE_STEPS)
            for g in range(NG):
                act.wait_ge(S["uqk_ps"], g + 1)
                half = 64 * (g // 2)
                a, b = uqk_banks[g % 2]
                nc.scalar.activation(uqk1[:, 0, g * GH:(g + 1) * GH, :], a[:, :].rearrange("p (h n) -> p h n", h=GH),
                                     ACT.Identity, scale=up[:, 1:2])
                nc.scalar.activation(uqk2[half:half + 64, 0, (g % 2) * GH:(g % 2 + 1) * GH, :],
                                     b[half:half + 64, :].rearrange("p (h n) -> p h n", h=GH),
                                     ACT.Identity, scale=up[half:half + 64, 1:2]).then_inc(S["uqk_hi"], 1)
                if g == 1:
                    act.wait_ge(S["vow_ld"], 32)
                    square(ternf[:, 10240:12288], 0, 0)
                    square(ternf[:, 0:8192], 1, 0, (0, 1024))
                if g == 2:
                    xT_out(0)
                    square(ternf[:, 0:8192], 1, 0, (2048,))
            nc.scalar.activation(qrs[:, 0, :], qr_in[:, :], ACT.Identity, scale=up[:, 2:3]).then_inc(S["qr_hi"], 1)
            square(ternf[:, 0:8192], 1, 0, (3072,))
            q_out(0)

            def output_products_high():
                act.wait_ge(S["scale_step"], 2 * SCALE_STEPS)
                act.wait_ge(S["kv_ps"], BATCH)
                for h in range(H):
                    act.wait_ge(S["vo_ps"], h + 1)
                    nc.scalar.activation(vo[:, h, 0, :], vo_banks[h % 4][:, :],
                                         ACT.Identity, scale=up[:, 0:1]).then_inc(S["vo_hi"], 1)

            def phase1(W):
                NU, HU, KW = NG * W, GH // W, W * P
                _, _, kvwin, ol = key_windows(W)
                nm, sm = ([r[:, 0:HU] for r in rs] for rs in (nm4, sm4))

                def keys_out(i):
                    act.wait_ge(S["kt_done"], i + 1)
                    wait(act, S["pv_done"], i * NU)
                    nc.scalar.activation(kvwin[:, 0, :, :], ps_prep[:, 0:KW].rearrange("p (w n) -> p w n", w=W),
                                         ACT.Identity, scale=up[:, 4:5]).then_inc(S["kv_hi"], 1)

                def ql_out(i, g):
                    G = i * NG + g
                    act.wait_ge(S["ql_done"], G + 1)
                    wait(act, S["sc_done"], (G - 1) * W)
                    nc.scalar.activation(ql[g % 2][:, :, :], ps_qa[:, :].rearrange("p (h n) -> p h n", h=GH),
                                         ACT.Identity, scale=undo[:, 1:2]).then_inc(S["ql_ready"], 1)

                def probsT_out(U):
                    act.wait_ge(S["pt_done"], U + 1)
                    wait(act, S["pv_done"], U)
                    nc.scalar.copy(ptT, ps_pt[:, :].bitcast(F16)).then_inc(S["pt_ready"], 1)

                def ol_high(U, r):
                    act.wait_ge(S["pv_done"], U + 1)
                    wait(act, S["op_done"], U - 1)
                    nc.scalar.copy(ol[r][:, 0, :, :], ps_ol[:, 0:HU * P].rearrange("p (j n) -> p j n", j=HU)).then_inc(S["ol_hi"], 1)

                def p_high(U, r):
                    act.wait_ge(S["p_ready"], U + 1)
                    wait(act, S["pt_done"], U)
                    nc.scalar.copy(psplit[:, 0, :], pr[r]).then_inc(S["p_hi"], 1)

                def ternary(i, m):
                    c = i - WCH
                    if m == 0:
                        act.wait_ge(S["st_ld"], (i + 1) * 16 * NM)
                    nc.scalar.activation(stage[:, m, :], stage[:, m, :], ACT.Identity, scale=rgam[:, m:m + 1],
                                         bias=magic[:, 0:1]).then_inc(S["w_round"], 1)
                    act.wait_ge(S["w_round"], c * NM + m + 1)
                    nc.scalar.activation(tern[:, m, bass.ds(c * WC, WC)], stage[:, m, :], ACT.Sign,
                                         bias=magic[:, 1:2]).then_inc(S["tern_done"], 1)

                def tile(i, first=False, last=False, sums=False, terns=False):
                    for u in range(NU):
                        U, g = i * NU + u, u // W
                        if not (first and u == 0):
                            probsT_out(U - 1)
                        if W == 1:
                            act.wait_ge(S["nm_done"], U + 1)
                            wait(act, S["p_split"], U - 1)
                            for j in range(HU):
                                ins = nc.scalar.activation(pr[u % 2][:, j * KW:(j + 1) * KW], ps_s[u % 2][:, j * KW:(j + 1) * KW], ACT.Exp,
                                                           scale=SCALE, bias=nm[u % 2][:, j:j + 1], accum_out=sm[u % 2][:, j:j + 1])
                            ins.then_inc(S["exp_done"], 1)
                        else:
                            act.wait_ge(S["sub_done"], U + 1)
                            nc.scalar.activation(pr[u % 2], pr[u % 2], ACT.Exp, scale=SCALE).then_inc(S["exp_done"], 1)
                        if u % W == 0:
                            if g < NG - 1:
                                ql_out(i, g + 1)
                            elif not last:
                                ql_out(i + 1, 0)
                            if g == 1 and not last:
                                xT_out(i + 1)
                            if g == 2 and not last:
                                q_out(i + 1)
                            if g == 3 and sums:
                                act.wait_ge(S["st_ld"], (i + 1) * 16 * NM)
                                for m in range(NM):
                                    nc.scalar.activation(stage[:, m, :], stage[:, m, :], ACT.Abs,
                                                         accum_out=asum[:, m, bass.ds(i, 1)]).then_inc(S["sums_done"], 1)
                        p_high(U, u % 2)
                        if u == 0:
                            keys_out(i)
                        if not (first and u == 0):
                            ol_high(U - 1, (u - 1) % 2)
                        if u % W == 0 and g < NM and terns:
                            ternary(i, g)

                ql_out(0, 0)
                output_products_high()
                tile(0, first=True, sums=True)
                with act.Fori(1, WCH) as i:
                    tile(i, sums=True)
                act.wait_ge(S["bias_step"], 1)
                with act.Fori(WCH, T - 1) as i:
                    tile(i, terns=True)
                tile(T - 1, last=True, terns=True)
                probsT_out(T * NU - 1)
                ol_high(T * NU - 1, (NU - 1) % 2)
                act.wait_ge(S["brow_zero"], 1)

            def xqT_out(t):
                act.wait_ge(S["xt2"], t + 1)
                wait(act, S["val_ps"], t * FC)
                nc.scalar.copy(xqT, ps_xt[:, 0:256].bitcast(BF16).rearrange("p (k n) -> p k n", k=KD))
                nc.scalar.copy(sxT[0:6, :], ps_xt[0:6, 256:320].bitcast(BF16)).then_inc(S["xqT_ready"], 1)

            def silu(t, c):
                C = t * FC + c
                act.wait_ge(S["gate_ps"], C + 1)
                if c == 0:
                    act.wait_ge(S["sgv_ready"], t + 1)
                wait(act, S["h_ready"], C - 1)
                nc.scalar.activation(s_sb[c % 2], ps_g[c % 2][:, :], ACT.Silu, scale=sgv[:, 0:1]).then_inc(S["s_ready"], 1)

            def hT_out(t, pieces):
                for j in pieces:
                    act.wait_ge(S["tr_done"], 4 * t + j + 1)
                    wait(act, S["o_done"], t)
                    nc.scalar.copy(hqT[:, 4 * j:4 * j + 4, :],
                                   ps_tr[j % 2][:, 0:256].bitcast(BF16).rearrange("p (k n) -> p k n", k=4)).then_inc(S["hqT_ready"], 1)

            def hq_out(t):
                wait(act, S["tr_done"], 4 * t)
                for n in range(2):
                    act.wait_ge(S["hr_done"], 2 * t + n + 1)
                    nc.scalar.activation(hq[:, n * 1024:(n + 1) * 1024], h_sb[:, n * 1024:(n + 1) * 1024], ACT.Copy,
                                         bias=-MAGIC).then_inc(S["hq_ready"], 1)

            def ffn(t, first=False, last=False):
                if first:
                    silu(t, 0)
                    silu(t, 1)
                else:
                    hT_out(t - 1, (0, 1))
                silu(t, 2)
                if not first:
                    hT_out(t - 1, (2, 3))
                silu(t, 3)
                if not last:
                    xqT_out(t + 1)
                    silu(t + 1, 0)
                    silu(t + 1, 1)
                hq_out(t)

            act.wait_ge(S["flag_ready"], 1)
            spread = act.value_load(flag_i[0:1, 0:1], min_val=0, max_val=4 * T)
            with act.If(spread < 1):
                phase1(1)
            with act.Else():
                phase1(WMAX)

            xqT_out(0)
            ffn(0, first=True)
            with act.Fori(1, T - 1) as t:
                ffn(t)
            ffn(T - 1, last=True)
            hT_out(T - 1, range(4))

        @block.gpsimd
        def _(pool):
            nc.gpsimd.memset(identf[:, :], 0.0).then_inc(S["pool_const"], 1)
            nc.gpsimd.memset(sel[:, :, :], 0.0).then_inc(S["pool_const"], 1)
            nc.gpsimd.iota(gpos_i, pattern=[[P, T]], base=0, channel_multiplier=1)
            nc.gpsimd.iota(lpos_i, pattern=[[0, BATCH], [P, 4]], base=0, channel_multiplier=1)
            nc.gpsimd.iota(bpos_i, pattern=[[LQ, BATCH], [0, 4]], base=0, channel_multiplier=0)
            nc.gpsimd.iota(lrow_i, pattern=[[1, LQ]], base=0, channel_multiplier=0)
            nc.gpsimd.iota(iota_i, pattern=[[1, LK]], base=0, channel_multiplier=0).then_inc(S["pool_const"], 1)
            pool.wait_ge(S["pool_const"], 3)
            nc.gpsimd.affine_select(out=identf[:, :], in_=identf[:, :], compare_op=ALU.not_equal, fill=1.0, base=0,
                                    pattern=[[-1, P]], channel_multiplier=1).then_inc(S["pool_const"], 1)
            for n in range(2):
                nc.gpsimd.affine_select(out=sel[:, n, :], in_=sel[:, n, :], compare_op=ALU.not_equal, fill=1.0,
                                        base=-n * (P - 1), pattern=[[0, P]], channel_multiplier=1).then_inc(S["pool_const"], 1)
            nc.gpsimd.memset(ones[:, :], 1.0)
            nc.gpsimd.memset(mhalf[:, :], -0.5)
            nc.gpsimd.memset(magic[:, 0:1], MAGIC)
            nc.gpsimd.memset(magic[:, 1:2], -MAGIC)
            nc.gpsimd.memset(ssq[:, :, :, :], 0.0).then_inc(S["pool_const"], 1)
            pool.wait_ge(S["pool_const"], 7)
            nc.gpsimd.memset(ssq[:, 1, 2:5, 0:1], 1.0 / P).then_inc(S["pool_const"], 1)
            pool.wait_ge(S["pool_const"], 8)
            nc.gpsimd.memset(ssq[:, 1, 3, 0:1], float(DM) / P)
            nc.gpsimd.memset(win[:, :], 0.0)
            nc.gpsimd.memset(qcs[:, :, :, :], 0.0).then_inc(S["zeros"], 1)

            def gather_x(t):
                nc.gpsimd.indirect_dma_start(x_all[:, t, :], None, x, bass.IndirectOffsetOnAxis(ap=idx[:, t:t + 1].bitcast(U32), axis=0)) \
                    .then_inc(S["x_ld" if t else "x0_ld"], 16)

            def gather_cs(i):
                wait(pool, S["qc_done"], i)
                nc.gpsimd.tensor_copy(idx_cs[:, :], idx_b[:, bass.ds(i, 1)]).then_inc(S["cs_idx"], 1)
                pool.wait_ge(S["cs_idx"], i + 1)
                nc.gpsimd.tensor_tensor(carry_p[:, :], mhalf[:, :], mhalf[:, :], ALU.add)
                nc.gpsimd.indirect_dma_start(cs_sb[:, :], None, cs, bass.IndirectOffsetOnAxis(ap=idx_cs[:, :].bitcast(U32), axis=0)) \
                    .then_inc(S["cs_ld"], 16)

            def inv_std(i, veps, done):
                pool.wait_ge(veps, i + 1)
                nc.gpsimd.tensor_tensor(rstd[:, :], ve[:, :], mhalf[:, :], ALU.pow).then_inc(done, 1)

            pool.wait_ge(S["idx_ready"], 1)
            gather_x(0)
            gather_cs(0)
            for t in range(1, T):
                gather_x(t)
                if t == T // 2:
                    inv_std(0, S["veps_done"], S["rstd_ready"])

            def phase1(W):
                NU, HU, KW = NG * W, GH // W, W * P
                rc = [r[:, 0:HU] for r in rc4]

                def rope_add(i, g):
                    G = i * NG + g
                    pool.wait_ge(S["rope_ab"], G + 1)
                    wait(pool, S["sc_done"], (G - 1) * W)
                    nc.gpsimd.tensor_tensor(qrt[g % 2][:, :, :], tA[:, :, :], tB[:, :, :], ALU.add).then_inc(S["qr_ready"], 1)

                def tile(i, last=False):
                    for u in range(NU):
                        U, g = i * NU + u, u // W
                        if u == NU - 1 and W == 1 and not last:
                            rope_add(i + 1, 0)
                        pool.wait_ge(S["rec_done"], U + 1)
                        p3 = pr[u % 2].rearrange("p (j n) -> p j n", j=HU)
                        nc.gpsimd.tensor_tensor(p3, p3, rc[u % 2][:, :].unsqueeze(2).to_broadcast([P, HU, KW]),
                                                ALU.mult).then_inc(S["p_ready"], 1)
                        if u % W == 0:
                            if g < NG - 1:
                                rope_add(i, g + 1)
                            elif not last and W > 1:
                                rope_add(i + 1, 0)
                        if last and u == NU - 1:
                            inv_std(0, S["veps2"], S["rstd2"])
                            pool.wait_ge(S["ql_done"], T * NG)
                            pool.wait_ge(S["qr_done"], T * NG)
                            pool.wait_ge(S["tern_done"], NM * WCH)
                            nc.gpsimd.memset(projw[:, 0:2048], 0.0)
                            nc.gpsimd.memset(stf[:, 576:640], 0.0).then_inc(S["brow_zero"], 1)
                        if u == 0 and not last:
                            inv_std(i + 1, S["veps_done"], S["rstd_ready"])
                            gather_cs(i + 1)

                rope_add(0, 0)
                tile(0)
                with pool.Fori(1, T - 1) as i:
                    tile(i)
                tile(T - 1, last=True)

            def x_bias(t):
                xt = x_all[:, bass.ds(t, 1), :].rearrange("p o n -> p (o n)")
                nc.gpsimd.tensor_tensor(xt, xt, ob_sb, ALU.add).then_inc(S["xb_ready"], 1)

            def scatter_y(t):
                pool.wait_ge(S["y_ready"], t + 1)
                wait(pool, S["stored"], t * 16)
                nc.gpsimd.tensor_copy(idx_y[:, :], idx[:, bass.ds(t, 1)]).then_inc(S["y_idx"], 1)
                pool.wait_ge(S["y_idx"], t + 1)
                nc.gpsimd.tensor_tensor(carry_p[:, :], mhalf[:, :], mhalf[:, :], ALU.add)
                nc.gpsimd.indirect_dma_start(y, bass.IndirectOffsetOnAxis(ap=idx_y[:, :].bitcast(U32), axis=0),
                                             y_sb, None).then_inc(S["stored"], 16)

            def ffn(t, first=False, last=False):
                if not last:
                    inv_std(t + 1, S["veps2"], S["rstd2"])
                pool.wait_ge(S["xn2"], t + 1)
                x_bias(t)
                if not first:
                    scatter_y(t - 1)

            pool.wait_ge(S["flag_ready"], 1)
            spread = pool.value_load(flag_i[0:1, 0:1], min_val=0, max_val=4 * T)
            with pool.If(spread < 1):
                phase1(1)
            with pool.Else():
                phase1(WMAX)

            pool.wait_ge(S["bias_ld"], 16)
            ffn(0, first=True)
            with pool.Fori(1, T - 1) as t:
                ffn(t)
            ffn(T - 1, last=True)
            scatter_y(T - 1)
            pool.wait_ge(S["stored"], 16 * T)

        @block.vector
        def _(dve):
            dve.wait_ge(S["pool_const"], 4)
            nc.vector.tensor_copy(iota[:, :], iota_i)
            nc.vector.tensor_copy(identb[:, :], identf[:, :])
            nc.vector.tensor_copy(identh[:, :], identf[:, :])
            nc.vector.tensor_copy(bpos[:, :], bpos_i[:, :])
            nc.vector.tensor_copy(val_c[:, :, 0], gpos_i[:, :])
            dve.wait_ge(S["seg_ld"], 32)
            step = [0]

            def stepped(ins):
                ins.then_inc(S["sort_step"], 1)
                step[0] += 1
                dve.wait_ge(S["sort_step"], step[0])

            stepped(nc.vector.tensor_scalar(val_c[:, :, 1], seg_i[:, :], -1.0, float(LK + LOOKBACK), ALU.max, ALU.min))
            stepped(nc.vector.scalar_tensor_tensor(out=key_c[:, :], in0=val_c[:, :, 1], scalar=float(LQ), in1=lpos_i[:, :],
                                                   op0=ALU.mult, op1=ALU.add))
            stepped(nc.vector.tensor_scalar(key_r, seg_r, -1.0, float(LK + LOOKBACK), ALU.max, ALU.min))
            stepped(nc.vector.scalar_tensor_tensor(out=key_r.rearrange("p (b n) -> p b n", b=BATCH),
                                                   in0=key_r.rearrange("p (b n) -> p b n", b=BATCH), scalar=float(LQ),
                                                   in1=lrow_i.unsqueeze(1).to_broadcast([P, BATCH, LQ]),
                                                   op0=ALU.mult, op1=ALU.add))
            dve.wait_ge(S["const_ld"], 32)
            def sort_batch(b):
                for q in range(4):
                    t = 4 * b + q
                    stepped(nc.vector.tensor_scalar(sort_junk, key_r[:, b * LQ:(b + 1) * LQ], key_c[:, t:t + 1], None,
                                                    ALU.is_lt, ALU.add, accum_out=rank[:, t:t + 1]))
                wait(dve, S["perm_ps"], b - 1)
                for q in range(4):
                    nc.vector.tensor_scalar(onehot[:, b % 2, q, :], iota[:, :], rank[:, 4 * b + q:4 * b + q + 1], None,
                                            ALU.is_equal).then_inc(S["onehot_ready"], 1)

            sort_batch(0)
            for b in range(BATCH):
                if b < BATCH - 1:
                    sort_batch(b + 1)
                kb = slice(b * LK, (b + 1) * LK)
                dve.wait_ge(S["kr_ps"], b + 1)
                nc.vector.tensor_tensor(kropeT[:, kb], ps_s[1][:, :], cosn_sb, ALU.mult).then_inc(S["kr_mul"], 1)
                wait(dve, S["kr_ready"], b)
                nc.vector.tensor_tensor(pt_sb[:, :], ps_pt[:, :], sinn_sb, ALU.mult).then_inc(S["kr_mul"], 1)
                dve.wait_ge(S["kr_mul"], 2 * b + 2)
                nc.vector.tensor_tensor(kropeT[:, kb], kropeT[:, kb], pt_sb[:, :], ALU.add).then_inc(S["kr_ready"], 1)
            dve.wait_ge(S["kr_ready"], BATCH)
            dve.wait_ge(S["perm_ps"], BATCH)
            perm = ps_ol[:, 0:2 * T].rearrange("p (t n) -> p t n", n=2)
            nc.vector.tensor_copy(seg_s[:, :], perm[:, :, 1]).then_inc(S["seg_ready"], 1)
            nc.vector.tensor_copy(idx[:, :], perm[:, :, 0])
            nc.vector.tensor_tensor(idx_b[:, :], perm[:, :, 0], bpos[:, :], ALU.subtract).then_inc(S["idx_ready"], 1)
            scale_step = [0]

            def stepped_s(ins):
                ins.then_inc(S["scale_step"], 1)
                scale_step[0] += 1
                dve.wait_ge(S["scale_step"], scale_step[0])

            def scales(n, columns):
                a = columns
                nc.vector.tensor_reduce(ssum[:, :, a], ssq[:, :, a, :], AX.X, ALU.add).then_inc(S["sum_step"], 1)
                dve.wait_ge(S["tot_ps"], n + 1)
                stepped_s(nc.vector.tensor_copy(bound[:, :, a], ps_out[:, 0:2 * (a.stop - a.start)].rearrange("p (s n) -> p s n", s=2)))
                stepped_s(nc.vector.tensor_tensor(bound[:, 0, a], bound[:, 0, a], bound[:, 1, a], ALU.mult))
                stepped_s(nc.vector.tensor_scalar(bound[:, 0, a], bound[:, 0, a], 1e-30, None, ALU.max))
                stepped_s(nc.vector.tensor_scalar(bexp[:, a], bound[:, 0, a].bitcast(I32), 24, None, ALU.logical_shift_right))
                stepped_s(nc.vector.tensor_scalar(up[:, a].bitcast(I32), bexp[:, a], -float(1 << 23), 204.0 * (1 << 23), ALU.mult, ALU.add))
                stepped_s(nc.vector.tensor_scalar(inv[:, a].bitcast(I32), bexp[:, a], float(1 << 23), 50.0 * (1 << 23), ALU.mult, ALU.add))

            dve.wait_ge(S["squared"], 3 + 2 + 2 + 1 + 2)
            scales(0, slice(1, 5))
            stepped_s(nc.vector.tensor_tensor(undo[:, 1:3], inv[:, 1:3], inv[:, 3:4].to_broadcast([P, 2]), ALU.mult))

            dve.wait_ge(S["edge_ps"], 1)
            least, most = ps_ol[:, 2 * T:3 * T], ps_ol[:, 3 * T:4 * T]
            stepped(nc.vector.tensor_scalar(base[:, :], least, -float(LOOKBACK), 0.0, ALU.add, ALU.max))
            stepped(nc.vector.tensor_scalar(base[:, :], base[:, :], float(LK - P), None, ALU.min))
            nc.vector.tensor_scalar(bad[:, 0, :], least, 0.0, None, ALU.is_lt)
            nc.vector.tensor_scalar(bad[:, 1, :], most, float(LK + LOOKBACK - 1), None, ALU.is_gt)
            stepped(nc.vector.tensor_scalar(bad[:, 3, :], most, float(LK - 1), None, ALU.min))
            stepped(nc.vector.tensor_tensor(bad[:, 3, :], bad[:, 3, :], base[:, :], ALU.subtract))
            stepped(nc.vector.tensor_scalar(bad[:, 2, :], bad[:, 3, :], float(P - 1), None, ALU.is_gt))
            stepped(nc.vector.tensor_reduce(flag[:, :], bad[:, 0:3, :], AX.XY, ALU.add))
            nc.vector.tensor_tensor(off_i[:, :], base[:, :], bpos[:, :], ALU.add)
            stepped(nc.vector.tensor_tensor(seg_hi[1][:, :], seg_s[:, :], base[:, :], ALU.subtract))
            nc.vector.tensor_scalar(seg_lo[1][:, :], seg_hi[1][:, :], -float(LOOKBACK), None, ALU.add)
            nc.vector.tensor_scalar(seg_lo[WMAX][:, :], seg_s[:, :], -float(LOOKBACK), None, ALU.add)
            stepped(nc.vector.tensor_copy(flag_i[:, :], flag[:, :]))
            nc.vector.memset(carry[:, :], 0.0).then_inc(S["flag_ready"], 1)

            def low(dst, src, n, high, rows=slice(0, P)):
                return nc.vector.scalar_tensor_tensor(out=dst, in0=src, scalar=up[rows, n:n + 1], in1=high,
                                                      op0=ALU.mult, op1=ALU.subtract)

            def stats(i, bn, aggr, veps):
                nc.vector.bn_stats(st6[:, :], x_all[:, bass.ds(i, 1), :].rearrange("p o n -> p (o n)")).then_inc(bn, 1)
                dve.wait_ge(bn, i + 1)
                nc.vector.memset(carry[:, :], 0.0)
                nc.vector.bn_aggr(mv[:, :], st6[:, :]).then_inc(aggr, 1)
                dve.wait_ge(aggr, i + 1)
                nc.vector.tensor_scalar(ve[:, :], mv[:, 1:2], EPS, None, ALU.add).then_inc(veps, 1)

            def norm(i, rs, done):
                dve.wait_ge(rs, i + 1)
                nc.vector.tensor_scalar(xn[:, :], x_all[:, bass.ds(i, 1), :].rearrange("p o n -> p (o n)"),
                                        mv[:, 0:1], rstd[:, :], ALU.subtract, ALU.mult).then_inc(done, 1)

            def q_low(i):
                dve.wait_ge(S["qc_hi"], i + 1)
                for rows, n in ((slice(0, P), 0), (slice(0, 64), 1), (slice(64, P), 2)):
                    ins = low(qcs[rows, n, 1, :], ps_prep[rows, (n > 0) * P:((n > 0) + 1) * P], 3, qcs[rows, n, 0, :], rows)
                ins.then_inc(S["qc_ready"], 1)

            def square_half(n):
                dve.wait_ge(S["vow_ld"], 32)
                nc.vector.scalar_tensor_tensor(out=ptT, in0=ternf[:, n * 1024:(n + 1) * 1024], scalar=1.0,
                                               in1=ternf[:, n * 1024:(n + 1) * 1024], op0=ALU.mult, op1=ALU.mult,
                                               accum_out=ssq[:, 1, 0, n:n + 1]).then_inc(S["squared_too"], 1)
                dve.wait_ge(S["squared_too"], n - 3)

            for g in range(NG):
                dve.wait_ge(S["uqk_hi"], g + 1)
                rows, hs = slice(64 * (g // 2), 64 * (g // 2) + 64), slice((g % 2) * GH, (g % 2 + 1) * GH)
                a, b = uqk_banks[g % 2]
                low(uqk1[:, 1, g * GH:(g + 1) * GH, :], a[:, :].rearrange("p (h n) -> p h n", h=GH), 1,
                    uqk1[:, 0, g * GH:(g + 1) * GH, :]).then_inc(S["uqk_ev"], 1)
                low(uqk2[rows, 1, hs, :], b[rows, :].rearrange("p (h n) -> p h n", h=GH), 1,
                    uqk2[rows, 0, hs, :], rows).then_inc(S["uqk_ev"], 1)
                if g == 1:
                    dve.wait_ge(S["x0_ld"], 16)
                    stats(0, S["bn_done"], S["aggr_done"], S["veps_done"])
                    square_half(4)
                    norm(0, S["rstd_ready"], S["xn_ready"])
                    square_half(5)
                    square_half(6)
                if g == 2:
                    square_half(7)
            q_low(0)
            dve.wait_ge(S["qr_hi"], 1)
            low(qrs[:, 1, :], qr_in[:, :], 2, qrs[:, 0, :]).then_inc(S["qr_parts"], 1)
            dve.wait_ge(S["squared"], 10 + 2 + 4)
            scales(1, slice(0, 1))
            stepped_s(nc.vector.tensor_tensor(undo[:, 0:1], inv[:, 0:1], inv[:, 4:5], ALU.mult))

            def output_products_low():
                for h in range(H):
                    dve.wait_ge(S["vo_hi"], h + 1)
                    low(vo[:, h, 1, :], vo_banks[h % 4][:, :], 0, vo[:, h, 0, :]).then_inc(S["vo_ev"], 1)

            def phase1(W):
                NU, HU, KW = NG * W, GH // W, W * P
                kwin, krz, kvwin, ol = key_windows(W)
                mask, maskt = mask4[:, 0:KW], maskt4[:, 0:KW]
                mx, sm, rc, nm = ([r[:, 0:HU] for r in rs] for rs in (mx4, sm4, rc4, nm4))

                def first_key(i):
                    if W == 1:
                        return dve.value_load(off_i[0:1, bass.ds(i, 1)], min_val=0, max_val=TOK - P)
                    return (i // 4) * LK

                def windows(i, off):
                    wait(dve, S["sc_done"], i * NU)
                    wait(dve, S["kt_done"], i)
                    nc.vector.tensor_copy(kwin[:, :], kv_cT[:, bass.ds(off, KW)]).then_inc(S["win_copied"], 1)
                    nc.vector.tensor_copy(krz[0:64, 0, :], kropeT[0:64, bass.ds(off, KW)]).then_inc(S["win_copied"], 1)
                    nc.vector.tensor_copy(krz[64:P, 1, :], kropeT[64:P, bass.ds(off, KW)]).then_inc(S["win_copied"], 1)
                    nc.vector.tensor_scalar(mask[:, :], iota[:, 0:KW], seg_hi[W][:, bass.ds(i, 1)], NEG, ALU.is_gt, ALU.mult).then_inc(S["mask_parts"], 1)
                    nc.vector.tensor_scalar(maskt[:, :], iota[:, 0:KW], seg_lo[W][:, bass.ds(i, 1)], NEG, ALU.is_lt, ALU.mult).then_inc(S["mask_parts"], 1)
                    dve.wait_ge(S["mask_parts"], 2 * i + 2)
                    dve.wait_ge(S["win_copied"], 3 * i + 3)
                    nc.vector.tensor_tensor(mask[:, :], mask[:, :], maskt[:, :], ALU.add).then_inc(S["win_ready"], 1)

                def rope_mul(i, g):
                    G = i * NG + g
                    n = GH // 2
                    dve.wait_ge(S["qr_done"], G + 1)
                    dve.wait_ge(S["qc_ready"], i + 1)
                    wait(dve, S["qr_ready"], G)
                    nc.vector.tensor_tensor(tA[:, :, :], ps_qb[:, 0:n * P].rearrange("p (j n) -> p j n", j=n),
                                            csT[:, 0, :].unsqueeze(1).to_broadcast([P, n, P]), ALU.mult)
                    for q in range(4):
                        here, there = slice(32 * q, 32 * q + 32), slice(32 * (q ^ 1), 32 * (q ^ 1) + 32)
                        ins = nc.vector.tensor_tensor(tB[here, :, :], ps_qb[there, 0:n * P].rearrange("p (j n) -> p j n", j=n),
                                                      csT[there, 1, :].unsqueeze(1).to_broadcast([32, n, P]), ALU.mult)
                    ins.then_inc(S["rope_ab"], 1)

                def latent_out(U, r):
                    dve.wait_ge(S["ol_hi"], U + 1)
                    nc.vector.tensor_tensor(ol[r][:, 1, :, :], ps_ol[:, 0:HU * P].rearrange("p (j n) -> p j n", j=HU),
                                            ol[r][:, 0, :, :], ALU.subtract).then_inc(S["ol_ready"], 1)

                def keys_low(i):
                    dve.wait_ge(S["kv_hi"], i + 1)
                    low(kvwin[:, 1, :, :], ps_prep[:, 0:KW].rearrange("p (w n) -> p w n", w=W), 4,
                        kvwin[:, 0, :, :]).then_inc(S["kv_ready"], 1)

                def p_low(U, r):
                    dve.wait_ge(S["p_hi"], U + 1)
                    nc.vector.tensor_tensor(psplit[:, 1, :], pr[r], psplit[:, 0, :], ALU.subtract).then_inc(S["p_split"], 1)

                def add_out(i):
                    dve.wait_ge(S["op_done"], (i + 1) * NU)
                    xt = x_all[:, bass.ds(i, 1), :].rearrange("p o n -> p (o n)")
                    nc.vector.scalar_tensor_tensor(out=xt, in0=ps_out[:, :], scalar=undo[:, 0:1], in1=xt,
                                                   op0=ALU.mult, op1=ALU.add).then_inc(S["out_added"], 1)

                def tile(i, first=False, last=False):
                    for u in range(NU):
                        U, g = i * NU + u, u // W
                        sc3 = ps_s[u % 2][:, :].rearrange("p (j n) -> p j n", j=HU)
                        p3 = pr[u % 2].rearrange("p (j n) -> p j n", j=HU)
                        ends = u == NU - 1 and not last
                        off = first_key(i + 1) if ends else None
                        dve.wait_ge(S["sc_done"], U + 1)
                        nc.vector.tensor_reduce(mx[u % 2][:, :], sc3, AX.X, ALU.max).then_inc(S["max_done"], 1)
                        dve.wait_ge(S["max_done"], U + 1)
                        if W == 1:
                            nc.vector.tensor_scalar(nm[u % 2][:, :], mx[u % 2][:, :], -SCALE, None, ALU.mult).then_inc(S["nm_done"], 1)
                        else:
                            nc.vector.tensor_tensor(p3, sc3, mx[u % 2][:, :].unsqueeze(2).to_broadcast([P, HU, KW]),
                                                    ALU.subtract).then_inc(S["sub_done"], 1)
                        if ends:
                            windows(i + 1, off)
                            if W == 1:
                                rope_mul(i + 1, 0)
                        dve.wait_ge(S["exp_done"], U + 1)
                        if W > 1:
                            nc.vector.tensor_reduce(sm[u % 2][:, :], p3, AX.X, ALU.add).then_inc(S["sum_done"], 1)
                            dve.wait_ge(S["sum_done"], U + 1)
                        nc.vector.reciprocal(rc[u % 2][:, :], sm[u % 2][:, :]).then_inc(S["rec_done"], 1)
                        if u % W == 0:
                            if g < NG - 1:
                                rope_mul(i, g + 1)
                            elif not last and W > 1:
                                rope_mul(i + 1, 0)
                        p_low(U, u % 2)
                        if not (first and u == 0):
                            latent_out(U - 1, (u - 1) % 2)
                        if u == 0:
                            keys_low(i)
                        if u == 1 and not first:
                            add_out(i - 1)
                        if u == 0 and first:
                            dve.wait_ge(S["x_ld"], 16 * (T - 1))
                        if u == 0 and not last:
                            wait(dve, S["xt_done"], i + 1)
                            stats(i + 1, S["bn_done"], S["aggr_done"], S["veps_done"])
                            norm(i + 1, S["rstd_ready"], S["xn_ready"])
                        if u % W == 0 and g == 2 and not last:
                            q_low(i + 1)
                        if last and u == NU - 1:
                            dve.wait_ge(S["qr_ready"], T * NG)
                            quant_x(0)

                rope_mul(0, 0)
                dve.wait_ge(S["zeros"], 1)
                windows(0, first_key(0))
                output_products_low()
                tile(0, first=True)
                with dve.Fori(1, WCH) as i:
                    tile(i)
                dve.wait_ge(S["sums_done"], NM * WCH)
                nc.vector.tensor_reduce(asum1[:, :], asum[:, :, :], AX.X, ALU.add).then_inc(S["asum_red"], 1)
                dve.wait_ge(S["gam_ps"], 1)
                nc.vector.tensor_scalar(gam[:, :], ps_prep[:, 0:NM], 1.0 / (DM * HID), 1e-5, ALU.mult, ALU.max).then_inc(S["gam_a"], 1)
                dve.wait_ge(S["gam_a"], 1)
                stepb = [0]

                def stepped_b(ins):
                    ins.then_inc(S["bias_step"], 1)
                    stepb[0] += 1
                    dve.wait_ge(S["bias_step"], stepb[0])

                dve.wait_ge(S["b_ld"], 32)
                stepped_b(nc.vector.reciprocal(rgam[:, :], gam[:, :]))
                for m in range(2):
                    stepped_b(nc.vector.tensor_scalar(b_sb[:, m, :], b_sb[:, m, :], rgam[:, m:m + 1], None, ALU.mult))
                stepped_b(nc.vector.tensor_copy(bsplit[:, 0, :, :], b_sb[:, :, :]))
                stepped_b(nc.vector.tensor_tensor(brest[:, :, :], b_sb[:, :, :], bsplit[:, 0, :, :], ALU.subtract))
                stepped_b(nc.vector.tensor_copy(bsplit[:, 1, :, :], brest[:, :, :]))
                stepped_b(nc.vector.tensor_tensor(b_sb[:, :, :], brest[:, :, :], bsplit[:, 1, :, :], ALU.subtract))
                stepped_b(nc.vector.tensor_copy(bsplit[:, 2, :, :], b_sb[:, :, :]))
                with dve.Fori(WCH, T - 1) as i:
                    tile(i)
                tile(T - 1, last=True)
                latent_out(T * NU - 1, (NU - 1) % 2)
                add_out(T - 1)

            def quant_x(t):
                stats(t, S["bn2"], S["aggr2"], S["veps2"])
                norm(t, S["rstd2"], S["xn2"])
                dve.wait_ge(S["xn2"], t + 1)
                nc.vector.tensor_reduce(gx[:, :], xn[:, :], AX.X, ALU.max, apply_absolute_value=True).then_inc(S["gx2"], 1)
                dve.wait_ge(S["gx2"], t + 1)
                nc.vector.tensor_scalar(gxc[:, :], gx[:, :], 1e-5, None, ALU.max).then_inc(S["gxc2"], 1)
                dve.wait_ge(S["gxc2"], t + 1)
                nc.vector.reciprocal(rx[:, :], gxc[:, :]).then_inc(S["rx2"], 1)
                nc.vector.tensor_scalar(dx[:, :], gxc[:, :], 1.0 / 127.0, None, ALU.mult).then_inc(S["dx2"], 1)
                dve.wait_ge(S["rx2"], t + 1)
                nc.vector.tensor_scalar(sx[:, :], rx[:, :], 127.0, None, ALU.mult).then_inc(S["sx2"], 1)
                dve.wait_ge(S["sx2"], t + 1)
                nc.vector.tensor_scalar(xn[:, :], xn[:, :], sx[:, :], MAGIC, ALU.mult, ALU.add).then_inc(S["xr2"], 1)
                dve.wait_ge(S["xr2"], t + 1)
                wait(dve, S["xt2"], t)
                nc.vector.tensor_scalar(xq, xn[:, :], -MAGIC, None, ALU.add).then_inc(S["xq_ready"], 1)
                nc.vector.tensor_copy(sxs[:, 0:3], sx.to_broadcast([P, 3])).then_inc(S["c0"], 1)
                dve.wait_ge(S["c0"], t + 1)
                nc.vector.tensor_tensor(sxr, sx, sxs[:, 0:1], ALU.subtract).then_inc(S["c1"], 1)
                dve.wait_ge(S["c1"], 2 * t + 1)
                nc.vector.tensor_copy(sxs[:, 3:5], sxr.to_broadcast([P, 2])).then_inc(S["c1"], 1)
                dve.wait_ge(S["c1"], 2 * t + 2)
                nc.vector.tensor_tensor(sxs[:, 5:6], sxr, sxs[:, 3:4], ALU.subtract).then_inc(S["c2"], 1)

            def scale_x(t):
                dve.wait_ge(S["dx2"], t + 1)
                nc.vector.tensor_scalar(sgv[:, :], gam[:, 0:2], dx[:, :], None, ALU.mult).then_inc(S["sgv_ready"], 1)
                dve.wait_ge(S["sgv_ready"], t + 1)

            def max_h(t, c):
                dve.wait_ge(S["h_ready"], t * FC + c + 1)
                nc.vector.tensor_reduce(mh4[:, c:c + 1], h_sb[:, c * 512:(c + 1) * 512], AX.X, ALU.max,
                                        apply_absolute_value=True).then_inc(S["mh_part"], 1)

            def chunk(t, c):
                C = t * FC + c
                dve.wait_ge(S["s_ready"], C + 1)
                dve.wait_ge(S["val_ps"], C + 1)
                wait(dve, S["hq_ready"], 2 * t - 1 + c // 2)
                nc.vector.scalar_tensor_tensor(out=h_sb[:, c * 512:(c + 1) * 512], in0=ps_v[c % 2][:, :], scalar=sgv[:, 1:2],
                                               in1=s_sb[c % 2], op0=ALU.mult, op1=ALU.mult).then_inc(S["h_ready"], 1)
                if c:
                    max_h(t, c - 1)

            def quant_h(t):
                dve.wait_ge(S["mh_part"], (t + 1) * FC)
                nc.vector.tensor_reduce(mh[:, :], mh4[:, :], AX.X, ALU.max).then_inc(S["mh_done"], 1)
                dve.wait_ge(S["mh_done"], t + 1)
                nc.vector.tensor_scalar(gh[:, :], mh[:, :], 1e-5, None, ALU.max).then_inc(S["gh_done"], 1)
                dve.wait_ge(S["gh_done"], t + 1)
                nc.vector.reciprocal(rh[:, :], gh[:, :]).then_inc(S["rh_done"], 1)
                dve.wait_ge(S["rh_done"], t + 1)
                nc.vector.tensor_scalar(sh[:, :], rh[:, :], 127.0, None, ALU.mult).then_inc(S["sh_done"], 1)
                dve.wait_ge(S["sh_done"], t + 1)
                for n in range(2):
                    half = h_sb[:, n * 1024:(n + 1) * 1024]
                    nc.vector.tensor_scalar(half, half, sh[:, :], MAGIC, ALU.mult, ALU.add).then_inc(S["hr_done"], 1)

            def finish(t):
                dve.wait_ge(S["o_done"], t + 1)
                dve.wait_ge(S["xb_ready"], t + 1)
                dve.wait_ge(S["so_ready"], t + 1)
                xt = x_all[:, bass.ds(t, 1), :].rearrange("p o n -> p (o n)")
                wait(dve, S["stored"], t * 16)
                nc.vector.scalar_tensor_tensor(out=y_sb, in0=ps_o[:, :], scalar=so[:, :], in1=xt,
                                               op0=ALU.mult, op1=ALU.add).then_inc(S["y_ready"], 1)

            def scale_o(t):
                wait(dve, S["y_ready"], t)
                nc.vector.tensor_scalar(so[:, :], gh[:, :], 1.0 / 127.0, gam[:, 2:3], ALU.mult, ALU.mult).then_inc(S["so_ready"], 1)

            def ffn(t, first=False, last=False):
                chunk(t, 0)
                chunk(t, 1)
                if not last:
                    quant_x(t + 1)
                chunk(t, 2)
                chunk(t, 3)
                max_h(t, 3)
                if not last:
                    scale_x(t + 1)
                quant_h(t)
                if not first:
                    finish(t - 1)
                scale_o(t)

            dve.wait_ge(S["flag_ready"], 1)
            spread = dve.value_load(flag_i[0:1, 0:1], min_val=0, max_val=4 * T)
            with dve.If(spread < 1):
                phase1(1)
            with dve.Else():
                phase1(WMAX)

            scale_x(0)
            ffn(0, first=True)
            with dve.Fori(1, T - 1) as t:
                ffn(t)
            ffn(T - 1, last=True)
            finish(T - 1)


def kernel(x, ctx_2048, itok_BxS_0_1023, L0_xattn_W_kvc, L0_xattn_W_dq, L0_xattn_W_uq, L0_xattn_W_qr,
           L0_xattn_W_uk, L0_xattn_W_kr, L0_xattn_W_uv, L0_xattn_W_o, L0_ffn_gate_w, L0_ffn_gate_b,
           L0_ffn_val_w, L0_ffn_val_b, L0_ffn_out_w, L0_ffn_out_b):
    import concourse.bacc as bacc
    from concourse.bass_utils import run_bass_kernel_spmd

    a = np.asarray
    half = ROPE // 2
    inv = (np.float32(1.0) / np.float32(10000.0) ** (np.arange(half, dtype=np.float32) / np.float32(half))).astype(np.float32)
    ang = np.arange(LQ, dtype=np.float32)[:, None] * inv
    cos, sin = np.cos(ang).astype(np.float32), np.sin(ang).astype(np.float32)
    cs = np.concatenate([cos] * 4 + [sin, -sin] * 2, axis=1)
    cosn = np.concatenate([cos.T] * 4, axis=0)
    sinn = np.concatenate([-sin.T, sin.T] * 2, axis=0)

    def swap(w):
        return np.concatenate([w.reshape(w.shape[0], -1, 2, half)[:, :, 1:2], w.reshape(w.shape[0], -1, 2, half)[:, :, 0:1]],
                              axis=2).reshape(w.shape)

    dq, wqr, wkr = a(L0_xattn_W_dq), a(L0_xattn_W_qr), a(L0_xattn_W_kr)
    arrays = {
        "x": a(x).reshape(TOK, DM),
        "ctxT": a(ctx_2048).transpose(0, 2, 1),
        "itok": a(itok_BxS_0_1023).reshape(TOK),
        "itokT": a(itok_BxS_0_1023).reshape(T, P).T,
        "cs": cs, "cosn": cosn, "sinn": sinn,
        "wkvc": a(L0_xattn_W_kvc),
        "wdq": np.concatenate([dq, dq[:, P:QC]], axis=1),
        "uqT": a(L0_xattn_W_uq).T,
        "ukT": a(L0_xattn_W_uk).T,
        "uvT": a(L0_xattn_W_uv).T,
        "wo": a(L0_xattn_W_o),
        "qr": np.concatenate([wqr[0:P], np.concatenate([wqr[P:QC, 0:512], wqr[P:QC, 512:1024]], axis=0)], axis=1),
        "kr": np.stack([np.concatenate([wkr, wkr], axis=1), np.concatenate([swap(wkr), swap(wkr)], axis=1)], axis=1),
        "gate": a(L0_ffn_gate_w).T.reshape(KD, P, 2, HID // 2).transpose(0, 2, 1, 3).reshape(WCH, P, WC),
        "val": a(L0_ffn_val_w).T.reshape(KD, P, 2, HID // 2).transpose(0, 2, 1, 3).reshape(WCH, P, WC),
        "outw": a(L0_ffn_out_w).T.reshape(WCH, 2, P, DM).transpose(0, 2, 1, 3).reshape(WCH, P, WC),
        "gate_b": a(L0_ffn_gate_b), "val_b": a(L0_ffn_val_b), "out_b": a(L0_ffn_out_b),
    }
    arrays = {n: np.ascontiguousarray(v) for n, v in arrays.items()}
    nc = bacc.Bacc("TRN2", target_bir_lowering=False, num_devices=1)
    args = [nc.dram_tensor(f"in_{n}", v.shape, mybir.dt.from_np(v.dtype), kind="ExternalInput").ap() for n, v in arrays.items()]
    args.append(nc.dram_tensor("y", (TOK, DM), F32, kind="ExternalOutput").ap())
    build(nc, *args)
    r = run_bass_kernel_spmd(nc, [{f"in_{n}": v for n, v in arrays.items()}], core_ids=[0])
    return r.results[0]["y"].reshape(BATCH, LQ, DM)
```
